# Optimizing a Trainium2 kernel written in Bass

```python
import numpy as np
import jax
import jax.numpy as jnp

def _softmax(x, axis=-1):
    return jax.nn.softmax(x, axis=axis)

def _gelu(x):
    return jax.nn.gelu(x, approximate=True)

def _silu(x):
    return jax.nn.silu(x)

def _sigmoid(x):
    return jax.nn.sigmoid(x)

def _layernorm(x, axis=-1, eps=1e-05):
    m = jnp.mean(x, axis=axis, keepdims=True)
    v = jnp.var(x, axis=axis, keepdims=True)
    return (x - m) / jnp.sqrt(v + eps)

def _scatter_add(tgt, idx, src, axis=0):
    return tgt.at[idx].add(src)

def _segment_sum(src, seg, n):
    return jax.ops.segment_sum(src, seg, n)
kernel_name = 'mk_flamingo_gated_d1_seqx_r4_fad4f6'

def setup_inputs(seed: int=0):
    np.random.seed(seed)
    _w = jnp.asarray

    def _rec_inputs():
        import jax
        import jax.numpy as jnp
        _rk = jax.random.key(seed)
        x = -0.0002928 + 1 * jax.random.normal(jax.random.fold_in(_rk, 1), (8, 512, 256), jnp.float32)
        _lenS = 512 - jax.random.randint(jax.random.fold_in(_rk, 7), (8,), 0, max(1, 512 // 4) + 1, jnp.int32)
        _lenS2 = 512 - jax.random.randint(jax.random.fold_in(_rk, 8), (8,), 0, max(1, 512 // 4) + 1, jnp.int32)
        _ctx_1024P = jax.random.normal(jax.random.fold_in(_rk, 11), (8, 16, 256), jnp.float32)
        _ctx_1024c = jax.random.dirichlet(jax.random.fold_in(_rk, 511), 0.3 * jnp.ones((16,), jnp.float32), (8, 512))
        _ctx_1024t = jnp.einsum('bsk,bkd->bsd', _ctx_1024c, _ctx_1024P)
        _ctx_1024t = _ctx_1024t * jax.lax.rsqrt(jnp.mean(jnp.square(_ctx_1024t)) + 1e-12) * 0.953939
        ctx_1024 = -1.39393e-06 + 0.999914 * (_ctx_1024t + 0.3 * jax.random.normal(jax.random.fold_in(_rk, 611), (8, 512, 256), jnp.float32))
        _g = jax.random.normal(jax.random.fold_in(_rk, 9001), (2, 1), jnp.float32)
        _g = jnp.sign(_g) * jnp.maximum(jnp.abs(_g), 1.0) + (_g == 0) * 1.0
        g_xattn = _g[0]
        g_ffn = _g[1]
        return (x, ctx_1024, g_xattn, g_ffn)
    x, ctx_1024, g_xattn, g_ffn = _rec_inputs()

    def _L0_xattn_setup():
        import jax, jax.numpy as jnp
        import numpy as np
        NUM_HEADS = 16
        key = jax.random.key(seed)
        kq, kk, kv = jax.random.split(key, 3)
        B, S, DIM = (2, 512, 256)
        q = jax.random.normal(kq, (B, S, DIM), dtype=jnp.float32)
        k = jax.random.normal(kk, (B, S, DIM), dtype=jnp.float32)
        v = jax.random.normal(kv, (B, S, DIM), dtype=jnp.float32)
        return {'q': q, 'k': k, 'v': v}
    _L0_xattn_all = _L0_xattn_setup()
    _L0_xattn_in = {k: v for k, v in _L0_xattn_all.items() if k in ()}
    del _L0_xattn_all

    def _L0_ffn_setup():
        import jax, jax.numpy as jnp
        import numpy as np
        EMBED = 256
        HEADS = 16
        HEAD_DIM = EMBED // HEADS
        NUM_EXPERTS = 8
        TOP_K = 2
        HIDDEN = (int(2 * (4 * EMBED) / 3) + 63) // 64 * 64
        SEQ = 512
        BATCH = 2
        ROPE_BASE = 10000.0
        EPS = 1e-06

        def _rope_tables(seq_len, dim):
            inv_freq = 1.0 / ROPE_BASE ** (np.arange(0, dim, 2, dtype=np.float32) / dim)
            t = np.arange(seq_len, dtype=np.float32)
            freqs = np.einsum('i,j->ij', t, inv_freq)
            emb = np.concatenate([freqs, freqs], axis=-1)
            return (jnp.asarray(np.cos(emb)), jnp.asarray(np.sin(emb)))

        def _rotate_half(x):
            x1, x2 = jnp.split(x, 2, axis=-1)
            return jnp.concatenate([-x2, x1], axis=-1)

        def _rmsnorm(x, w):
            return x * jax.lax.rsqrt(jnp.mean(x * x, axis=-1, keepdims=True) + EPS) * w

        def _attention(x, wq, wk, wv, wo):
            B, S, _ = x.shape
            q = (x @ wq).reshape(B, S, HEADS, HEAD_DIM).transpose(0, 2, 1, 3)
            k = (x @ wk).reshape(B, S, HEADS, HEAD_DIM).transpose(0, 2, 1, 3)
            v = (x @ wv).reshape(B, S, HEADS, HEAD_DIM).transpose(0, 2, 1, 3)
            cos, sin = _rope_tables(S, HEAD_DIM)
            cos = cos[None, None]
            sin = sin[None, None]
            q = q * cos + _rotate_half(q) * sin
            k = k * cos + _rotate_half(k) * sin
            scale = HEAD_DIM ** (-0.5)
            scores = jnp.einsum('bhqd,bhkd->bhqk', q, k) * scale
            causal = jnp.triu(jnp.ones((S, S), bool), k=1)
            scores = jnp.where(causal, -jnp.inf, scores)
            attn = jax.nn.softmax(scores, axis=-1)
            out = jnp.einsum('bhqk,bhkd->bhqd', attn, v)
            out = out.transpose(0, 2, 1, 3).reshape(B, S, EMBED)
            return out @ wo

        def _moe(x, w_router, wg, wu, wd):
            B, S, E = x.shape
            xf = x.reshape(-1, E)
            logits = xf @ w_router
            probs = jax.nn.softmax(logits, axis=-1)
            topw, topi = jax.lax.top_k(probs, TOP_K)
            topw = topw / jnp.sum(topw, axis=-1, keepdims=True)
            combine = jnp.sum(jax.nn.one_hot(topi, NUM_EXPERTS, dtype=xf.dtype) * topw[..., None], axis=1)
            g = jax.nn.silu(jnp.einsum('td,xdh->txh', xf, wg))
            u = jnp.einsum('td,xdh->txh', xf, wu)
            eo = jnp.einsum('txh,xhd->txd', g * u, wd)
            out = jnp.einsum('txd,tx->td', eo, combine)
            return out.reshape(B, S, E)
        key = jax.random.key(seed)
        ks = jax.random.split(key, 12)
        s = 0.02
        return {'x': jax.random.normal(ks[0], (BATCH, SEQ, EMBED), jnp.float32), 'wq': jax.random.normal(ks[1], (EMBED, EMBED), jnp.float32) * s, 'wk': jax.random.normal(ks[2], (EMBED, EMBED), jnp.float32) * s, 'wv': jax.random.normal(ks[3], (EMBED, EMBED), jnp.float32) * s, 'wo': jax.random.normal(ks[4], (EMBED, EMBED), jnp.float32) * s, 'w_router': jax.random.normal(ks[5], (EMBED, NUM_EXPERTS), jnp.float32) * s, 'wg': jax.random.normal(ks[6], (NUM_EXPERTS, EMBED, HIDDEN), jnp.float32) * s, 'wu': jax.random.normal(ks[7], (NUM_EXPERTS, EMBED, HIDDEN), jnp.float32) * s, 'wd': jax.random.normal(ks[8], (NUM_EXPERTS, HIDDEN, EMBED), jnp.float32) * s, 'g1': jnp.ones((EMBED,), jnp.float32), 'g2': jnp.ones((EMBED,), jnp.float32)}
    _L0_ffn_all = _L0_ffn_setup()
    _L0_ffn_in = {k: v for k, v in _L0_ffn_all.items() if k in ('wq', 'wk', 'wv', 'wo', 'w_router', 'wg', 'wu', 'wd', 'g1', 'g2')}
    del _L0_ffn_all
    return {'x': x, 'ctx_1024': ctx_1024, 'g_xattn': g_xattn, 'g_ffn': g_ffn, 'L0_ffn_wq': _L0_ffn_in['wq'], 'L0_ffn_wk': _L0_ffn_in['wk'], 'L0_ffn_wv': _L0_ffn_in['wv'], 'L0_ffn_wo': _L0_ffn_in['wo'], 'L0_ffn_w_router': _L0_ffn_in['w_router'], 'L0_ffn_wg': _L0_ffn_in['wg'], 'L0_ffn_wu': _L0_ffn_in['wu'], 'L0_ffn_wd': _L0_ffn_in['wd'], 'L0_ffn_g1': _L0_ffn_in['g1'], 'L0_ffn_g2': _L0_ffn_in['g2']}

def reference(x, ctx_1024, g_xattn, g_ffn, L0_ffn_wq, L0_ffn_wk, L0_ffn_wv, L0_ffn_wo, L0_ffn_w_router, L0_ffn_wg, L0_ffn_wu, L0_ffn_wd, L0_ffn_g1, L0_ffn_g2):
    import jax
    import jax.numpy as jnp

    def _L0_xattn_ref(q, k, v):
        import jax, jax.numpy as jnp
        import numpy as np
        NUM_HEADS = 16
        B, S, dim = q.shape
        H = NUM_HEADS
        D = dim // H
        scale = D ** (-0.5)
        qh = q.reshape(B, S, H, D) * scale
        kh = k.reshape(B, S, H, D)
        vh = v.reshape(B, S, H, D)
        scores = jnp.einsum('bqhd,bkhd->bhqk', qh, kh)
        weights = jax.nn.softmax(scores, axis=-1)
        out = jnp.einsum('bhqk,bkhd->bqhd', weights, vh)
        return out.reshape(B, S, dim)

    def _L0_ffn_ref(x, wq, wk, wv, wo, w_router, wg, wu, wd, g1, g2):
        import jax, jax.numpy as jnp
        import numpy as np
        EMBED = 256
        HEADS = 16
        HEAD_DIM = EMBED // HEADS
        NUM_EXPERTS = 8
        TOP_K = 2
        HIDDEN = (int(2 * (4 * EMBED) / 3) + 63) // 64 * 64
        SEQ = 512
        BATCH = 2
        ROPE_BASE = 10000.0
        EPS = 1e-06

        def _rope_tables(seq_len, dim):
            inv_freq = 1.0 / ROPE_BASE ** (np.arange(0, dim, 2, dtype=np.float32) / dim)
            t = np.arange(seq_len, dtype=np.float32)
            freqs = np.einsum('i,j->ij', t, inv_freq)
            emb = np.concatenate([freqs, freqs], axis=-1)
            return (jnp.asarray(np.cos(emb)), jnp.asarray(np.sin(emb)))

        def _rotate_half(x):
            x1, x2 = jnp.split(x, 2, axis=-1)
            return jnp.concatenate([-x2, x1], axis=-1)

        def _rmsnorm(x, w):
            return x * jax.lax.rsqrt(jnp.mean(x * x, axis=-1, keepdims=True) + EPS) * w

        def _attention(x, wq, wk, wv, wo):
            B, S, _ = x.shape
            q = (x @ wq).reshape(B, S, HEADS, HEAD_DIM).transpose(0, 2, 1, 3)
            k = (x @ wk).reshape(B, S, HEADS, HEAD_DIM).transpose(0, 2, 1, 3)
            v = (x @ wv).reshape(B, S, HEADS, HEAD_DIM).transpose(0, 2, 1, 3)
            cos, sin = _rope_tables(S, HEAD_DIM)
            cos = cos[None, None]
            sin = sin[None, None]
            q = q * cos + _rotate_half(q) * sin
            k = k * cos + _rotate_half(k) * sin
            scale = HEAD_DIM ** (-0.5)
            scores = jnp.einsum('bhqd,bhkd->bhqk', q, k) * scale
            causal = jnp.triu(jnp.ones((S, S), bool), k=1)
            scores = jnp.where(causal, -jnp.inf, scores)
            attn = jax.nn.softmax(scores, axis=-1)
            out = jnp.einsum('bhqk,bhkd->bhqd', attn, v)
            out = out.transpose(0, 2, 1, 3).reshape(B, S, EMBED)
            return out @ wo

        def _moe(x, w_router, wg, wu, wd):
            B, S, E = x.shape
            xf = x.reshape(-1, E)
            logits = xf @ w_router
            probs = jax.nn.softmax(logits, axis=-1)
            topw, topi = jax.lax.top_k(probs, TOP_K)
            topw = topw / jnp.sum(topw, axis=-1, keepdims=True)
            combine = jnp.sum(jax.nn.one_hot(topi, NUM_EXPERTS, dtype=xf.dtype) * topw[..., None], axis=1)
            g = jax.nn.silu(jnp.einsum('td,xdh->txh', xf, wg))
            u = jnp.einsum('td,xdh->txh', xf, wu)
            eo = jnp.einsum('txh,xhd->txd', g * u, wd)
            out = jnp.einsum('txd,tx->td', eo, combine)
            return out.reshape(B, S, E)
        h = x + _attention(_rmsnorm(x, g1), wq, wk, wv, wo)
        y = h + _moe(_rmsnorm(h, g2), w_router, wg, wu, wd)
        return y
    x = x + jnp.tanh(g_xattn[0]) * _L0_xattn_ref(_layernorm(x, axis=-1), ctx_1024, ctx_1024)
    x = x + jnp.tanh(g_ffn[0]) * _L0_ffn_ref(_layernorm(x, axis=-1), L0_ffn_wq, L0_ffn_wk, L0_ffn_wv, L0_ffn_wo, L0_ffn_w_router, L0_ffn_wg, L0_ffn_wu, L0_ffn_wd, L0_ffn_g1, L0_ffn_g2)
    return x

_drawn_inputs = setup_inputs


def setup_inputs(seed=0):
    import zlib

    import numpy as np

    out = dict(_drawn_inputs(seed))
    spreads = {'L0_ffn_g1': (1.0, 0.6), 'L0_ffn_g2': (1.0, 0.2)}
    factors = {'L0_ffn_wq': 8.0, 'L0_ffn_wk': 8.0}
    for name, (base, spread) in spreads.items():
        noise = np.random.default_rng([zlib.crc32(name.encode()), seed]).standard_normal(out[name].shape)
        drawn = base * np.exp(spread * noise) if base else spread * noise
        out[name] = jnp.asarray(drawn.astype(out[name].dtype))
    for name, factor in factors.items():
        out[name] = (out[name] * factor).astype(out[name].dtype)
    return out
```

```python
from contextlib import ExitStack

import numpy as np
import concourse.bass as bass
from concourse import mybir

ALU = mybir.AluOpType
ACT = mybir.ActivationFunctionType
AX = mybir.AxisListType
F32, BF16 = mybir.dt.float32, mybir.dt.bfloat16
I32, U32 = mybir.dt.int32, mybir.dt.uint32

P = 128
B, S, D = 8, 512, 256
H, DH = 16, 16
E, F = 8, 704
QT = S // P
DC = D // P
HG = 4
G = H // HG
KROWS = 6 * DH
NEGROWS = 3
T = B * S
NT = T // P
CAP = T + P
TILES = 2 * T // P + E
SPARE = TILES - 2 * T // P
ROWS = E * CAP + SPARE * P
FH = F // 2
FC = (F + P - 1) // P
SCALE = float(DH) ** -0.5
MASKED = -3.0e38
DVE_LINKS, POOL_LINKS = 17, 21
LAST = B - 1


class Lin:

    def __init__(self, a, c):
        self.a, self.c = a, c

    def __add__(self, n):
        return Lin(self.a, self.c + n)

    def __sub__(self, n):
        return Lin(self.a, self.c - n)

    def __mul__(self, n):
        return Lin(self.a * n, self.c * n)

    __radd__, __rmul__ = __add__, __mul__


class Step:

    def __init__(self, i, reg=None):
        self.reg = reg
        v = Lin(1, 0) if reg is not None else i
        has = (lambda n: True) if reg is not None else (lambda n: 0 <= i + n <= LAST)
        self.cross = v + 1 if has(1) else None
        self.own = v + 0 if has(0) else None
        self.past = v - 1 if has(-1) else None
        self.ahead = v + 2 if has(2) else None
        if reg is not None:
            self.u_cross, self.u_own, self.u_past = Lin(2, 1), Lin(2, 2), Lin(2, 0)
        else:
            self.u_cross = 0 if i == -1 else 2 * i + 1
            self.u_own = 15 if i == LAST else 2 * i + 2
            self.u_past = 15 if i == LAST + 1 else 2 * i
        self.i = i

    def value(self, v):
        if isinstance(v, Lin):
            return self.reg * v.a + v.c if v.a else v.c
        return v

    def wait(self, eng, sem, v):
        if isinstance(v, Lin) or v > 0:
            eng.wait_ge(sem, self.value(v))

    def named(self, which):
        b, u = {"cross": (self.cross, self.u_cross), "own": (self.own, self.u_own), "past": (self.past, self.u_past)}[which]
        return None if b is None else (which, b, u)

    def max_of(self, s):
        u = self.named("cross" if s < 4 else "own")
        return u and (*u, s % 4)

    def main_of(self, s):
        which, g = [("past", 2), ("past", 3), ("cross", 0), ("cross", 1), ("cross", 2), ("cross", 3), ("own", 0), ("own", 1)][s]
        u = self.named(which)
        return u and (*u, g)

    def tail_of(self, s):
        return self.main_of(s - 1) if s else self._past(1)

    def neg_of(self, s):
        return self.max_of(s - 1) if s else self._past(3)

    def _past(self, g):
        u = self.named("past")
        return u and (*u, g)


def most(v, n):
    return v if isinstance(v, Lin) else min(v, n)


def is_self(which):
    return which != "cross"


def run_steps(eng, body):
    for i in (-2, -1, 0):
        body(Step(i))
    with eng.Fori(1, B - 2) as reg:
        body(Step(None, reg))
    for i in range(B - 2, B + 1):
        body(Step(i))


def reads_before(step, s, kind):
    of = Step.tail_of if kind == "tail" else Step.neg_of
    cur, s = step, s - 1
    while True:
        while s >= 0:
            u = of(cur, s)
            if u:
                return u[2] * G + u[3] + 1
            s -= 1
        if cur.i is None:
            return (Lin(2, 0) * G + 1) if kind == "tail" else (Lin(2, 0) * G + 3)
        if cur.i <= -2:
            return 0
        cur, s = Step(cur.i - 1), 7


def host_constants():
    p = np.arange(P)
    upper = np.where(p[None, :] > p[:, None], MASKED, 0.0)
    squares = np.stack([
        np.eye(P),
        upper,
        upper.T,
        (p[:, None] < p[None, :]) * 1.0,
        np.ones((P, P)),
    ], 1).astype(np.float32)
    inv_freq = 1.0 / 10000.0 ** (np.arange(0, DH, 2, dtype=np.float32) / DH)
    freqs = np.einsum("i,j->ij", np.arange(S, dtype=np.float32), inv_freq)
    emb = np.concatenate([freqs, freqs], -1)
    sign = np.where(np.arange(DH) < DH // 2, -1.0, 1.0).astype(np.float32)
    rope = np.stack([np.tile(np.cos(emb).T, (P // DH, 1)), np.tile((np.sin(emb) * sign).T, (P // DH, 1))], 1)
    small = np.zeros((P, 2 * E + 1), np.float32)
    small[:, :E] = np.arange(E)
    small[:, E:2 * E] = np.arange(E) * CAP
    small[:, 2 * E] = p
    return squares, rope.astype(np.float32), small


def table_constants():
    j = np.arange(TILES, dtype=np.float32)
    return np.stack([np.repeat(j[:, None], E, 1), np.repeat(j[:, None] * P, E, 1)])[None].astype(np.float32)


def flamingo_block(nc, x, ctx, g_xattn, g_ffn, wq, wk, wv, wo, w_router, wg, wu, wd, g1, g2, out):
    squares, rope, small = host_constants()
    c_squares = nc.inline_tensor(squares, "c_squares").ap()
    c_rope = nc.inline_tensor(rope, "c_rope").ap()
    c_small = nc.inline_tensor(small, "c_small").ap()
    c_table = nc.inline_tensor(table_constants(), "c_table").ap()

    def scratch(name, shape, dt=F32):
        return nc.dram_tensor(name, shape, dt, kind="Internal").ap()

    parts_d = {(a, o): scratch(f"parts_{a}_{o}", (B, 3, DH, H, S), BF16) for a in ("cross", "own") for o in "qk"}
    kept_d = scratch("kept", (B, 2, P, QT, D))
    base_d = scratch("base", (B, P, QT, D))
    rows_in = scratch("rows_in", (ROWS, D))
    rows_out = scratch("rows_out", (TILES * P, D))

    x_d = x.rearrange("b (t p) d -> b p t d", p=P)
    ctx_d = ctx.rearrange("b (t p) d -> b p t d", p=P)
    out_d = out.rearrange("b (t p) d -> (b t) p d", p=P)
    base_tiles = base_d.rearrange("b p t d -> b t p d")

    outer = ExitStack()
    with outer:
        def sb(name, shape, dt=F32, stack=None):
            return (stack or outer).enter_context(nc.sbuf_tensor(name, list(shape), dt))

        def sem(name, stack=None):
            return (stack or outer).enter_context(nc.semaphore(name))

        ident = sb("ident", (P, P))
        small_sb = sb("small_sb", (P, 2 * E + 1))
        iota_e, region_e = small_sb[:, 0:E], small_sb[:, E:2 * E]
        gate = sb("gate", (P, 2))
        g1_sb, g2_sb = sb("g1_sb", (P, DC)), sb("g2_sb", (P, DC))
        pos_all = sb("pos_all", (P, B, 2 * QT))
        mix_all = sb("mix_all", (P, B, 2 * QT))
        count = sb("count", (P, E))
        zeros = sb("zeros", (P, D))

        with ExitStack() as st:
            def s1(name, *shape, dt=F32):
                return sb(name, (P, *shape), dt, st)

            squares_sb = s1("squares_sb", 5, P)
            squares_b = s1("squares_b", 5, P, dt=BF16)
            ident_b, mask_qk, mask_kq, before_b, ones_b = (squares_b[:, n, :] for n in range(5))
            rope_sb = s1("rope_sb", 2, S)
            w_sb = {n: s1("sb_" + n, DC, D) for n in ("wq", "wk", "wv", "wo")}
            wr_sb = s1("wr_sb", DC, E)
            gates_in = sb("gates_in", (1, 2), F32, st)
            half = s1("half", 2 * QT)

            q_stack = [s1(f"q_stack{g}", HG, S, dt=BF16) for g in range(G)]
            k_stack = [s1(f"k_stack{g}", HG, S, dt=BF16) for g in range(G)]
            probs = s1("probs", 2, HG, S)
            v_of = {"cross": s1("v_cross", QT, H, 32), "own": s1("v_own", QT, H, 32)}
            x_in, ctx_in, x_again = s1("x_in", QT, D), s1("ctx_in", QT, D), s1("x_again", QT, D)
            xq = s1("xq", QT, D)
            x1, xn, hn1 = s1("x1", QT, D), s1("xn", QT, D), s1("hn1", QT, D)
            att = {"cross": s1("att_cross", QT, D), "own": s1("att_own", QT, D)}
            hn1_t, flat_q, flat_k = s1("hn1_t", DC, S), s1("flat_q", DC, S), s1("flat_k", DC, S)
            turned, with_cos = s1("turned", DC, S), s1("with_cos", DC, S)
            rest = s1("rest", DC, S)
            parts = {"q": s1("parts_q", 3, DC, S, dt=BF16), "k": s1("parts_k", 3, DC, S, dt=BF16)}
            out_t = s1("out_t", S)
            own_t = s1("own_t", DC, S)
            kept = s1("kept_sb", 2, QT, D)
            h, hn2, base = s1("h", QT, D), s1("hn2", QT, D), s1("base_sb", QT, D)
            hn2_t = s1("hn2_t", DC, S)
            neg = s1("neg", 2, HG, QT)
            neg_rest = s1("neg_rest", 2, HG * QT)
            neg_parts = s1("neg_parts", 2, NEGROWS, HG * QT, dt=BF16)
            neg_rows = sb("neg_rows", (NEGROWS * HG * QT, P), BF16, st)
            recip = s1("recip", HG * QT)
            st_x, mv_x = s1("st_x", QT, 6), s1("mv_x", QT, 2)
            st_1, mv_1 = s1("st_1", QT, 6), s1("mv_1", QT, 2)
            r_x, r_1, r_h = s1("r_x", QT), s1("r_1", 2 * QT), s1("r_h", QT)
            tmp_r = s1("tmp_r", QT)
            sq, ss = s1("sq", D), s1("ss", QT)
            lg, top, idx = s1("lg", QT, E), s1("top", QT, 8), s1("idx", QT, 8, dt=U32)
            idx_f = s1("idx_f", QT, 8)
            hot = s1("hot", 2, QT, E)
            hot_b = s1("hot_b", QT, E, dt=BF16)
            where, picked = s1("where", QT, E), s1("picked", 2, QT, E)
            pos_f, pos_i = s1("pos_f", 2 * QT), s1("pos_i", 2 * QT, dt=I32)
            gap, e_gap, mix = s1("gap", QT), s1("e_gap", QT), s1("mix", 2, QT)

            def bank(name, dt=F32, n=512):
                return st.enter_context(nc.psum_tensor(name, [P, n], dt))

            max_ps = [bank("max_ps0"), bank("max_ps1")]
            key_ps = [bank("key_ps0"), bank("key_ps1")]
            pv_ps, turn_ps = bank("pv_ps"), bank("turn_ps")
            aux = [bank("aux0"), bank("aux1")]
            turn_b = turn_ps[:, :].bitcast(BF16)

            names = """ld_const ld_w ready_c ready_b ready_v gate_mm gate_act
                max_mm max_red neg_split neg_chain neg_tr neg_ev neg_dma
                key_mm exp_done pv_mm out_ev post_tr post_norm post_rc
                x_ld ctx_ld xa_ld kept_ld kept_st base_st x_stat x_rstd x_norm x_tr x_ev c_tr c_ev v_cross
                x1_stat x1_rstd x1_norm dve pool hn1_tr hn1_ev q_mm q_ev k_mm k_ev v_mm v_ev
                rope_q rope_k rope_used x_parts c_parts oq_parts ok_parts x_st c_st oq_st ok_st
                own_tr own_ev wo_mm h_sum h_sq h_rstd h_norm h_base hn2_tr hn2_ev lg_mm gap_r gap_exp hot_r rank_mm
                rank_r route scat route_r""".split()
            m = {n: sem("s_" + n, st) for n in names}
            s_stack = [sem(f"s_stack{g}", st) for g in range(G)]

            class Chain:

                def __init__(self, eng, s):
                    self.eng, self.s, self.n, self.per, self.start = eng, s, 0, 0, 0

                def link(self, ins, step=None):
                    ins.then_inc(self.s, 1)
                    self.n += 1
                    if step is None or step.reg is None:
                        self.eng.wait_ge(self.s, self.n)
                    else:
                        wait_apart(step, self.eng, (self.s, Lin(self.per, self.n - self.per)))

                def loop_body(self, step, body, per):
                    if step.reg is None:
                        return body(step)
                    before, self.per = self.n, per
                    body(step)
                    assert self.n - before == per, (self.n - before, per)
                    self.n = before + per * (B - 3)

            block = st.enter_context(nc.Block())

            def wait_apart(step, eng, *waits):
                values = [(s_, step.value(v)) for s_, v in waits]
                for s_, v in values:
                    if not isinstance(v, int):
                        eng.compute_val(v)
                eng.wait_ge(m["ready_c"], 1)
                for s_, v in values:
                    if not isinstance(v, int) or v > 0:
                        eng.wait_ge(s_, v)

            @block.sync
            def _(sp):
                sp.dma_start(squares_sb[:, :, :], c_squares).then_inc(m["ld_const"], 16)
                sp.dma_start(ident[:, :], c_squares[:, 0, :]).then_inc(m["ld_const"], 16)
                sp.dma_start(rope_sb[:, :, :], c_rope).then_inc(m["ld_const"], 16)
                sp.dma_start(small_sb[:, :], c_small).then_inc(m["ld_const"], 16)
                sp.dma_start(gates_in[:, 0:1], g_xattn.rearrange("(a n) -> a n", a=1)).then_inc(m["ld_const"], 16)
                sp.dma_start(gates_in[:, 1:2], g_ffn.rearrange("(a n) -> a n", a=1)).then_inc(m["ld_const"], 16)
                sp.dma_start(g1_sb[:, :], g1.rearrange("(c p) -> p c", p=P), allow_slow_non_contiguous=True).then_inc(m["ld_const"], 16)
                sp.dma_start(g2_sb[:, :], g2.rearrange("(c p) -> p c", p=P), allow_slow_non_contiguous=True).then_inc(m["ld_const"], 16)

                def load_x(step):
                    if step.ahead is None:
                        return
                    b = step.ahead
                    step.wait(sp, m["x_norm"], b)
                    sp.dma_start(x_in[:, :, :], x_d[step.value(b)]).then_inc(m["x_ld"], 16)
                    step.wait(sp, m["c_tr"], b)
                    step.wait(sp, m["v_cross"], b)
                    sp.dma_start(ctx_in[:, :, :], ctx_d[step.value(b)]).then_inc(m["ctx_ld"], 16)

                def load_stack(step, which, b, u, g):
                    wait_apart(step, sp, (m["key_mm"], (u - 1) * (16 * G) + (16 * g + 16)))
                    kind = "own" if is_self(which) else "cross"
                    q_d, k_d = (parts_d[kind, o][step.value(b)] for o in "qk")
                    hs = slice(g * HG, (g + 1) * HG)
                    if g == 0:
                        step.wait(sp, m["oq_st" if kind == "own" else "x_st"], (b + 1) * 96)
                        step.wait(sp, m["ok_st" if kind == "own" else "c_st"], (b + 1) * 96)
                    for r0, n in ((0, 3), (3, 2), (5, 1)):
                        sp.dma_start(q_stack[g][r0 * DH:(r0 + n) * DH, :, :],
                                     q_d[0:n, :, hs, :].rearrange("p d h t -> (p d) h t")).then_inc(s_stack[g], 16)
                    for r, part in enumerate((0, 0, 0, 1, 1, 2)):
                        sp.dma_start(k_stack[g][r * DH:(r + 1) * DH, :, :], k_d[part, :, hs, :]).then_inc(s_stack[g], 16)

                def store_parts(step, kind, o, b, ready, done):
                    step.wait(sp, m[ready], b + 1)
                    for part in range(3):
                        for c in range(DC):
                            dst = parts_d[kind, o][step.value(b)][part, :, c * 8:(c + 1) * 8, :]
                            sp.dma_start(dst.rearrange("d h t -> h d t"), parts[o][:, part, c, :]).then_inc(m[done], 16)

                def body(step):
                    cross, own, past, ahead = step.cross, step.own, step.past, step.ahead
                    if cross is not None:
                        load_stack(step, "cross", cross, step.u_cross, 1)
                    if own is not None:
                        step.wait(sp, m["x1_norm"], own + 1)
                        sp.dma_start(kept_d[step.value(own), 0], x1[:, :, :]).then_inc(m["kept_st"], 16)
                        sp.dma_start(kept_d[step.value(own), 1], xn[:, :, :]).then_inc(m["kept_st"], 16)
                    load_x(step)
                    if cross is not None:
                        load_stack(step, "cross", cross, step.u_cross, 2)
                    if past is not None:
                        wait_apart(step, sp, (m["kept_st"], (past + 1) * 32), (m["h_base"], past))
                        for n in range(2):
                            sp.dma_start(kept[:, n, :, :], kept_d[step.value(past), n]).then_inc(m["kept_ld"], 16)
                    if cross is not None:
                        load_stack(step, "cross", cross, step.u_cross, 3)
                        step.wait(sp, m["x1_stat"], cross)
                        sp.dma_start(x_again[:, :, :], x_d[step.value(cross)]).then_inc(m["xa_ld"], 16)
                    if own is not None:
                        store_parts(step, "own", "q", own, "oq_parts", "oq_st")
                        store_parts(step, "own", "k", own, "ok_parts", "ok_st")
                        for g in range(G):
                            if g == 2 and past is not None:
                                step.wait(sp, m["h_base"], past + 1)
                                sp.dma_start(base_d[step.value(past)], base[:, :, :]).then_inc(m["base_st"], 16)
                            load_stack(step, "own", own, step.u_own, g)
                    elif past is not None:
                        step.wait(sp, m["h_base"], past + 1)
                        sp.dma_start(base_d[step.value(past)], base[:, :, :]).then_inc(m["base_st"], 16)
                    if ahead is not None:
                        store_parts(step, "cross", "q", ahead, "x_parts", "x_st")
                        store_parts(step, "cross", "k", ahead, "c_parts", "c_st")
                        u_next = 0 if step.i == -2 else step.u_own + 1
                        load_stack(step, "cross", ahead, u_next, 0)

                first = Step(-2)
                load_x(first)
                for name, w in (("wq", wq), ("wk", wk), ("wv", wv), ("wo", wo)):
                    sp.dma_start(w_sb[name][:, :, :], w.rearrange("(c p) n -> p c n", p=P)).then_inc(m["ld_w"], 16)
                sp.dma_start(wr_sb[:, :, :], w_router.rearrange("(c p) n -> p c n", p=P)).then_inc(m["ld_w"], 16)
                sp.wait_ge(m["ready_v"], 1)
                for n in range(SPARE):
                    sp.dma_start(rows_in[E * CAP + n * P:E * CAP + (n + 1) * P, :], zeros[:, :]).then_inc(m["ld_w"], 16)
                def sp_body(step):
                    if step.i == -2:
                        store_parts(step, "cross", "q", 0, "x_parts", "x_st")
                        store_parts(step, "cross", "k", 0, "c_parts", "c_st")
                        load_stack(step, "cross", 0, 0, 0)
                    else:
                        body(step)

                run_steps(sp, sp_body)
                sp.wait_ge(m["base_st"], 16 * B)
                sp.wait_ge(m["kept_st"], 32 * B)
                sp.wait_ge(m["ld_w"], 16 * (5 + SPARE))

            @block.tensor
            def _(pe):
                mm = nc.tensor.matmul
                tr = nc.tensor.transpose
                pe.wait_ge(m["ready_c"], 1)
                pe.wait_ge(m["ready_b"], 1)
                pe.wait_ge(m["ready_v"], 2)
                pe.wait_ge(m["ld_const"], 16 * 8)
                pe.wait_ge(m["ld_w"], 16 * (5 + SPARE))
                mm(aux[0][:, 0:2], squares_sb[0:1, 4, :], gates_in[0:1, 0:2], start=True, stop=True).then_inc(m["gate_mm"], 1)
                pe.wait_ge(m["gate_act"], 1)

                def max_unit(step, unit, qt, hd):
                    which, b, u, g = unit
                    n = u * G + g
                    j = HG * qt + hd
                    if j == 0:
                        step.wait(pe, s_stack[g], (u + 1) * (9 * 16))
                    step.wait(pe, m["max_red"], n * 16 + (j - 1))
                    own = is_self(which)
                    keys = (qt + 1) * P if own else S
                    ps = max_ps[j % 2]
                    r = mm(ps[:, 0:keys], q_stack[g][0:KROWS, hd, qt * P:(qt + 1) * P], k_stack[g][0:KROWS, hd, 0:keys],
                           start=True, stop=not own)
                    if own:
                        r = mm(ps[:, qt * P:keys], ident_b, mask_qk, start=False, stop=True)
                    r.then_inc(m["max_mm"], 1)

                def key_unit(step, unit, kt, hd):
                    which, b, u, g = unit
                    n = u * G + g
                    j = HG * kt + hd
                    if j == 0:
                        step.wait(pe, m["neg_dma"], (n + 1) * 16)
                    step.wait(pe, m["exp_done"], n * 16 + (j - 1))
                    own = is_self(which)
                    q0 = kt * P if own else 0
                    ps = key_ps[j % 2]
                    r = mm(ps[:, q0:S], k_stack[g][0:KROWS + NEGROWS, hd, kt * P:(kt + 1) * P],
                           q_stack[g][0:KROWS + NEGROWS, hd, q0:S], start=True, stop=not own)
                    if own:
                        r = mm(ps[:, q0:q0 + P], ident_b, mask_kq, start=False, stop=True)
                    r.then_inc(m["key_mm"], 1)

                def value_unit(step, unit, kt):
                    which, b, u, g = unit
                    n = u * G + g
                    step.wait(pe, m["exp_done"], n * 16 + HG * (kt + 1))
                    own = is_self(which)
                    if kt == 0:
                        step.wait(pe, m["out_ev"], n)
                        if g == 0:
                            step.wait(pe, m["v_ev" if own else "v_cross"], (b + 1) * (DC if own else 1))
                    q0 = kt * P if own else 0
                    for hd in range(HG):
                        r = mm(pv_ps[32 * hd:32 * hd + 32, q0:S], v_of["own" if own else "cross"][:, kt, g * HG + hd, :],
                               probs[:, kt % 2, hd, q0:S], start=(kt == 0), stop=(kt == QT - 1), skip_group_check=True)
                    r.then_inc(m["pv_mm"], 1)

                def neg_turn(step, s):
                    unit = step.neg_of(s)
                    if not unit:
                        return
                    n = unit[2] * G + unit[3]
                    wait_apart(step, pe, (m["neg_split"], n + 1), (m["neg_ev"], n), (m["post_norm"], reads_before(step, s, "tail")))
                    tr(turn_b[0:NEGROWS * HG * QT, 0:P], neg_parts[:, unit[3] % 2, :, :].rearrange("p a b -> p (a b)"), ident_b)\
                        .then_inc(m["neg_tr"], 1)

                def post_turn(step, s):
                    unit = step.tail_of(s)
                    if not unit:
                        return
                    n = unit[2] * G + unit[3]
                    step.wait(pe, m["out_ev"], n + 1)
                    step.wait(pe, m["post_norm"], n)
                    step.wait(pe, m["neg_ev"], reads_before(step, s + 1, "neg"))
                    for qt in range(QT):
                        r = tr(turn_ps[:, qt * P:(qt + 1) * P], out_t[:, qt * P:(qt + 1) * P], ident[:, :])
                    r.then_inc(m["post_tr"], 1)

                def turn(dst, src, done):
                    for c in range(DC):
                        for t in range(QT):
                            r = tr(dst[c][:, t * P:(t + 1) * P], src[:, t, c * P:(c + 1) * P], ident[:, :])
                        r.then_inc(m[done], 1)

                def project(dst, w, src, done):
                    for o in range(DC):
                        for c in range(DC):
                            r = mm(dst[o][:, :], w[:, c, o * P:(o + 1) * P], src[:, c, :], start=(c == 0), stop=(c == DC - 1))
                        r.then_inc(m[done], 1)

                def project_rows(dst, src, w, done):
                    for t in range(QT):
                        for c in range(DC):
                            r = mm(dst[t // 2][:, (t % 2) * D:(t % 2 + 1) * D], src[:, c, t * P:(t + 1) * P], w[:, c, :],
                                   start=(c == 0), stop=(c == DC - 1))
                        if t % 2:
                            r.then_inc(m[done], 1)

                def extra(step, s, kt):
                    cross, own, past, ahead = step.cross, step.own, step.past, step.ahead
                    at = (s, kt)
                    if at == (0, 0) and own is not None:
                        step.wait(pe, m["x1_norm"], own + 1)
                        step.wait(pe, m["rank_r"], own - 1)
                        step.wait(pe, m["c_ev"], most(own + 2, B) * DC)
                        step.wait(pe, m["hn2_ev"], (own - 1) * DC)
                        turn(aux, hn1, "hn1_tr")
                    if at == (0, 2) and own is not None:
                        step.wait(pe, m["hn1_ev"], (own + 1) * DC)
                        project(aux, w_sb["wq"], hn1_t, "q_mm")
                    if at == (1, 1) and own is not None:
                        step.wait(pe, m["q_ev"], (own + 1) * DC)
                        project(aux, w_sb["wk"], hn1_t, "k_mm")
                    if at == (2, 2) and own is not None:
                        step.wait(pe, m["k_ev"], (own + 1) * DC)
                        project_rows(aux, hn1_t, w_sb["wv"], "v_mm")
                    if at == (3, 1) and past is not None:
                        step.wait(pe, m["post_norm"], step.u_past * G + 4)
                        step.wait(pe, m["v_ev"], most(past + 2, B) * DC)
                        step.wait(pe, m["rank_r"], past)
                        turn(aux, att["own"], "own_tr")
                    if at == (3, 3) and past is not None:
                        step.wait(pe, m["own_ev"], (past + 1) * DC)
                        project_rows(aux, own_t, w_sb["wo"], "wo_mm")
                    if at == (4, 2) and ahead is not None:
                        step.wait(pe, m["x_norm"], ahead + 1)
                        if past is not None:
                            step.wait(pe, m["h_sum"], (past + 1) * DC)
                        elif own is not None:
                            step.wait(pe, m["v_ev"], (own + 1) * DC)
                        else:
                            step.wait(pe, m["c_ev"], ahead * DC)
                        turn(aux, xq, "x_tr")
                    if at == (5, 0) and ahead is not None:
                        step.wait(pe, m["x_ev"], (ahead + 1) * DC)
                        step.wait(pe, m["ctx_ld"], (ahead + 1) * 16)
                        turn(aux, ctx_in, "c_tr")
                    if at == (5, 2) and past is not None:
                        step.wait(pe, m["h_norm"], past + 1)
                        step.wait(pe, m["h_sum"], (past + 1) * DC)
                        if ahead is not None:
                            step.wait(pe, m["c_ev"], (ahead + 1) * DC)
                        turn(aux, hn2, "hn2_tr")
                    if at == (6, 0) and past is not None:
                        step.wait(pe, m["hn2_ev"], (past + 1) * DC)
                        for t in range(QT):
                            for c in range(DC):
                                r = mm(aux[0][:, t * E:(t + 1) * E], hn2_t[:, c, t * P:(t + 1) * P], wr_sb[:, c, :],
                                       start=(c == 0), stop=(c == DC - 1))
                        r.then_inc(m["lg_mm"], 1)
                    if at == (6, 3) and past is not None:
                        step.wait(pe, m["hot_r"], past + 1)
                        for t in range(QT + 1):
                            for s_ in range(min(t + 1, QT)):
                                r = mm(aux[1][:, t * E:(t + 1) * E], before_b if s_ == t else ones_b, hot_b[:, s_, :],
                                       start=(s_ == 0), stop=(s_ == min(t, QT - 1)))
                        r.then_inc(m["rank_mm"], 1)

                def body(step):
                    for s in range(8):
                        mx, mn, tail = step.max_of(s), step.main_of(s), step.tail_of(s)
                        for kt in range(QT):
                            extra(step, s, kt)
                            for hd in range(HG):
                                if mx:
                                    max_unit(step, mx, kt, hd)
                                if mn:
                                    key_unit(step, mn, kt, hd)
                            if kt == 0 and tail:
                                value_unit(step, tail, QT - 1)
                            if kt and mn:
                                value_unit(step, mn, kt - 1)
                            if kt == 2:
                                neg_turn(step, s)
                            if kt == 3:
                                post_turn(step, s)

                run_steps(pe, body)

            @block.scalar
            def _(act):
                act.wait_ge(m["gate_mm"], 1)
                act.activation(gate[:, :], aux[0][:, 0:2], ACT.Tanh).then_inc(m["gate_act"], 1)
                act.wait_ge(m["ld_const"], 16 * 8)

                def exp_unit(step, unit, kt, hd):
                    which, b, u, g = unit
                    n = u * G + g
                    j = HG * kt + hd
                    step.wait(act, m["key_mm"], n * 16 + (j + 1))
                    if hd == 0:
                        step.wait(act, m["pv_mm"], n * QT + (kt - 1))
                    q0 = kt * P if is_self(which) else 0
                    act.activation(probs[:, kt % 2, hd, q0:S], key_ps[j % 2][:, q0:S], ACT.Exp).then_inc(m["exp_done"], 1)

                def evacuate(step, which, mm_done, ev_done, dst, src, scale=1.0):
                    b = which
                    for c in range(DC):
                        step.wait(act, m[mm_done], b * DC + (c + 1))
                        sc = scale[:, c:c + 1] if not isinstance(scale, float) else scale
                        act.activation(dst[:, c, :], src[c][:, :], ACT.Copy if isinstance(scale, float) else ACT.Identity, scale=sc)\
                            .then_inc(m[ev_done], 1)

                def extra(step, s, kt):
                    cross, own, past, ahead = step.cross, step.own, step.past, step.ahead
                    at = (s, kt)
                    if at == (0, 1) and own is not None:
                        step.wait(act, m["v_mm"], own * DC)
                        evacuate(step, own, "hn1_tr", "hn1_ev", hn1_t, aux, g1_sb)
                    if at == (0, 3) and own is not None:
                        step.wait(act, m["x_parts"], most(own + 2, B))
                        evacuate(step, own, "q_mm", "q_ev", flat_q, aux, SCALE)
                    if at == (1, 2) and own is not None:
                        step.wait(act, m["c_parts"], most(own + 2, B))
                        evacuate(step, own, "k_mm", "k_ev", flat_k, aux)
                    if at == (2, 3) and own is not None:
                        if past is not None:
                            step.wait(act, m["pv_mm"], step.u_past * (G * QT) + G * QT)
                        for c in range(DC):
                            step.wait(act, m["v_mm"], own * DC + (c + 1))
                            act.activation(v_of["own"][:, 2 * c:2 * c + 2, :, 0:DH],
                                           aux[c][:, :].rearrange("p (t h d) -> p t h d", t=2, d=DH), ACT.Copy).then_inc(m["v_ev"], 1)
                    if at == (3, 2) and past is not None:
                        step.wait(act, m["wo_mm"], past * DC)
                        evacuate(step, past, "own_tr", "own_ev", own_t, aux)
                    if at == (4, 2) and past is not None:
                        step.wait(act, m["h_sum"], (past + 1) * DC)
                        step.wait(act, m["h_rstd"], past)
                        for t in range(QT):
                            step.wait(act, m["h_sq"], past * QT + t)
                            act.activation(sq[:, :], h[:, t, :], ACT.Square, accum_out=ss[:, t:t + 1]).then_inc(m["h_sq"], 1)
                    if at == (4, 3) and ahead is not None:
                        step.wait(act, m["x_parts"], ahead)
                        if own is not None:
                            step.wait(act, m["oq_parts"], own + 1)
                        evacuate(step, ahead, "x_tr", "x_ev", flat_q, aux, SCALE)
                    if at == (5, 1) and ahead is not None:
                        step.wait(act, m["c_parts"], ahead)
                        if own is not None:
                            step.wait(act, m["ok_parts"], own + 1)
                        evacuate(step, ahead, "c_tr", "c_ev", flat_k, aux)
                    if at == (5, 3) and past is not None:
                        step.wait(act, m["lg_mm"], past)
                        evacuate(step, past, "hn2_tr", "hn2_ev", hn2_t, aux, g2_sb)
                    if at == (6, 2) and past is not None:
                        step.wait(act, m["gap_r"], past + 1)
                        act.activation(e_gap[:, :], gap[:, :], ACT.Exp).then_inc(m["gap_exp"], 1)

                def body(step):
                    for s in range(8):
                        mn, tail, ng = step.main_of(s), step.tail_of(s), step.neg_of(s)
                        for kt in range(QT):
                            if kt == 1 and tail:
                                n = tail[2] * G + tail[3]
                                step.wait(act, m["pv_mm"], (n + 1) * QT)
                                step.wait(act, m["post_tr"], n)
                                act.activation(out_t[:, :], pv_ps[:, :], ACT.Copy).then_inc(m["out_ev"], 1)
                            if kt == 3 and ng:
                                n = ng[2] * G + ng[3]
                                step.wait(act, m["neg_tr"], n + 1)
                                step.wait(act, m["neg_dma"], n * 16)
                                act.activation(neg_rows[:, :], turn_b[0:NEGROWS * HG * QT, 0:P], ACT.Copy).then_inc(m["neg_ev"], 1)
                                step.wait(act, m["neg_ev"], n + 1)
                                act.dma_start(q_stack[ng[3]][KROWS:KROWS + NEGROWS, :, :], neg_rows[:, :]).then_inc(m["neg_dma"], 16)
                            extra(step, s, kt)
                            if mn:
                                for hd in range(HG):
                                    exp_unit(step, mn, kt, hd)

                run_steps(act, body)

            @block.vector
            def _(dve):
                v = nc.vector
                chain = Chain(dve, m["dve"])
                dve.wait_ge(m["ld_const"], 16 * 8)
                v.tensor_copy(squares_b[:, :, :], squares_sb[:, :, :]).then_inc(m["ready_c"], 1)
                v.memset(count[:, :], 0.0)
                v.memset(half[:, :], -0.5)
                v.memset(zeros[:, :], 0.0).then_inc(m["ready_v"], 1)
                for g in range(G):
                    chain.link(v.memset(k_stack[g][KROWS:KROWS + NEGROWS, :, :], 1.0))
                for kind in ("cross", "own"):
                    chain.link(v.memset(v_of[kind][:, :, :, DH + 1:32], 0.0))
                    chain.link(v.memset(v_of[kind][:, :, :, DH:DH + 1], 1.0))
                v.memset(gap[:, :], 0.0).then_inc(m["ready_b"], 1)
                v.memset(e_gap[:, :], 0.0).then_inc(m["ready_v"], 1)

                def reduce_unit(step, unit, qt, hd):
                    which, b, u, g = unit
                    n = u * G + g
                    j = HG * qt + hd
                    step.wait(dve, m["max_mm"], n * 16 + (j + 1))
                    if j == 0:
                        step.wait(dve, m["neg_split"], n - 1)
                    keys = (qt + 1) * P if is_self(which) else S
                    v.tensor_reduce(neg[:, g % 2, hd, qt:qt + 1], max_ps[j % 2][:, 0:keys], op=ALU.max, axis=AX.X,
                                    negate=True).then_inc(m["max_red"], 1)

                def split_neg(step, unit):
                    n, g2 = unit[2] * G + unit[3], unit[3] % 2
                    step.wait(dve, m["max_red"], (n + 1) * 16)
                    step.wait(dve, m["neg_tr"], n - 1)
                    src = neg[:, g2, :, :].rearrange("p a b -> p (a b)")
                    r = neg_rest[:, g2, :]
                    v.tensor_copy(neg_parts[:, g2, 0, :], src).then_inc(m["neg_chain"], 1)
                    step.wait(dve, m["neg_chain"], n * 3 + 1)
                    v.tensor_tensor(r, src, neg_parts[:, g2, 0, :], ALU.subtract).then_inc(m["neg_chain"], 1)
                    step.wait(dve, m["neg_chain"], n * 3 + 2)
                    v.tensor_copy(neg_parts[:, g2, 1, :], r).then_inc(m["neg_chain"], 1)
                    step.wait(dve, m["neg_chain"], n * 3 + 3)
                    v.tensor_tensor(neg_parts[:, g2, 2, :], r, neg_parts[:, g2, 1, :], ALU.subtract).then_inc(m["neg_split"], 1)

                def post_norm(step, unit):
                    which, b, u, g = unit
                    n = u * G + g
                    kind = "own" if is_self(which) else "cross"
                    step.wait(dve, m["post_tr"], n + 1)
                    step.wait(dve, m["post_norm"], n)
                    if g == 0 and kind == "own":
                        step.wait(dve, m["own_tr"], b * DC)
                    if g == 0 and kind == "cross":
                        step.wait(dve, m["x1_stat"], b)
                    o = turn_ps[:, :].rearrange("p (t e) -> p t e", e=32)
                    v.reciprocal(recip[:, :].rearrange("p (t e) -> p t e", e=1), o[:, :, DH:DH + 1]).then_inc(m["post_rc"], 1)
                    step.wait(dve, m["post_rc"], n + 1)
                    src = turn_ps[:, :].rearrange("p (t h e) -> p t h e", h=HG, e=32)[:, :, :, 0:DH]
                    dst = att[kind][:, :, g * HG * DH:(g + 1) * HG * DH].rearrange("p t (h d) -> p t h d", d=DH)
                    rc = recip[:, :].rearrange("p (t h e) -> p t h e", h=HG, e=1).broadcast_to([P, QT, HG, DH])
                    v.tensor_tensor(dst, src, rc, ALU.mult).then_inc(m["post_norm"], 1)

                def layer_stats(src, st_, mv_, step):
                    for t in range(QT):
                        r = v.bn_stats(st_[:, t, :], src[:, t, :])
                    chain.link(r, step)
                    for t in range(QT):
                        r = v.bn_aggr(mv_[:, t, :], st_[:, t, :])
                    return r

                def extra(step, s, kt):
                    cross, own, past, ahead = step.cross, step.own, step.past, step.ahead
                    at = (s, kt)
                    if at in ((0, 3), (1, 3)) and own is not None:
                        flat, ev, done, used, prev = (
                            (flat_q, "q_ev", "rope_q", "ok_parts", own) if s == 0 else (flat_k, "k_ev", "rope_k", "oq_parts", own + 1))
                        step.wait(dve, m[ev], (own + 1) * DC)
                        step.wait(dve, m["rope_used"], own * 2 + s)
                        cos = rope_sb[:, 0:1, :].broadcast_to([P, DC, S])
                        swap = [(p + DH // 2) % DH + (p // DH) * DH for p in range(32)]
                        v.tensor_tensor(with_cos[:, :, :], flat[:, :, :], cos, ALU.mult).then_inc(m[done], 1)
                        v.stream_shuffle(out=turned[:, :, :], in_=flat[:, :, :], mask=swap).then_inc(m[done], 1)
                    if at == (3, 0) and ahead is not None:
                        step.wait(dve, m["x_ld"], (ahead + 1) * 16)
                        step.wait(dve, m["x_rstd"], ahead)
                        layer_stats(x_in, st_x, mv_x, step).then_inc(m["x_stat"], 1)
                    if at == (4, 0) and ahead is not None:
                        step.wait(dve, m["x_rstd"], ahead + 1)
                        step.wait(dve, m["x_tr"], ahead * DC)
                        step.wait(dve, m["x_stat"], ahead + 1)
                        for t in range(QT):
                            r = v.tensor_scalar(xq[:, t, :], x_in[:, t, :], mv_x[:, t, 0:1], r_x[:, t:t + 1], ALU.subtract, ALU.mult)
                        r.then_inc(m["x_norm"], 1)
                    if at == (4, 1) and past is not None:
                        step.wait(dve, m["kept_ld"], (past + 1) * 32)
                        step.wait(dve, m["h_norm"], past)
                        step.wait(dve, m["h_sq"], past * QT)
                        for c in range(DC):
                            step.wait(dve, m["wo_mm"], past * DC + (c + 1))
                            v.tensor_tensor(h[:, 2 * c:2 * c + 2, :], kept[:, 1, 2 * c:2 * c + 2, :],
                                            aux[c][:, :].rearrange("p (t d) -> p t d", t=2), ALU.add).then_inc(m["h_sum"], 1)
                        step.wait(dve, m["h_sum"], (past + 1) * DC)
                        step.wait(dve, m["base_st"], past * 16)
                        v.scalar_tensor_tensor(out=base[:, :, :], in0=h[:, :, :], scalar=gate[:, 1:2], in1=kept[:, 0, :, :],
                                               op0=ALU.mult, op1=ALU.add).then_inc(m["h_base"], 1)
                    if at == (5, 0) and past is not None:
                        step.wait(dve, m["h_rstd"], past + 1)
                        step.wait(dve, m["hn2_tr"], past * DC)
                        step.wait(dve, m["scat"], past * (2 * QT * 16))
                        for t in range(QT):
                            r = v.tensor_scalar(hn2[:, t, :], h[:, t, :], r_h[:, t:t + 1], None, ALU.mult)
                        r.then_inc(m["h_norm"], 1)
                    if at == (6, 1) and past is not None:
                        step.wait(dve, m["lg_mm"], past + 1)
                        chain.link(v.tensor_copy(lg[:, :, :], aux[0][:, 0:QT * E].rearrange("p (t e) -> p t e", e=E)), step)
                        for t in range(QT):
                            r = v.max(top[:, t, :], lg[:, t, :])
                        chain.link(r, step)
                        step.wait(dve, m["gap_exp"], past)
                        v.tensor_tensor(gap[:, :].rearrange("p (t e) -> p t e", e=1), top[:, :, 1:2], top[:, :, 0:1], ALU.subtract)\
                            .then_inc(m["gap_r"], 1)
                        for t in range(QT):
                            r = v.max_index(idx[:, t, :], top[:, t, :], lg[:, t, :])
                        chain.link(r, step)
                        chain.link(v.tensor_copy(idx_f[:, :, :], idx[:, :, :]), step)
                        experts = iota_e.rearrange("p (t e) -> p t e", t=1).broadcast_to([P, QT, E])
                        for k in range(2):
                            r = v.tensor_tensor(hot[:, k, :, :], idx_f[:, :, k:k + 1].broadcast_to([P, QT, E]), experts, ALU.is_equal)
                        chain.link(r, step)
                        step.wait(dve, m["rank_mm"], past)
                        v.tensor_tensor(hot_b[:, :, :], hot[:, 0, :, :], hot[:, 1, :, :], ALU.add).then_inc(m["hot_r"], 1)
                    if at == (7, 0) and past is not None:
                        step.wait(dve, m["rank_mm"], past + 1)
                        step.wait(dve, m["hot_r"], past + 1)
                        ranks = aux[1][:, 0:QT * E].rearrange("p (t e) -> p t e", e=E)
                        so_far = count[:, :].rearrange("p (t e) -> p t e", t=1).broadcast_to([P, QT, E])
                        regions = region_e.rearrange("p (t e) -> p t e", t=1).broadcast_to([P, QT, E])
                        chain.link(v.tensor_tensor(where[:, :, :], ranks, so_far, ALU.add), step)
                        chain.link(v.tensor_tensor(count[:, :], aux[1][:, QT * E:(QT + 1) * E], count[:, :], ALU.add), step)
                        v.tensor_tensor(where[:, :, :], where[:, :, :], regions, ALU.add).then_inc(m["rank_r"], 1)
                        step.wait(dve, m["rank_r"], past + 1)
                        for k in range(2):
                            r = v.tensor_tensor(picked[:, k, :, :], where[:, :, :], hot[:, k, :, :], ALU.mult)
                        chain.link(r, step)
                        chain.link(v.tensor_reduce(pos_f[:, :], picked[:, :, :, :].rearrange("p k t e -> p (k t) e"), op=ALU.add, axis=AX.X), step)
                        step.wait(dve, m["scat"], past * (2 * QT * 16))
                        v.tensor_copy(pos_i[:, :], pos_f[:, :]).then_inc(m["route"], 1)
                        v.tensor_copy(pos_all[:, bass.ds(step.value(past), 1), :].rearrange("p a b -> p (a b)"), pos_f[:, :])
                        step.wait(dve, m["gap_exp"], past + 1)
                        chain.link(v.tensor_scalar(mix[:, 1, :], e_gap[:, :], 1.0, None, ALU.add), step)
                        chain.link(v.reciprocal(mix[:, 0, :], mix[:, 1, :]), step)
                        chain.link(v.tensor_tensor(mix[:, 1, :], mix[:, 0, :], e_gap[:, :], ALU.mult), step)
                        chain.link(v.tensor_scalar(mix_all[:, bass.ds(step.value(past), 1), :].rearrange("p a b -> p (a b)"),
                                                   mix[:, :, :].rearrange("p a b -> p (a b)"), gate[:, 1:2], None, ALU.mult), step)
                    if at == (7, 1) and cross is not None:
                        step.wait(dve, m["xa_ld"], (cross + 1) * 16)
                        step.wait(dve, m["post_norm"], step.u_cross * G + 4)
                        step.wait(dve, m["kept_st"], cross * 32)
                        chain.link(v.scalar_tensor_tensor(out=x1[:, :, :], in0=att["cross"][:, :, :], scalar=gate[:, 0:1],
                                                          in1=x_again[:, :, :], op0=ALU.mult, op1=ALU.add), step)
                        step.wait(dve, m["x1_rstd"], cross)
                        layer_stats(x1, st_1, mv_1, step).then_inc(m["x1_stat"], 1)
                    if at == (7, 3) and cross is not None:
                        step.wait(dve, m["x1_rstd"], cross + 1)
                        step.wait(dve, m["x1_stat"], cross + 1)
                        step.wait(dve, m["hn1_tr"], cross * DC)
                        for t in range(QT):
                            r = v.tensor_scalar(xn[:, t, :], x1[:, t, :], mv_1[:, t, 0:1], r_1[:, t:t + 1], ALU.subtract, ALU.mult)
                        chain.link(r, step)
                        for t in range(QT):
                            r = v.tensor_scalar(hn1[:, t, :], xn[:, t, :], r_1[:, QT + t:QT + t + 1], None, ALU.mult)
                        r.then_inc(m["x1_norm"], 1)

                def body(step):
                    for s in range(8):
                        mx, tail = step.max_of(s), step.tail_of(s)
                        for kt in range(QT):
                            extra(step, s, kt)
                            if mx:
                                for hd in range(HG):
                                    reduce_unit(step, mx, kt, hd)
                        if tail:
                            post_norm(step, tail)
                        if mx:
                            split_neg(step, mx)

                run_steps(dve, lambda step: chain.loop_body(step, body, DVE_LINKS))

            @block.gpsimd
            def _(pool):
                g_ = nc.gpsimd
                chain = Chain(pool, m["pool"])
                pool.wait_ge(m["ready_v"], 2)

                def split(step, src, dst, done, after, sent):
                    flat = lambda a: a.rearrange("p a b -> p (a b)")
                    s_, r = flat(src[:, :, :]), flat(rest[:, :, :])
                    p_ = [flat(dst[:, n, :, :]) for n in range(3)]
                    wait_apart(step, pool, (m[sent[0]], sent[1]))
                    chain.link(g_.tensor_scalar(p_[0], s_, 1.0, 0.0, ALU.mult, ALU.add), step)
                    chain.link(g_.tensor_tensor(r, s_, p_[0], ALU.subtract), step)
                    chain.link(g_.tensor_scalar(p_[1], r, 1.0, 0.0, ALU.mult, ALU.add), step)
                    g_.tensor_tensor(p_[2], r, p_[1], ALU.subtract).then_inc(m[done], 1)
                    wait_apart(step, pool, (m[done], after))

                def rsqrt(step, dst, src, scale, eps):
                    chain.link(g_.tensor_scalar(tmp_r[:, :].rearrange("p (a b) -> p a b", b=1), src, scale, eps, ALU.mult, ALU.add), step)
                    return g_.tensor_tensor(dst, tmp_r[:, :], half[:, 0:QT], ALU.pow)

                def extra(step, s):
                    cross, own, past, ahead = step.cross, step.own, step.past, step.ahead
                    if s in (0, 1) and own is not None:
                        o = "qk"[s]
                        flat = (flat_q, flat_k)[s]
                        step.wait(pool, m["rope_q" if s == 0 else "rope_k"], (own + 1) * 2)
                        sin = rope_sb[:, 1:2, :].broadcast_to([P, DC, S])
                        chain.link(g_.tensor_tensor(turned[:, :, :], turned[:, :, :], sin, ALU.mult), step)
                        g_.tensor_tensor(flat[:, :, :], turned[:, :, :], with_cos[:, :, :], ALU.add).then_inc(m["rope_used"], 1)
                        wait_apart(step, pool, (m["rope_used"], own * 2 + (s + 1)))
                        split(step, flat, parts[o], "oq_parts" if s == 0 else "ok_parts", own + 1,
                              ("x_st" if s == 0 else "c_st", most(own + 2, B) * 96))
                    if s == 3 and ahead is not None:
                        step.wait(pool, m["x_stat"], ahead + 1)
                        wait_apart(step, pool, (m["x_norm"], ahead))
                        rsqrt(step, r_x[:, :], mv_x[:, :, 1:2], 1.0, 1e-5).then_inc(m["x_rstd"], 1)
                    if s == 4 and past is not None:
                        step.wait(pool, m["h_sq"], (past + 1) * QT)
                        wait_apart(step, pool, (m["h_norm"], past))
                        rsqrt(step, r_h[:, :], ss[:, :].rearrange("p (a b) -> p a b", b=1), 1.0 / D, 1e-6).then_inc(m["h_rstd"], 1)
                    if s in (4, 5) and ahead is not None:
                        o = "qk"[s - 4]
                        src, ev, done = ((flat_q, "x_ev", "x_parts"), (flat_k, "c_ev", "c_parts"))[s - 4]
                        wait_apart(step, pool, (m[ev], (ahead + 1) * DC))
                        if own is not None:
                            sent = ("oq_st" if s == 4 else "ok_st", (own + 1) * 96)
                        else:
                            sent = ("x_st" if s == 4 else "c_st", ahead * 96)
                        split(step, src, parts[o], done, ahead + 1, sent)
                    if s == 6 and ahead is not None:
                        if cross is not None:
                            step.wait(pool, m["pv_mm"], step.u_cross * (G * QT) + G * QT)
                        wait_apart(step, pool, (m["ctx_ld"], (ahead + 1) * 16))
                        g_.tensor_scalar(v_of["cross"][:, :, :, 0:DH].rearrange("p t h d -> p (t h) d"),
                                         ctx_in[:, :, :].rearrange("p t (h d) -> p (t h) d", d=DH), 1.0, 0.0, ALU.mult, ALU.add)\
                            .then_inc(m["v_cross"], 1)
                    if s == 7 and past is not None:
                        wait_apart(step, pool, (m["route"], past + 1), (m["h_norm"], past + 1))
                        for k in range(2):
                            for t in range(QT):
                                g_.indirect_dma_start(
                                    out=rows_in, out_offset=bass.IndirectOffsetOnAxis(ap=pos_i[:, k * QT + t:k * QT + t + 1], axis=0),
                                    in_=hn2[:, t, :], in_offset=None).then_inc(m["scat"], 16)
                    if s == 7 and cross is not None:
                        wait_apart(step, pool, (m["x1_stat"], cross + 1), (m["x1_norm"], cross))
                        chain.link(rsqrt(step, r_1[:, 0:QT], mv_1[:, :, 1:2], 1.0, 1e-5), step)
                        var = mv_1[:, :, 1:2].rearrange("p a b -> p (a b)")
                        chain.link(g_.tensor_tensor(tmp_r[:, :], var, r_1[:, 0:QT], ALU.mult), step)
                        chain.link(g_.tensor_tensor(tmp_r[:, :], tmp_r[:, :], r_1[:, 0:QT], ALU.mult), step)
                        rsqrt(step, r_1[:, QT:2 * QT], tmp_r[:, :].rearrange("p (a b) -> p a b", b=1), 1.0, 1e-6).then_inc(m["x1_rstd"], 1)

                def body(step):
                    for s in range(8):
                        extra(step, s)

                run_steps(pool, lambda step: chain.loop_body(step, body, POOL_LINKS))
                pool.wait_ge(m["scat"], B * 2 * QT * 16)

        with ExitStack() as st:
            def s2(name, *shape, dt=F32):
                return sb(name, (P, *shape), dt, st)

            def one(name, *shape, dt=F32):
                return sb(name, (1, *shape), dt, st)

            WG, WD = DC * F, FC * D
            wg_sb, wu_sb, wd_sb = s2("wg_sb", 2 * WG), s2("wu_sb", 2 * WG), s2("wd_sb", 2 * WD)
            rows_sb = [s2("rows0", D), s2("rows1", D)]
            rows_t = s2("rows_t", DC, P)
            silu, hidden, hidden_t = s2("silu", F), s2("hidden", F), s2("hidden_t", FC, P)
            y_sb = s2("y_sb", D)
            pad_i = s2("pad_i", E, dt=I32)
            pad_f = s2("pad_f", E)
            table_sb = one("table_sb", 2, TILES, E)
            full_i, full_f, skip = s2("full_i", E, dt=I32), s2("full_f", E), s2("skip", E)
            cum, ones_e = one("cum", E), one("ones_e", E)
            beyond = s2("beyond", B * 2 * QT, E)
            left, pos_out = s2("left", B * 2 * QT), s2("pos_out", B, 2 * QT, dt=I32)
            passed, skipped = one("passed", TILES, E), one("skipped", TILES, E)
            expert_f, row_f, odd_f = one("expert_f", TILES), one("row_f", TILES), one("odd_f", TILES)
            expert_i, row_i = one("expert_i", TILES, dt=I32), one("row_i", TILES, dt=I32)
            odd_i, wg_off, wd_off = (one(n, TILES, dt=I32) for n in ("odd_i", "wg_off", "wd_off"))
            cum_i = one("cum_i", E, dt=I32)
            idx_now = [s2(f"idx_now{n}", 2 * QT, dt=I32) for n in range(2)]
            got = [s2(f"got{n}", 2 * QT, D) for n in range(2)]
            mix_now = [s2(f"mix_now{n}", 2 * QT) for n in range(2)]
            base_in = [s2(f"base_in{n}", QT, D) for n in range(2)]
            res = [s2(f"res{n}", QT, D) for n in range(2)]

            def bank(name):
                return st.enter_context(nc.psum_tensor(name, [P, 512], F32))

            gate_ps, up_ps = [bank("gate_ps0"), bank("gate_ps1")], [bank("up_ps0"), bank("up_ps1")]
            rows_ps, y_ps = bank("rows_ps"), bank("y_ps")
            hid_ps = [bank("hid_ps0"), bank("hid_ps1")]

            m = {n: sem("t_" + n, st) for n in """tab_ld chain tab pad pad_i w_ld x_tr x_ev gate_mm up_mm silu hid
                hid_tr hid_ev_a hid_ev_v y_mm y_ev y_st idx base0 base1 got0 got1 sum mixes out_st0 out_st1""".split()}
            x_ld = [sem("t_x_ld0", st), sem("t_x_ld1", st)]
            base_ld, got_ld, out_st = ([m[f"{k}{n}"] for n in range(2)] for k in ("base", "got", "out_st"))
            block = st.enter_context(nc.Block())
            PAIRS = TILES // 2

            def pairs(eng, body):
                body(0, True, False)
                with eng.Fori(1, PAIRS - 1) as jj:
                    body(jj, False, False)
                body(PAIRS - 1, False, True)

            def wait_apart(eng, s_, v):
                if not isinstance(v, int):
                    eng.compute_val(v)
                eng.wait_ge(m["tab"], 1)
                wait(eng, s_, v)

            def wait(eng, s_, v):
                if not isinstance(v, int) or v > 0:
                    eng.wait_ge(s_, v)

            @block.sync
            def _(sp):
                sp.dma_start(table_sb[:, :, :, :], c_table).then_inc(m["tab_ld"], 16)
                sp.wait_ge(m["tab"], 1)
                sp.wait_ge(m["pad"], 16 * E)

                def row_of(j):
                    return sp.value_load(row_i[0:1, bass.ds(j, 1)], min_val=0, max_val=ROWS - P)

                def load(j, par):
                    sp.dma_start(rows_sb[par][:, :], rows_in[bass.ds(row_of(j), P), :]).then_inc(x_ld[par], 16)

                def store(j):
                    wait(sp, m["y_ev"], j + 1)
                    sp.dma_start(rows_out[bass.ds(j * P, P), :], y_sb[:, :]).then_inc(m["y_st"], 16)

                def body(jj, first, last):
                    for h_ in range(2):
                        j = jj * 2 + h_
                        if not (last and h_):
                            wait_apart(sp, m["x_tr"], j)
                            load(j + 1, (h_ + 1) % 2)
                        if not (first and h_ == 0):
                            store(j - 1)

                load(0, 0)
                pairs(sp, body)
                store(TILES - 1)
                with sp.Fori(0, B // 2) as bb:
                    for n in range(2):
                        wait(sp, m["sum"], bb * 2 + (n - 1) if n else bb * 2)
                        sp.dma_start(base_in[n][:, :, :], base_d[bb * 2 + n]).then_inc(base_ld[n], 16)
                        sp.wait_ge(m["sum"], bb * 2 + (n + 1))
                        sp.dma_start(out.rearrange("b (t p) d -> b p t d", p=P)[bb * 2 + n], res[n][:, :, :]).then_inc(out_st[n], 16)
                for n in range(2):
                    sp.wait_ge(out_st[n], 16 * (B // 2))

            @block.gpsimd
            def _(pool):
                g_ = nc.gpsimd
                pool.wait_ge(m["pad_i"], 1)
                for e in range(E):
                    g_.indirect_dma_start(out=rows_in, out_offset=bass.IndirectOffsetOnAxis(ap=pad_i[:, e:e + 1], axis=0),
                                          in_=zeros[:, :], in_offset=None).then_inc(m["pad"], 16)

                def load_expert(e, par):
                    wait(pool, m["w_ld"], e * 64)
                    g_.dma_start(wg_sb[:, par * WG:(par + 1) * WG].rearrange("p (c f) -> p c f", c=DC),
                                 wg[e].rearrange("(c p) f -> p c f", p=P)).then_inc(m["w_ld"], 16)
                    g_.dma_start(wu_sb[:, par * WG:(par + 1) * WG].rearrange("p (c f) -> p c f", c=DC),
                                 wu[e].rearrange("(c p) f -> p c f", p=P)).then_inc(m["w_ld"], 16)
                    whole = (F // P) * P
                    g_.dma_start(wd_sb[:, par * WD:par * WD + whole // P * D].rearrange("p (k d) -> p k d", d=D),
                                 wd[e][0:whole, :].rearrange("(k p) d -> p k d", p=P)).then_inc(m["w_ld"], 16)
                    g_.dma_start(wd_sb[0:F - whole, par * WD + whole // P * D:(par + 1) * WD], wd[e][whole:F, :]).then_inc(m["w_ld"], 16)

                load_expert(0, 0)
                load_expert(1, 1)
                pool.wait_ge(m["tab"], 1)
                with pool.Fori(1, E // 2) as ee:
                    for par in range(2):
                        e = ee * 2 + par
                        done = pool.value_load(cum_i[0:1, bass.ds(e - 2, 1)], min_val=0, max_val=TILES)
                        pool.wait_ge(m["y_mm"], done)
                        load_expert(e, par)
                pool.wait_ge(m["y_st"], 16 * TILES)
                with pool.Fori(0, B // 2) as bb:
                    for n in range(2):
                        wait(pool, m["sum"], bb * 2 + (n - 1) if n else bb * 2)
                        g_.tensor_copy(idx_now[n][:, :], pos_out[:, bass.ds(bb * 2 + n, 1), :].rearrange("p a b -> p (a b)")).then_inc(m["idx"], 1)
                        wait_apart(pool, m["idx"], bb * 2 + (n + 1))
                        for k in range(2 * QT):
                            g_.indirect_dma_start(out=got[n][:, k, :], out_offset=None, in_=rows_out,
                                                  in_offset=bass.IndirectOffsetOnAxis(ap=idx_now[n][:, k:k + 1], axis=0)).then_inc(got_ld[n], 16)

            @block.vector
            def _(dve):
                v = nc.vector
                links = [0]

                def link(ins):
                    links[0] += 1
                    ins.then_inc(m["chain"], 1)
                    dve.wait_ge(m["chain"], links[0])

                link(v.tensor_tensor(pad_f[:, :], count[:, :], region_e, ALU.add))
                link(v.tensor_scalar(pad_f[:, :], pad_f[:, :], small_sb[:, 2 * E:2 * E + 1], None, ALU.add))
                v.tensor_copy(pad_i[:, :], pad_f[:, :]).then_inc(m["pad_i"], 1)
                link(v.tensor_scalar(full_i[:, :], count[:, :], float(P - 1), None, ALU.add))
                link(v.tensor_scalar(full_i[:, :], full_i[:, :], 7, None, ALU.logical_shift_right))
                link(v.tensor_copy(full_f[:, :], full_i[:, :]))
                link(v.memset(ones_e[:, :], 1.0))
                link(v.tensor_tensor_scan(cum[:, :], ones_e[:, :], full_f[0:1, :], 0.0, ALU.mult, ALU.add))
                link(v.tensor_copy(cum_i[:, :], cum[:, :]))
                dve.wait_ge(m["tab_ld"], 16)
                wide = lambda a: a.rearrange("p (t e) -> p t e", t=1).broadcast_to([1, TILES, E])
                link(v.tensor_tensor(passed[:, :, :], wide(cum[:, :]), table_sb[:, 0, :, :], ALU.is_le))
                link(v.tensor_reduce(expert_f[:, :], passed[:, :, :], op=ALU.add, axis=AX.X))
                link(v.tensor_scalar(expert_f[:, :], expert_f[:, :], float(E - 1), None, ALU.min))
                link(v.tensor_copy(expert_i[:, :], expert_f[:, :]))
                link(v.tensor_scalar(skip[:, :], full_f[:, :], -float(P), float(CAP), ALU.mult, ALU.add))
                link(v.tensor_tensor(skipped[:, :, :], wide(skip[0:1, :]), passed[:, :, :], ALU.mult))
                link(v.tensor_reduce(row_f[:, :], skipped[:, :, :], op=ALU.add, axis=AX.X))
                link(v.tensor_tensor(row_f[:, :], row_f[:, :], table_sb[:, 1, :, 0:1].rearrange("p t e -> p (t e)"), ALU.add))
                link(v.tensor_copy(row_i[:, :], row_f[:, :]))
                link(v.tensor_scalar(odd_i[:, :], expert_i[:, :], 1, None, ALU.bitwise_and))
                link(v.tensor_copy(odd_f[:, :], odd_i[:, :]))
                link(v.tensor_scalar(wg_off[:, :], odd_f[:, :], float(WG), None, ALU.mult))
                link(v.tensor_scalar(wd_off[:, :], odd_f[:, :], float(WD), None, ALU.mult))
                flat_pos = pos_all[:, :, :].rearrange("p b k -> p (b k)")
                here = flat_pos.rearrange("p (n e) -> p n e", e=1).broadcast_to([P, B * 2 * QT, E - 1])
                each = lambda a: a.rearrange("p (n e) -> p n e", n=1).broadcast_to([P, B * 2 * QT, E - 1])
                link(v.tensor_tensor(beyond[:, :, 0:E - 1], here, each(region_e[:, 1:E]), ALU.is_ge))
                link(v.tensor_tensor(beyond[:, :, 0:E - 1], beyond[:, :, 0:E - 1], each(skip[:, 0:E - 1]), ALU.mult))
                link(v.tensor_reduce(left[:, :], beyond[:, :, 0:E - 1], op=ALU.add, axis=AX.X))
                link(v.tensor_tensor(left[:, :], flat_pos, left[:, :], ALU.subtract))
                v.tensor_copy(pos_out[:, :, :].rearrange("p b k -> p (b k)"), left[:, :]).then_inc(m["tab"], 1)

                def body(jj, first, last):
                    for h_ in range(2):
                        j = jj * 2 + h_
                        if not (first and h_ == 0):
                            copy_y(j - 1)
                        wait(dve, m["hid_tr"], j * 2)
                        for n in range(2):
                            wait(dve, m["silu"], j * 2 + (n + 1))
                            wait(dve, m["up_mm"], j * 2 + (n + 1))
                            v.tensor_tensor(hidden[:, n * FH:(n + 1) * FH], silu[:, n * FH:(n + 1) * FH], up_ps[n][:, 0:FH], ALU.mult)\
                                .then_inc(m["hid"], 1)
                        wait(dve, m["hid_tr"], j * 2 + 2)
                        v.tensor_copy(hidden_t[:, 4, :], hid_ps[1][:, 0:P])
                        v.tensor_copy(hidden_t[0:F % P, 5, :], hid_ps[1][0:F % P, P:2 * P]).then_inc(m["hid_ev_v"], 1)

                def copy_y(j):
                    wait(dve, m["y_mm"], j + 1)
                    wait(dve, m["y_st"], j * 16)
                    v.tensor_copy(y_sb[:, :], y_ps[:, 0:D]).then_inc(m["y_ev"], 1)

                pairs(dve, body)
                copy_y(TILES - 1)
                with dve.Fori(0, B // 2) as bb:
                    for n in range(2):
                        b = bb * 2 + n
                        wait(dve, m["sum"], bb * 2 + n if n else bb * 2)
                        v.tensor_copy(mix_now[n][:, :], mix_all[:, bass.ds(b, 1), :].rearrange("p a b -> p (a b)")).then_inc(m["mixes"], 1)
                        dve.wait_ge(m["mixes"], (bb * 2 + n) * 2 + 1)
                        wait(dve, base_ld[n], bb * 16 + 16)
                        wait(dve, got_ld[n], bb * (16 * 2 * QT) + 16 * 2 * QT)
                        wait(dve, out_st[n], bb * 16)
                        for t in range(QT):
                            r = v.scalar_tensor_tensor(out=base_in[n][:, t, :], in0=got[n][:, t, :], scalar=mix_now[n][:, t:t + 1],
                                                       in1=base_in[n][:, t, :], op0=ALU.mult, op1=ALU.add)
                        r.then_inc(m["mixes"], 1)
                        dve.wait_ge(m["mixes"], (bb * 2 + n) * 2 + 2)
                        for t in range(QT):
                            r = v.scalar_tensor_tensor(out=res[n][:, t, :], in0=got[n][:, QT + t, :], scalar=mix_now[n][:, QT + t:QT + t + 1],
                                                       in1=base_in[n][:, t, :], op0=ALU.mult, op1=ALU.add)
                        r.then_inc(m["sum"], 1)

            @block.scalar
            def _(act):
                def rows(j):
                    wait(act, m["x_tr"], j + 1)
                    for c in range(DC):
                        act.activation(rows_t[:, c, :], rows_ps[:, c * P:(c + 1) * P], ACT.Identity,
                                       scale=g2_sb[:, c:c + 1]).then_inc(m["x_ev"], 1)

                def body(jj, first, last):
                    for h_ in range(2):
                        j = jj * 2 + h_
                        wait(act, m["hid"], j * 2)
                        for n in range(2):
                            wait(act, m["gate_mm"], j * 2 + (n + 1))
                            act.activation(silu[:, n * FH:(n + 1) * FH], gate_ps[n][:, 0:FH], ACT.Silu).then_inc(m["silu"], 1)
                        wait(act, m["hid_tr"], j * 2 + 1)
                        act.activation(hidden_t[:, 0:4, :].rearrange("p k t -> p (k t)"), hid_ps[0][:, :], ACT.Copy).then_inc(m["hid_ev_a"], 1)
                        if not (last and h_):
                            rows(j + 1)

                rows(0)
                pairs(act, body)

            @block.tensor
            def _(pe):
                mm, tr = nc.tensor.matmul, nc.tensor.transpose
                pe.wait_ge(m["tab"], 1)

                def reg(tab, j, most_):
                    return pe.value_load(tab[0:1, bass.ds(j, 1)], min_val=0, max_val=most_)

                def turn_rows(j, par):
                    jj_, h_ = j
                    wait(pe, x_ld[par], (jj_ if isinstance(jj_, int) else jj_) * 16 + 16)
                    for c in range(DC):
                        r = tr(rows_ps[:, c * P:(c + 1) * P], rows_sb[par][:, c * P:(c + 1) * P], ident[:, :])
                    r.then_inc(m["x_tr"], 1)

                def up(j):
                    e = reg(expert_i, j, E - 1)
                    off = reg(wg_off, j, WG)
                    pe.wait_ge(m["w_ld"], e * 64 + 64)
                    wait(pe, m["x_ev"], j * DC + DC)
                    for w, ps, used, done in ((wg_sb, gate_ps, "silu", "gate_mm"), (wu_sb, up_ps, "hid", "up_mm")):
                        for n in range(2):
                            wait(pe, m[used], j * 2 + (n - 1) if n == 0 else j * 2)
                            for c in range(DC):
                                r = mm(ps[n][:, 0:FH], rows_t[:, c, :], w[:, bass.ds(off + (c * F + n * FH), FH)],
                                       start=(c == 0), stop=(c == DC - 1))
                            r.then_inc(m[done], 1)

                def turn_hidden(j):
                    wait(pe, m["hid_ev_a"], j)
                    wait(pe, m["hid_ev_v"], j)
                    for k in range(FC):
                        n = min(P, F - k * P)
                        if k == 0:
                            wait(pe, m["hid"], j * 2 + 1)
                        if k * P + n > FH and (k - 1) * P + P <= FH:
                            wait(pe, m["hid"], j * 2 + 2)
                        r = tr(hid_ps[k // 4][0:n, (k % 4) * P:(k % 4 + 1) * P], hidden[:, k * P:k * P + n], ident[:, :])
                        if k == 3 or k == FC - 1:
                            r.then_inc(m["hid_tr"], 1)

                def down(j):
                    off = reg(wd_off, j, WD)
                    wait(pe, m["hid_ev_a"], j + 1)
                    wait(pe, m["hid_ev_v"], j + 1)
                    wait(pe, m["y_ev"], j)
                    for k in range(FC):
                        n = min(P, F - k * P)
                        r = mm(y_ps[:, 0:D], hidden_t[0:n, k, :], wd_sb[0:n, bass.ds(off + k * D, D)], start=(k == 0), stop=(k == FC - 1))
                    r.then_inc(m["y_mm"], 1)

                def body(jj, first, last):
                    for h_ in range(2):
                        j = jj * 2 + h_
                        up(j)
                        if not (first and h_ == 0):
                            down(j - 1)
                        turn_hidden(j)
                        if not (last and h_):
                            wait(pe, m["x_ev"], j * DC + DC)
                            turn_rows((jj + h_, (h_ + 1) % 2), (h_ + 1) % 2)

                turn_rows((0, 0), 0)
                pairs(pe, body)
                down(TILES - 1)


_INS = ["x", "ctx_1024", "g_xattn", "g_ffn", "L0_ffn_wq", "L0_ffn_wk", "L0_ffn_wv", "L0_ffn_wo", "L0_ffn_w_router",
        "L0_ffn_wg", "L0_ffn_wu", "L0_ffn_wd", "L0_ffn_g1", "L0_ffn_g2"]


def kernel(**inputs):
    import concourse.bacc as bacc
    from concourse.bass_utils import run_bass_kernel_spmd

    nc = bacc.Bacc("TRN2", target_bir_lowering=False, num_devices=1)
    arrays, args = {}, []
    for name in _INS:
        a = np.ascontiguousarray(inputs[name])
        arrays[f"in_{name}"] = a
        args.append(nc.dram_tensor(f"in_{name}", a.shape, mybir.dt.from_np(a.dtype), kind="ExternalInput").ap())
    out = nc.dram_tensor("out_0", (B, S, D), F32, kind="ExternalOutput").ap()
    flamingo_block(nc, *args, out)
    r = run_bass_kernel_spmd(nc, [arrays], core_ids=[0])
    return r.results[0]["out_0"]
```

```python
from contextlib import ExitStack

import numpy as np
import concourse.bass as bass
from concourse import mybir

ALU = mybir.AluOpType
ACT = mybir.ActivationFunctionType
AX = mybir.AxisListType
F32, BF16 = mybir.dt.float32, mybir.dt.bfloat16
I32, U32 = mybir.dt.int32, mybir.dt.uint32

P = 128
B, S, D = 8, 512, 256
H, DH = 16, 16
E, F = 8, 704
QT = S // P
DC = D // P
HG = 4
G = H // HG
KROWS = 6 * DH
NEGROWS = 3
DX = D + 2
T = B * S
NT = T // P
CAP = T + P
TILES = 2 * T // P + E
SPARE = TILES - 2 * T // P
ROWS = E * CAP + SPARE * P
FH = F // 2
FC = (F + P - 1) // P
SCALE = float(DH) ** -0.5
MASKED = -3.0e38
DVE_LINKS, POOL_LINKS = 19, 24
LAST = B - 1
VALUES_AT = 1


class Lin:

    def __init__(self, a, c):
        self.a, self.c = a, c

    def __add__(self, n):
        return Lin(self.a, self.c + n)

    def __sub__(self, n):
        return Lin(self.a, self.c - n)

    def __mul__(self, n):
        return Lin(self.a * n, self.c * n)

    __radd__, __rmul__ = __add__, __mul__


class Step:

    def __init__(self, i, reg=None):
        self.reg = reg
        v = Lin(1, 0) if reg is not None else i
        has = (lambda n: True) if reg is not None else (lambda n: 0 <= i + n <= LAST)
        self.cross = v + 1 if has(1) else None
        self.own = v + 0 if has(0) else None
        self.past = v - 1 if has(-1) else None
        self.ahead = v + 2 if has(2) else None
        if reg is not None:
            self.u_cross, self.u_own, self.u_past = Lin(2, 1), Lin(2, 2), Lin(2, 0)
        else:
            self.u_cross = 0 if i == -1 else 2 * i + 1
            self.u_own = 15 if i == LAST else 2 * i + 2
            self.u_past = 15 if i == LAST + 1 else 2 * i
        self.i = i

    def value(self, v):
        if isinstance(v, Lin):
            return self.reg * v.a + v.c if v.a else v.c
        return v

    def wait(self, eng, sem, v):
        if isinstance(v, Lin) or v > 0:
            eng.wait_ge(sem, self.value(v))

    def named(self, which):
        b, u = {"cross": (self.cross, self.u_cross), "own": (self.own, self.u_own), "past": (self.past, self.u_past)}[which]
        return None if b is None else (which, b, u)

    def max_of(self, s):
        u = self.named("cross" if s < 4 else "own")
        return u and (*u, s % 4)

    def main_of(self, s):
        which, g = [("past", 2), ("past", 3), ("cross", 0), ("cross", 1), ("cross", 2), ("cross", 3), ("own", 0), ("own", 1)][s]
        u = self.named(which)
        return u and (*u, g)

    def tail_of(self, s):
        return self.main_of(s - 1) if s else self._past(1)

    def neg_of(self, s):
        return self.max_of(s - 1) if s else self._past(3)

    def _past(self, g):
        u = self.named("past")
        return u and (*u, g)


def most(v, n):
    return v if isinstance(v, Lin) else min(v, n)


def is_self(which):
    return which != "cross"


def run_steps(eng, body):
    for i in (-2, -1, 0):
        body(Step(i))
    with eng.Fori(1, B - 2) as reg:
        body(Step(None, reg))
    for i in range(B - 2, B + 1):
        body(Step(i))


def reads_before(step, s, kind):
    of = Step.tail_of if kind == "tail" else Step.neg_of
    cur, s = step, s - 1
    while True:
        while s >= 0:
            u = of(cur, s)
            if u:
                return u[2] * G + u[3] + 1
            s -= 1
        if cur.i is None:
            return (Lin(2, 0) * G + 1) if kind == "tail" else (Lin(2, 0) * G + 3)
        if cur.i <= -2:
            return 0
        cur, s = Step(cur.i - 1), 7


def host_constants():
    p = np.arange(P)
    upper = np.where(p[None, :] > p[:, None], MASKED, 0.0)
    squares = np.stack([
        np.eye(P),
        upper,
        upper.T,
        (p[:, None] < p[None, :]) * 1.0,
        np.ones((P, P)),
    ], 1).astype(np.float32)
    inv_freq = 1.0 / 10000.0 ** (np.arange(0, DH, 2, dtype=np.float32) / DH)
    freqs = np.einsum("i,j->ij", np.arange(S, dtype=np.float32), inv_freq)
    emb = np.concatenate([freqs, freqs], -1)
    sign = np.where(np.arange(DH) < DH // 2, -1.0, 1.0).astype(np.float32)
    rope = np.stack([np.tile(np.cos(emb).T, (P // DH, 1)), np.tile((np.sin(emb) * sign).T, (P // DH, 1))], 1)
    small = np.zeros((P, 2 * E + QT), np.float32)
    small[:, :E] = np.arange(E)
    small[:, E:2 * E] = np.arange(E) * CAP
    small[:, 2 * E:] = p[:, None] + P * np.arange(QT)[None, :]
    return squares, rope.astype(np.float32), small


def table_constants():
    j = np.arange(TILES, dtype=np.float32)
    return np.stack([np.repeat(j[:, None], E, 1), np.repeat(j[:, None] * P, E, 1)])[None].astype(np.float32)


def flamingo_block(nc, x, ctx, g_xattn, g_ffn, wq, wk, wv, wo, w_router, wg, wu, wd, g1, g2, out):
    squares, rope, small = host_constants()
    c_squares = nc.inline_tensor(squares, "c_squares").ap()
    c_rope = nc.inline_tensor(rope, "c_rope").ap()
    c_small = nc.inline_tensor(small, "c_small").ap()
    c_table = nc.inline_tensor(table_constants(), "c_table").ap()

    def scratch(name, shape, dt=F32):
        return nc.dram_tensor(name, shape, dt, kind="Internal").ap()

    parts_d = {(a, o): scratch(f"parts_{a}_{o}", (B, 3, DH, H, S), BF16) for a in ("cross", "own") for o in "qk"}
    kept_d = scratch("kept", (B, 2, P, QT, D))
    rows_in = scratch("rows_in", (ROWS, DX))

    x_d = x.rearrange("b (t p) d -> b p t d", p=P)
    ctx_d = ctx.rearrange("b (t p) d -> b p t d", p=P)
    out_d = out.rearrange("b (t p) d -> b p t d", p=P)
    out_rows = out.rearrange("b s d -> (b s) d")

    outer = ExitStack()
    with outer:
        def sb(name, shape, dt=F32, stack=None):
            return (stack or outer).enter_context(nc.sbuf_tensor(name, list(shape), dt))

        def sem(name, stack=None):
            return (stack or outer).enter_context(nc.semaphore(name))

        ident = sb("ident", (P, P))
        small_sb = sb("small_sb", (P, 2 * E + QT))
        iota_e, region_e = small_sb[:, 0:E], small_sb[:, E:2 * E]
        gate = sb("gate", (P, 2))
        g1_sb, g2_sb = sb("g1_sb", (P, DC)), sb("g2_sb", (P, DC))
        count = sb("count", (P, E))
        padding = sb("padding", (P, DX))

        with ExitStack() as st:
            def s1(name, *shape, dt=F32):
                return sb(name, (P, *shape), dt, st)

            squares_sb = s1("squares_sb", 5, P)
            squares_b = s1("squares_b", 5, P, dt=BF16)
            ident_b, mask_qk, mask_kq, before_b, ones_b = (squares_b[:, n, :] for n in range(5))
            rope_sb = s1("rope_sb", 2, S)
            w_sb = {n: s1("sb_" + n, DC, D) for n in ("wq", "wk", "wv", "wo")}
            wr_sb = s1("wr_sb", DC, E)
            gates_in = sb("gates_in", (1, 2), F32, st)
            half = s1("half", 2 * QT)

            q_stack = [s1(f"q_stack{g}", HG, S, dt=BF16) for g in range(G)]
            k_stack = [s1(f"k_stack{g}", HG, S, dt=BF16) for g in range(G)]
            probs = s1("probs", 2, HG, S)
            v_of = {"cross": s1("v_cross", QT, H, 32), "own": s1("v_own", QT, H, 32)}
            x_in, ctx_in, x_again = s1("x_in", QT, D), s1("ctx_in", QT, D), s1("x_again", QT, D)
            xq = s1("xq", QT, D)
            x1, xn, hn1 = s1("x1", QT, D), s1("xn", QT, D), s1("hn1", QT, D)
            att = {"cross": s1("att_cross", QT, D), "own": s1("att_own", QT, D)}
            hn1_t, flat_q, flat_k = s1("hn1_t", DC, S), s1("flat_q", DC, S), s1("flat_k", DC, S)
            turned, with_cos = s1("turned", DC, S), s1("with_cos", DC, S)
            rest = s1("rest", DC, S)
            parts = {"q": s1("parts_q", 3, DC, S, dt=BF16), "k": s1("parts_k", 3, DC, S, dt=BF16)}
            out_t = s1("out_t", S)
            own_t = s1("own_t", DC, S)
            kept = s1("kept_sb", 2, QT, D)
            h, hn2, base = s1("h", QT, D), s1("hn2", QT, DX), s1("base_sb", QT, D)
            hn2_t = s1("hn2_t", DC, S)
            neg = s1("neg", 2, HG, QT)
            neg_rest = s1("neg_rest", 2, HG * QT)
            neg_parts = s1("neg_parts", 2, NEGROWS, HG * QT, dt=BF16)
            neg_rows = sb("neg_rows", (NEGROWS * HG * QT, P), BF16, st)
            recip = s1("recip", HG * QT)
            st_x, mv_x = s1("st_x", QT, 6), s1("mv_x", QT, 2)
            st_1, mv_1 = s1("st_1", QT, 6), s1("mv_1", QT, 2)
            r_x, r_1, r_h = s1("r_x", QT), s1("r_1", 2 * QT), s1("r_h", QT)
            tmp_r = s1("tmp_r", QT)
            sq, ss = s1("sq", D), s1("ss", QT)
            lg, top, idx = s1("lg", QT, E), s1("top", QT, 8), s1("idx", QT, 8, dt=U32)
            idx_f = s1("idx_f", QT, 8)
            hot = s1("hot", 2, QT, E)
            hot_b = s1("hot_b", QT, E, dt=BF16)
            where, picked = s1("where", QT, E), s1("picked", 2, QT, E)
            pos_f, pos_i = s1("pos_f", 2 * QT), s1("pos_i", 2 * QT, dt=I32)
            gap, e_gap, mix, weight = s1("gap", QT), s1("e_gap", QT), s1("mix", 2, QT), s1("weight", 2, QT)
            token = s1("token", QT)

            def bank(name, dt=F32, n=512):
                return st.enter_context(nc.psum_tensor(name, [P, n], dt))

            max_ps = [bank("max_ps0"), bank("max_ps1")]
            key_ps = [bank("key_ps0"), bank("key_ps1")]
            pv_ps, turn_ps = bank("pv_ps"), bank("turn_ps")
            aux = [bank("aux0"), bank("aux1")]
            turn_b = turn_ps[:, :].bitcast(BF16)

            names = """ld_const ld_w ready_c ready_b ready_v gate_mm gate_act
                max_mm max_red neg_split neg_chain neg_tr neg_ev neg_dma
                key_mm exp_done pv_mm out_ev post_tr post_norm post_rc
                x_ld ctx_ld xa_ld kept_ld kept_st base_st x_stat x_rstd x_norm x_tr x_ev c_tr c_ev v_cross
                x1_stat x1_rstd x1_norm dve pool hn1_tr hn1_ev xn_done q_mm q_ev k_mm k_ev v_mm v_ev
                rope_q rope_k rope_used x_parts c_parts oq_parts ok_parts x_st c_st oq_st ok_st
                own_tr own_ev wo_mm h_sum h_sq h_rstd h_norm h_base hn2_tr hn2_ev lg_mm gap_r gap_exp hot_r rank_mm
                rank_r route scat route_r""".split()
            m = {n: sem("s_" + n, st) for n in names}
            s_stack = [sem(f"s_stack{g}", st) for g in range(G)]

            class Chain:

                def __init__(self, eng, s):
                    self.eng, self.s, self.n, self.per, self.start = eng, s, 0, 0, 0

                def link(self, ins, step=None):
                    ins.then_inc(self.s, 1)
                    self.n += 1
                    if step is None or step.reg is None:
                        self.eng.wait_ge(self.s, self.n)
                    else:
                        wait_apart(step, self.eng, (self.s, Lin(self.per, self.n - self.per)))

                def loop_body(self, step, body, per):
                    if step.reg is None:
                        return body(step)
                    before, self.per = self.n, per
                    body(step)
                    assert self.n - before == per, (self.n - before, per)
                    self.n = before + per * (B - 3)

            block = st.enter_context(nc.Block())

            def wait_apart(step, eng, *waits):
                values = [(s_, step.value(v)) for s_, v in waits]
                for s_, v in values:
                    if not isinstance(v, int):
                        eng.compute_val(v)
                eng.wait_ge(m["ready_c"], 1)
                for s_, v in values:
                    if not isinstance(v, int) or v > 0:
                        eng.wait_ge(s_, v)

            @block.sync
            def _(sp):
                sp.dma_start(squares_sb[:, :, :], c_squares).then_inc(m["ld_const"], 16)
                sp.dma_start(ident[:, :], c_squares[:, 0, :]).then_inc(m["ld_const"], 16)
                sp.dma_start(rope_sb[:, :, :], c_rope).then_inc(m["ld_const"], 16)
                sp.dma_start(small_sb[:, :], c_small).then_inc(m["ld_const"], 16)
                sp.dma_start(gates_in[:, 0:1], g_xattn.rearrange("(a n) -> a n", a=1)).then_inc(m["ld_const"], 16)
                sp.dma_start(gates_in[:, 1:2], g_ffn.rearrange("(a n) -> a n", a=1)).then_inc(m["ld_const"], 16)
                sp.dma_start(g1_sb[:, :], g1.rearrange("(c p) -> p c", p=P), allow_slow_non_contiguous=True).then_inc(m["ld_const"], 16)
                sp.dma_start(g2_sb[:, :], g2.rearrange("(c p) -> p c", p=P), allow_slow_non_contiguous=True).then_inc(m["ld_const"], 16)

                def load_x(step):
                    if step.ahead is None:
                        return
                    b = step.ahead
                    step.wait(sp, m["x_norm"], b)
                    sp.dma_start(x_in[:, :, :], x_d[step.value(b)]).then_inc(m["x_ld"], 16)
                    step.wait(sp, m["c_tr"], b)
                    step.wait(sp, m["v_cross"], b)
                    sp.dma_start(ctx_in[:, :, :], ctx_d[step.value(b)]).then_inc(m["ctx_ld"], 16)

                def load_stack(step, which, b, u, g):
                    wait_apart(step, sp, (m["key_mm"], (u - 1) * (16 * G) + (16 * g + 16)))
                    kind = "own" if is_self(which) else "cross"
                    q_d, k_d = (parts_d[kind, o][step.value(b)] for o in "qk")
                    hs = slice(g * HG, (g + 1) * HG)
                    if g == 0:
                        step.wait(sp, m["oq_st" if kind == "own" else "x_st"], (b + 1) * 96)
                        step.wait(sp, m["ok_st" if kind == "own" else "c_st"], (b + 1) * 96)
                    for r0, n in ((0, 3), (3, 2), (5, 1)):
                        sp.dma_start(q_stack[g][r0 * DH:(r0 + n) * DH, :, :],
                                     q_d[0:n, :, hs, :].rearrange("p d h t -> (p d) h t")).then_inc(s_stack[g], 16)
                    for r, part in enumerate((0, 0, 0, 1, 1, 2)):
                        sp.dma_start(k_stack[g][r * DH:(r + 1) * DH, :, :], k_d[part, :, hs, :]).then_inc(s_stack[g], 16)

                def store_parts(step, kind, o, b, ready, done):
                    step.wait(sp, m[ready], b + 1)
                    for part in range(3):
                        for c in range(DC):
                            dst = parts_d[kind, o][step.value(b)][part, :, c * 8:(c + 1) * 8, :]
                            sp.dma_start(dst.rearrange("d h t -> h d t"), parts[o][:, part, c, :]).then_inc(m[done], 16)

                def body(step):
                    cross, own, past, ahead = step.cross, step.own, step.past, step.ahead
                    if cross is not None:
                        load_stack(step, "cross", cross, step.u_cross, 1)
                    if own is not None:
                        step.wait(sp, m["xn_done"], own + 1)
                        sp.dma_start(kept_d[step.value(own), 0], x1[:, :, :]).then_inc(m["kept_st"], 16)
                        sp.dma_start(kept_d[step.value(own), 1], xn[:, :, :]).then_inc(m["kept_st"], 16)
                    load_x(step)
                    if cross is not None:
                        load_stack(step, "cross", cross, step.u_cross, 2)
                    if past is not None:
                        wait_apart(step, sp, (m["kept_st"], (past + 1) * 32), (m["h_base"], past))
                        for n in range(2):
                            sp.dma_start(kept[:, n, :, :], kept_d[step.value(past), n]).then_inc(m["kept_ld"], 16)
                    if cross is not None:
                        load_stack(step, "cross", cross, step.u_cross, 3)
                        step.wait(sp, m["x1_stat"], cross)
                        sp.dma_start(x_again[:, :, :], x_d[step.value(cross)]).then_inc(m["xa_ld"], 16)
                    if own is not None:
                        store_parts(step, "own", "q", own, "oq_parts", "oq_st")
                        store_parts(step, "own", "k", own, "ok_parts", "ok_st")
                        for g in range(G):
                            load_stack(step, "own", own, step.u_own, g)
                    if ahead is not None:
                        store_parts(step, "cross", "q", ahead, "x_parts", "x_st")
                        store_parts(step, "cross", "k", ahead, "c_parts", "c_st")
                        u_next = 0 if step.i == -2 else step.u_own + 1
                        load_stack(step, "cross", ahead, u_next, 0)
                    if past is not None:
                        step.wait(sp, m["h_base"], past + 1)
                        sp.dma_start(out_d[step.value(past)], base[:, :, :]).then_inc(m["base_st"], 16)

                first = Step(-2)
                load_x(first)
                for name, w in (("wq", wq), ("wk", wk), ("wv", wv), ("wo", wo)):
                    sp.dma_start(w_sb[name][:, :, :], w.rearrange("(c p) n -> p c n", p=P)).then_inc(m["ld_w"], 16)
                sp.dma_start(wr_sb[:, :, :], w_router.rearrange("(c p) n -> p c n", p=P)).then_inc(m["ld_w"], 16)
                sp.wait_ge(m["ready_v"], 1)
                for n in range(SPARE):
                    sp.dma_start(rows_in[E * CAP + n * P:E * CAP + (n + 1) * P, :], padding[:, :]).then_inc(m["ld_w"], 16)
                def sp_body(step):
                    if step.i == -2:
                        store_parts(step, "cross", "q", 0, "x_parts", "x_st")
                        store_parts(step, "cross", "k", 0, "c_parts", "c_st")
                        load_stack(step, "cross", 0, 0, 0)
                    else:
                        body(step)

                run_steps(sp, sp_body)
                sp.wait_ge(m["base_st"], 16 * B)
                sp.wait_ge(m["kept_st"], 32 * B)
                sp.wait_ge(m["ld_w"], 16 * (5 + SPARE))

            @block.tensor
            def _(pe):
                mm = nc.tensor.matmul
                tr = nc.tensor.transpose
                pe.wait_ge(m["ready_c"], 1)
                pe.wait_ge(m["ready_b"], 1)
                pe.wait_ge(m["ready_v"], 2)
                pe.wait_ge(m["ld_const"], 16 * 8)
                pe.wait_ge(m["ld_w"], 16 * (5 + SPARE))
                mm(aux[0][:, 0:2], squares_sb[0:1, 4, :], gates_in[0:1, 0:2], start=True, stop=True).then_inc(m["gate_mm"], 1)
                pe.wait_ge(m["gate_act"], 1)

                def max_unit(step, unit, qt, hd):
                    which, b, u, g = unit
                    n = u * G + g
                    j = HG * qt + hd
                    if j == 0:
                        step.wait(pe, s_stack[g], (u + 1) * (9 * 16))
                    step.wait(pe, m["max_red"], n * 16 + (j - 1))
                    own = is_self(which)
                    keys = (qt + 1) * P if own else S
                    ps = max_ps[j % 2]
                    r = mm(ps[:, 0:keys], q_stack[g][0:KROWS, hd, qt * P:(qt + 1) * P], k_stack[g][0:KROWS, hd, 0:keys],
                           start=True, stop=not own)
                    if own:
                        r = mm(ps[:, qt * P:keys], ident_b, mask_qk, start=False, stop=True)
                    r.then_inc(m["max_mm"], 1)

                def key_unit(step, unit, kt, hd):
                    which, b, u, g = unit
                    n = u * G + g
                    j = HG * kt + hd
                    if j == 0:
                        step.wait(pe, m["neg_dma"], (n + 1) * 16)
                    step.wait(pe, m["exp_done"], n * 16 + (j - 1))
                    own = is_self(which)
                    q0 = kt * P if own else 0
                    ps = key_ps[j % 2]
                    r = mm(ps[:, q0:S], k_stack[g][0:KROWS + NEGROWS, hd, kt * P:(kt + 1) * P],
                           q_stack[g][0:KROWS + NEGROWS, hd, q0:S], start=True, stop=not own)
                    if own:
                        r = mm(ps[:, q0:q0 + P], ident_b, mask_kq, start=False, stop=True)
                    r.then_inc(m["key_mm"], 1)

                def value_unit(step, unit, kt, hd):
                    which, b, u, g = unit
                    n = u * G + g
                    step.wait(pe, m["exp_done"], n * 16 + (HG * kt + hd + 1))
                    own = is_self(which)
                    if kt == 0 and hd == 0:
                        step.wait(pe, m["out_ev"], n)
                        if g == 0:
                            step.wait(pe, m["v_ev" if own else "v_cross"], (b + 1) * (DC if own else 1))
                    q0 = kt * P if own else 0
                    mm(pv_ps[32 * hd:32 * hd + 32, q0:S], v_of["own" if own else "cross"][:, kt, g * HG + hd, :],
                       probs[:, kt % 2, hd, q0:S], start=(kt == 0), stop=(kt == QT - 1), skip_group_check=True)\
                        .then_inc(m["pv_mm"], 1)

                def neg_turn(step, s):
                    unit = step.neg_of(s)
                    if not unit:
                        return
                    n = unit[2] * G + unit[3]
                    wait_apart(step, pe, (m["neg_split"], n + 1), (m["neg_ev"], n), (m["post_norm"], reads_before(step, s + 1, "tail")))
                    tr(turn_b[0:NEGROWS * HG * QT, 0:P], neg_parts[:, unit[3] % 2, :, :].rearrange("p a b -> p (a b)"), ident_b)\
                        .then_inc(m["neg_tr"], 1)

                def post_turn(step, s):
                    unit = step.tail_of(s)
                    if not unit:
                        return
                    n = unit[2] * G + unit[3]
                    step.wait(pe, m["out_ev"], n + 1)
                    step.wait(pe, m["post_norm"], n)
                    step.wait(pe, m["neg_ev"], reads_before(step, s, "neg"))
                    for qt in range(QT):
                        r = tr(turn_ps[:, qt * P:(qt + 1) * P], out_t[:, qt * P:(qt + 1) * P], ident[:, :])
                    r.then_inc(m["post_tr"], 1)

                def turn(c, src, done):
                    for t in range(QT):
                        r = tr(aux[c][:, t * P:(t + 1) * P], src[:, t, c * P:(c + 1) * P], ident[:, :])
                    r.then_inc(m[done], 1)

                def project(k, w, src, done):
                    o, c = k // DC, k % DC
                    r = mm(aux[o][:, :], w[:, c, o * P:(o + 1) * P], src[:, c, :], start=(c == 0), stop=(c == DC - 1))
                    if c == DC - 1:
                        r.then_inc(m[done], 1)

                def project_rows(t, src, w, done):
                    for c in range(DC):
                        r = mm(aux[t // 2][:, (t % 2) * D:(t % 2 + 1) * D], src[:, c, t * P:(t + 1) * P], w[:, c, :],
                               start=(c == 0), stop=(c == DC - 1))
                    if t % 2:
                        r.then_inc(m[done], 1)

                def extra(step, s, kt, hd):
                    cross, own, past, ahead = step.cross, step.own, step.past, step.ahead
                    at = (s, kt, hd)
                    if own is not None:
                        if at == (0, 1, 0):
                            step.wait(pe, m["x1_norm"], own + 1)
                            step.wait(pe, m["rank_r"], own - 1)
                            step.wait(pe, m["c_ev"], most(own + 2, B) * DC)
                            step.wait(pe, m["hn2_ev"], (own - 1) * DC)
                            turn(0, hn1, "hn1_tr")
                        if at == (0, 1, 2):
                            turn(1, hn1, "hn1_tr")
                        for k, where_ in enumerate(((0, 2, 2), (0, 3, 0), (0, 3, 2), (1, 0, 0))):
                            if at == where_:
                                if k == 0:
                                    step.wait(pe, m["hn1_ev"], (own + 1) * DC)
                                project(k, w_sb["wq"], hn1_t, "q_mm")
                        for k, where_ in enumerate(((1, 1, 0), (1, 1, 2), (1, 2, 0), (1, 2, 2))):
                            if at == where_:
                                if k % DC == 0:
                                    step.wait(pe, m["q_ev"], own * DC + (k // DC + 1))
                                project(k, w_sb["wk"], hn1_t, "k_mm")
                        for k, where_ in enumerate(((2, 0, 0), (2, 0, 2), (2, 1, 0), (2, 1, 2))):
                            if at == where_:
                                if k % 2 == 0:
                                    step.wait(pe, m["k_ev"], own * DC + (k // 2 + 1))
                                project_rows(k, hn1_t, w_sb["wv"], "v_mm")
                    if past is not None:
                        if at == (3, 0, 2):
                            step.wait(pe, m["post_norm"], step.u_past * G + 4)
                            step.wait(pe, m["v_ev"], most(past + 2, B) * DC)
                            step.wait(pe, m["rank_r"], past)
                            turn(0, att["own"], "own_tr")
                        if at == (3, 1, 0):
                            turn(1, att["own"], "own_tr")
                        for k, where_ in enumerate(((3, 2, 0), (3, 2, 2), (3, 3, 0), (3, 3, 2))):
                            if at == where_:
                                if k == 0:
                                    step.wait(pe, m["own_ev"], (past + 1) * DC)
                                project_rows(k, own_t, w_sb["wo"], "wo_mm")
                    if ahead is not None:
                        if at == (4, 2, 0):
                            step.wait(pe, m["x_norm"], ahead + 1)
                            if past is not None:
                                step.wait(pe, m["h_sum"], (past + 1) * DC)
                            elif own is not None:
                                step.wait(pe, m["v_ev"], (own + 1) * DC)
                            else:
                                step.wait(pe, m["c_ev"], ahead * DC)
                            turn(0, xq, "x_tr")
                        if at == (4, 2, 2):
                            turn(1, xq, "x_tr")
                        if at == (5, 0, 0):
                            step.wait(pe, m["x_ev"], (ahead + 1) * DC)
                            step.wait(pe, m["ctx_ld"], (ahead + 1) * 16)
                            turn(0, ctx_in, "c_tr")
                        if at == (5, 0, 2):
                            turn(1, ctx_in, "c_tr")
                    if past is not None:
                        if at == (5, 2, 0):
                            step.wait(pe, m["h_norm"], past + 1)
                            step.wait(pe, m["h_sum"], (past + 1) * DC)
                            if ahead is not None:
                                step.wait(pe, m["c_ev"], (ahead + 1) * DC)
                            turn(0, hn2, "hn2_tr")
                        if at == (5, 2, 2):
                            turn(1, hn2, "hn2_tr")
                        if at[:2] == (6, 0):
                            if hd == 0:
                                step.wait(pe, m["hn2_ev"], (past + 1) * DC)
                            for c in range(DC):
                                r = mm(aux[0][:, hd * E:(hd + 1) * E], hn2_t[:, c, hd * P:(hd + 1) * P], wr_sb[:, c, :],
                                       start=(c == 0), stop=(c == DC - 1))
                            if hd == QT - 1:
                                r.then_inc(m["lg_mm"], 1)
                        if at == (6, 2, 2):
                            step.wait(pe, m["hot_r"], past + 1)
                            for t in range(QT + 1):
                                for s_ in range(min(t + 1, QT)):
                                    r = mm(aux[1][:, t * E:(t + 1) * E], before_b if s_ == t else ones_b, hot_b[:, s_, :],
                                           start=(s_ == 0), stop=(s_ == min(t, QT - 1)))
                            r.then_inc(m["rank_mm"], 1)

                def body(step):
                    for s in range(8):
                        mx, mn, tail = step.max_of(s), step.main_of(s), step.tail_of(s)
                        for kt in range(QT):
                            for hd in range(HG):
                                extra(step, s, kt, hd)
                                if mx:
                                    max_unit(step, mx, kt, hd)
                                if mn:
                                    key_unit(step, mn, kt, hd)
                                if hd == VALUES_AT:
                                    for each in range(HG):
                                        if kt == 0 and tail:
                                            value_unit(step, tail, QT - 1, each)
                                        if kt and mn:
                                            value_unit(step, mn, kt - 1, each)
                            if kt == 1:
                                post_turn(step, s)
                            if kt == 2:
                                neg_turn(step, s)

                run_steps(pe, body)

            @block.scalar
            def _(act):
                act.wait_ge(m["gate_mm"], 1)
                act.activation(gate[:, :], aux[0][:, 0:2], ACT.Tanh).then_inc(m["gate_act"], 1)
                act.wait_ge(m["ld_const"], 16 * 8)

                def exp_unit(step, unit, kt, hd):
                    which, b, u, g = unit
                    n = u * G + g
                    j = HG * kt + hd
                    step.wait(act, m["key_mm"], n * 16 + (j + 1))
                    step.wait(act, m["pv_mm"], n * 16 + (HG * (kt - 2) + hd + 1))
                    q0 = kt * P if is_self(which) else 0
                    act.activation(probs[:, kt % 2, hd, q0:S], key_ps[j % 2][:, q0:S], ACT.Exp).then_inc(m["exp_done"], 1)

                def evacuate(step, c, b, mm_done, ev_done, dst, scale=1.0):
                    step.wait(act, m[mm_done], b * DC + (c + 1))
                    plain = isinstance(scale, float)
                    act.activation(dst[:, c, :], aux[c][:, :], ACT.Copy if plain else ACT.Identity, scale=scale if plain else scale[:, c:c + 1])\
                        .then_inc(m[ev_done], 1)

                def extra(step, s, kt, hd):
                    cross, own, past, ahead = step.cross, step.own, step.past, step.ahead
                    at = (s, kt, hd)
                    if own is not None:
                        if at[:2] == (0, 0) and hd < 2:
                            if hd == 0:
                                step.wait(act, m["xn_done"], own + 1)
                                step.wait(act, m["hn1_tr"], own * DC)
                            for t in (2 * hd, 2 * hd + 1):
                                r = act.activation(hn1[:, t, :], xn[:, t, :], ACT.Identity, scale=r_1[:, QT + t:QT + t + 1])
                            if hd == 1:
                                r.then_inc(m["x1_norm"], 1)
                        for c, where_ in enumerate(((0, 1, 2), (0, 2, 0))):
                            if at == where_:
                                if c == 0:
                                    step.wait(act, m["v_mm"], own * DC)
                                evacuate(step, c, own, "hn1_tr", "hn1_ev", hn1_t, g1_sb)
                        for c, where_ in enumerate(((0, 3, 2), (1, 0, 2))):
                            if at == where_:
                                if c == 0:
                                    step.wait(act, m["x_parts"], most(own + 2, B))
                                evacuate(step, c, own, "q_mm", "q_ev", flat_q, SCALE)
                        for c, where_ in enumerate(((1, 2, 0), (1, 3, 0))):
                            if at == where_:
                                if c == 0:
                                    step.wait(act, m["c_parts"], most(own + 2, B))
                                evacuate(step, c, own, "k_mm", "k_ev", flat_k)
                        for c, where_ in enumerate(((2, 1, 0), (2, 2, 0))):
                            if at == where_:
                                if c == 0 and past is not None:
                                    step.wait(act, m["pv_mm"], (step.u_past + 1) * (G * 16))
                                step.wait(act, m["v_mm"], own * DC + (c + 1))
                                act.activation(v_of["own"][:, 2 * c:2 * c + 2, :, 0:DH],
                                               aux[c][:, :].rearrange("p (t h d) -> p t h d", t=2, d=DH), ACT.Copy).then_inc(m["v_ev"], 1)
                    if past is not None:
                        for c, where_ in enumerate(((3, 1, 0), (3, 1, 2))):
                            if at == where_:
                                if c == 0:
                                    step.wait(act, m["wo_mm"], past * DC)
                                evacuate(step, c, past, "own_tr", "own_ev", own_t)
                        if at[:2] == (4, 1):
                            if hd == 0:
                                step.wait(act, m["h_sum"], (past + 1) * DC)
                                step.wait(act, m["h_rstd"], past)
                            step.wait(act, m["h_sq"], past * QT + hd)
                            act.activation(sq[:, :], h[:, hd, :], ACT.Square, accum_out=ss[:, hd:hd + 1]).then_inc(m["h_sq"], 1)
                    if ahead is not None:
                        for c, where_ in enumerate(((4, 2, 2), (4, 3, 0))):
                            if at == where_:
                                if c == 0:
                                    step.wait(act, m["x_parts"], ahead)
                                    if own is not None:
                                        step.wait(act, m["oq_parts"], own + 1)
                                evacuate(step, c, ahead, "x_tr", "x_ev", flat_q, SCALE)
                        for c, where_ in enumerate(((5, 0, 2), (5, 1, 0))):
                            if at == where_:
                                if c == 0:
                                    step.wait(act, m["c_parts"], ahead)
                                    if own is not None:
                                        step.wait(act, m["ok_parts"], own + 1)
                                evacuate(step, c, ahead, "c_tr", "c_ev", flat_k)
                    if past is not None:
                        for c, where_ in enumerate(((5, 2, 2), (5, 3, 0))):
                            if at == where_:
                                if c == 0:
                                    step.wait(act, m["lg_mm"], past)
                                evacuate(step, c, past, "hn2_tr", "hn2_ev", hn2_t, g2_sb)
                        if at == (6, 2, 0):
                            step.wait(act, m["gap_r"], past + 1)
                            act.activation(e_gap[:, :], gap[:, :], ACT.Exp).then_inc(m["gap_exp"], 1)

                def body(step):
                    for s in range(8):
                        mn, tail, ng = step.main_of(s), step.tail_of(s), step.neg_of(s)
                        for kt in range(QT):
                            if kt == 1 and tail:
                                n = tail[2] * G + tail[3]
                                step.wait(act, m["pv_mm"], (n + 1) * 16)
                                step.wait(act, m["post_tr"], n)
                                act.activation(out_t[:, :], pv_ps[:, :], ACT.Copy).then_inc(m["out_ev"], 1)
                            if kt == 3 and ng:
                                n = ng[2] * G + ng[3]
                                step.wait(act, m["neg_tr"], n + 1)
                                step.wait(act, m["neg_dma"], n * 16)
                                act.activation(neg_rows[:, :], turn_b[0:NEGROWS * HG * QT, 0:P], ACT.Copy).then_inc(m["neg_ev"], 1)
                                step.wait(act, m["neg_ev"], n + 1)
                                act.dma_start(q_stack[ng[3]][KROWS:KROWS + NEGROWS, :, :], neg_rows[:, :]).then_inc(m["neg_dma"], 16)
                            for hd in range(HG):
                                extra(step, s, kt, hd)
                                if mn:
                                    exp_unit(step, mn, kt, hd)

                run_steps(act, body)

            @block.vector
            def _(dve):
                v = nc.vector
                chain = Chain(dve, m["dve"])
                dve.wait_ge(m["ld_const"], 16 * 8)
                v.tensor_copy(squares_b[:, :, :], squares_sb[:, :, :]).then_inc(m["ready_c"], 1)
                v.memset(count[:, :], 0.0)
                v.memset(half[:, :], -0.5)
                v.tensor_copy(token[:, :], small_sb[:, 2 * E:2 * E + QT])
                v.memset(padding[:, D:D + 1], float(T))
                v.memset(padding[:, D + 1:DX], 0.0)
                v.memset(padding[:, 0:D], 0.0).then_inc(m["ready_v"], 1)
                for g in range(G):
                    chain.link(v.memset(k_stack[g][KROWS:KROWS + NEGROWS, :, :], 1.0))
                for kind in ("cross", "own"):
                    chain.link(v.memset(v_of[kind][:, :, :, DH + 1:32], 0.0))
                    chain.link(v.memset(v_of[kind][:, :, :, DH:DH + 1], 1.0))
                v.memset(gap[:, :], 0.0).then_inc(m["ready_b"], 1)
                v.memset(e_gap[:, :], 0.0).then_inc(m["ready_v"], 1)

                def reduce_unit(step, unit, qt, hd):
                    which, b, u, g = unit
                    n = u * G + g
                    j = HG * qt + hd
                    step.wait(dve, m["max_mm"], n * 16 + (j + 1))
                    if j == 0:
                        step.wait(dve, m["neg_split"], n - 1)
                    keys = (qt + 1) * P if is_self(which) else S
                    v.tensor_reduce(neg[:, g % 2, hd, qt:qt + 1], max_ps[j % 2][:, 0:keys], op=ALU.max, axis=AX.X,
                                    negate=True).then_inc(m["max_red"], 1)

                def split_neg(step, unit, k):
                    n, g2 = unit[2] * G + unit[3], unit[3] % 2
                    src = neg[:, g2, :, :].rearrange("p a b -> p (a b)")
                    rest_, part = neg_rest[:, g2, :], lambda a: neg_parts[:, g2, a, :]
                    if k == 0:
                        step.wait(dve, m["max_red"], (n + 1) * 16)
                        step.wait(dve, m["neg_tr"], n - 1)
                        v.tensor_copy(part(0), src).then_inc(m["neg_chain"], 1)
                        return
                    step.wait(dve, m["neg_chain"], n * 3 + k)
                    if k == 1:
                        v.tensor_tensor(rest_, src, part(0), ALU.subtract).then_inc(m["neg_chain"], 1)
                    if k == 2:
                        v.tensor_copy(part(1), rest_).then_inc(m["neg_chain"], 1)
                    if k == 3:
                        v.tensor_tensor(part(2), rest_, part(1), ALU.subtract).then_inc(m["neg_split"], 1)

                def post_norm(step, unit):
                    which, b, u, g = unit
                    n = u * G + g
                    kind = "own" if is_self(which) else "cross"
                    step.wait(dve, m["post_tr"], n + 1)
                    step.wait(dve, m["post_norm"], n)
                    if g == 0 and kind == "own":
                        step.wait(dve, m["own_tr"], b * DC)
                    if g == 0 and kind == "cross":
                        step.wait(dve, m["x1_stat"], b)
                    o = turn_ps[:, :].rearrange("p (t e) -> p t e", e=32)
                    v.reciprocal(recip[:, :].rearrange("p (t e) -> p t e", e=1), o[:, :, DH:DH + 1]).then_inc(m["post_rc"], 1)
                    step.wait(dve, m["post_rc"], n + 1)
                    src = turn_ps[:, :].rearrange("p (t h e) -> p t h e", h=HG, e=32)[:, :, :, 0:DH]
                    dst = att[kind][:, :, g * HG * DH:(g + 1) * HG * DH].rearrange("p t (h d) -> p t h d", d=DH)
                    rc = recip[:, :].rearrange("p (t h e) -> p t h e", h=HG, e=1).broadcast_to([P, QT, HG, DH])
                    v.tensor_tensor(dst, src, rc, ALU.mult).then_inc(m["post_norm"], 1)

                def extra(step, s, kt, hd):
                    cross, own, past, ahead = step.cross, step.own, step.past, step.ahead
                    at = (s, kt, hd)
                    if own is not None:
                        for flat, ev, done, c, where_ in ((flat_q, "q_ev", "rope_q", 0, (1, 0, 0)), (flat_q, "q_ev", "rope_q", 1, (1, 0, 3)),
                                                          (flat_k, "k_ev", "rope_k", 0, (2, 0, 0)), (flat_k, "k_ev", "rope_k", 1, (2, 0, 2))):
                            if at == where_:
                                step.wait(dve, m[ev], own * DC + (c + 1))
                                if c == 0:
                                    step.wait(dve, m["rope_used"], own * 2 + (0 if done == "rope_q" else 1))
                                v.tensor_tensor(with_cos[:, c, :], flat[:, c, :], rope_sb[:, 0, :], ALU.mult).then_inc(m[done], 1)
                                swap = [(p + DH // 2) % DH + (p // DH) * DH for p in range(32)]
                                v.stream_shuffle(out=turned[:, c, :], in_=flat[:, c, :], mask=swap).then_inc(m[done], 1)
                    if ahead is not None:
                        if at[:2] == (3, 2):
                            if hd == 0:
                                step.wait(dve, m["x_ld"], (ahead + 1) * 16)
                                step.wait(dve, m["x_rstd"], ahead)
                            r = v.bn_stats(st_x[:, hd, :], x_in[:, hd, :])
                            if hd == QT - 1:
                                chain.link(r, step)
                        if at == (3, 3, 0):
                            for t in range(QT):
                                r = v.bn_aggr(mv_x[:, t, :], st_x[:, t, :])
                            r.then_inc(m["x_stat"], 1)
                        if at[:2] == (4, 1):
                            if hd == 0:
                                step.wait(dve, m["x_rstd"], ahead + 1)
                                step.wait(dve, m["x_tr"], ahead * DC)
                                step.wait(dve, m["x_stat"], ahead + 1)
                            r = v.tensor_scalar(xq[:, hd, :], x_in[:, hd, :], mv_x[:, hd, 0:1], r_x[:, hd:hd + 1], ALU.subtract, ALU.mult)
                            if hd == QT - 1:
                                r.then_inc(m["x_norm"], 1)
                    if past is not None:
                        for c, where_ in enumerate(((4, 0, 0), (4, 0, 2))):
                            if at == where_:
                                if c == 0:
                                    step.wait(dve, m["kept_ld"], (past + 1) * 32)
                                    step.wait(dve, m["h_norm"], past)
                                    step.wait(dve, m["h_sq"], past * QT)
                                    step.wait(dve, m["h_base"], past)
                                step.wait(dve, m["wo_mm"], past * DC + (c + 1))
                                v.tensor_tensor(h[:, 2 * c:2 * c + 2, :], kept[:, 1, 2 * c:2 * c + 2, :],
                                                aux[c][:, :].rearrange("p (t d) -> p t d", t=2), ALU.add).then_inc(m["h_sum"], 1)
                        if at[:2] == (5, 0):
                            if hd == 0:
                                step.wait(dve, m["h_rstd"], past + 1)
                                step.wait(dve, m["hn2_tr"], past * DC)
                                step.wait(dve, m["scat"], past * (2 * QT * 16))
                            r = v.tensor_scalar(hn2[:, hd, 0:D], h[:, hd, :], r_h[:, hd:hd + 1], None, ALU.mult)
                            if hd == QT - 1:
                                r.then_inc(m["h_norm"], 1)
                    if at == (6, 1, 0) and past is not None:
                        step.wait(dve, m["lg_mm"], past + 1)
                        chain.link(v.tensor_copy(lg[:, :, :], aux[0][:, 0:QT * E].rearrange("p (t e) -> p t e", e=E)), step)
                        for t in range(QT):
                            r = v.max(top[:, t, :], lg[:, t, :])
                        chain.link(r, step)
                        step.wait(dve, m["gap_exp"], past)
                        v.tensor_tensor(gap[:, :].rearrange("p (t e) -> p t e", e=1), top[:, :, 1:2], top[:, :, 0:1], ALU.subtract)\
                            .then_inc(m["gap_r"], 1)
                    if at == (6, 1, 2) and past is not None:
                        for t in range(QT):
                            r = v.max_index(idx[:, t, :], top[:, t, :], lg[:, t, :])
                        chain.link(r, step)
                        chain.link(v.tensor_copy(idx_f[:, :, :], idx[:, :, :]), step)
                    if at == (6, 2, 0) and past is not None:
                        experts = iota_e.rearrange("p (t e) -> p t e", t=1).broadcast_to([P, QT, E])
                        for k in range(2):
                            r = v.tensor_tensor(hot[:, k, :, :], idx_f[:, :, k:k + 1].broadcast_to([P, QT, E]), experts, ALU.is_equal)
                        chain.link(r, step)
                        step.wait(dve, m["rank_mm"], past)
                        v.tensor_tensor(hot_b[:, :, :], hot[:, 0, :, :], hot[:, 1, :, :], ALU.add).then_inc(m["hot_r"], 1)
                    if at == (6, 3, 0) and past is not None:
                        step.wait(dve, m["rank_mm"], past + 1)
                        step.wait(dve, m["hot_r"], past + 1)
                        ranks = aux[1][:, 0:QT * E].rearrange("p (t e) -> p t e", e=E)
                        so_far = count[:, :].rearrange("p (t e) -> p t e", t=1).broadcast_to([P, QT, E])
                        regions = region_e.rearrange("p (t e) -> p t e", t=1).broadcast_to([P, QT, E])
                        chain.link(v.tensor_tensor(where[:, :, :], ranks, so_far, ALU.add), step)
                        chain.link(v.tensor_tensor(count[:, :], aux[1][:, QT * E:(QT + 1) * E], count[:, :], ALU.add), step)
                        v.tensor_tensor(where[:, :, :], where[:, :, :], regions, ALU.add).then_inc(m["rank_r"], 1)
                        step.wait(dve, m["rank_r"], past + 1)
                    if at == (6, 3, 2) and past is not None:
                        for k in range(2):
                            r = v.tensor_tensor(picked[:, k, :, :], where[:, :, :], hot[:, k, :, :], ALU.mult)
                        chain.link(r, step)
                        chain.link(v.tensor_reduce(pos_f[:, :], picked[:, :, :, :].rearrange("p k t e -> p (k t) e"), op=ALU.add, axis=AX.X), step)
                        step.wait(dve, m["scat"], past * (2 * QT * 16))
                        chain.link(v.tensor_copy(pos_i[:, :], pos_f[:, :]), step)
                    if at == (6, 3, 3) and past is not None:
                        step.wait(dve, m["gap_exp"], past + 1)
                        chain.link(v.tensor_scalar(mix[:, 1, :], e_gap[:, :], 1.0, None, ALU.add), step)
                        chain.link(v.reciprocal(mix[:, 0, :], mix[:, 1, :]), step)
                        chain.link(v.tensor_tensor(mix[:, 1, :], mix[:, 0, :], e_gap[:, :], ALU.mult), step)
                        v.tensor_copy(hn2[:, :, D:D + 1], token[:, :].rearrange("p (t e) -> p t e", e=1))
                        chain.link(v.tensor_scalar(weight[:, :, :].rearrange("p a b -> p (a b)"),
                                                   mix[:, :, :].rearrange("p a b -> p (a b)"), gate[:, 1:2], None, ALU.mult), step)
                        v.tensor_scalar(token[:, :], token[:, :], float(S), None, ALU.add).then_inc(m["route"], 1)
                    if cross is not None:
                        for c, where_ in enumerate(((7, 0, 0), (7, 0, 2))):
                            if at == where_:
                                if c == 0:
                                    step.wait(dve, m["xa_ld"], (cross + 1) * 16)
                                    step.wait(dve, m["post_norm"], step.u_cross * G + 4)
                                    step.wait(dve, m["kept_st"], cross * 32)
                                two = slice(2 * c, 2 * c + 2)
                                chain.link(v.scalar_tensor_tensor(out=x1[:, two, :], in0=att["cross"][:, two, :], scalar=gate[:, 0:1],
                                                                  in1=x_again[:, two, :], op0=ALU.mult, op1=ALU.add), step)
                        for c, where_ in enumerate(((7, 0, 1), (7, 0, 3))):
                            if at == where_:
                                for t in (2 * c, 2 * c + 1):
                                    r = v.bn_stats(st_1[:, t, :], x1[:, t, :])
                                chain.link(r, step)
                        if at == (7, 1, 0):
                            wait_apart(step, dve, (m["x1_rstd"], cross))
                            for t in range(QT):
                                r = v.bn_aggr(mv_1[:, t, :], st_1[:, t, :])
                            r.then_inc(m["x1_stat"], 1)
                        if at[:2] == (7, 3):
                            if hd == 0:
                                step.wait(dve, m["x1_rstd"], cross + 1)
                                step.wait(dve, m["x1_stat"], cross + 1)
                                step.wait(dve, m["x1_norm"], cross)
                            r = v.tensor_scalar(xn[:, hd, :], x1[:, hd, :], mv_1[:, hd, 0:1], r_1[:, hd:hd + 1], ALU.subtract, ALU.mult)
                            if hd == QT - 1:
                                r.then_inc(m["xn_done"], 1)

                def body(step):
                    for s in range(8):
                        mx, tail, ng = step.max_of(s), step.tail_of(s), step.neg_of(s)
                        for kt in range(QT):
                            for hd in range(HG):
                                extra(step, s, kt, hd)
                                if kt == 0 and ng:
                                    split_neg(step, ng, hd)
                                if (kt, hd) == (2, 1) and tail:
                                    post_norm(step, tail)
                                if mx:
                                    reduce_unit(step, mx, kt, hd)

                run_steps(dve, lambda step: chain.loop_body(step, body, DVE_LINKS))

            @block.gpsimd
            def _(pool):
                g_ = nc.gpsimd
                chain = Chain(pool, m["pool"])
                pool.wait_ge(m["ready_v"], 2)

                def split(step, src, dst, done, after, sent):
                    flat = lambda a: a.rearrange("p a b -> p (a b)")
                    s_, r = flat(src[:, :, :]), flat(rest[:, :, :])
                    p_ = [flat(dst[:, n, :, :]) for n in range(3)]
                    wait_apart(step, pool, (m[sent[0]], sent[1]))
                    chain.link(g_.tensor_scalar(p_[0], s_, 1.0, 0.0, ALU.mult, ALU.add), step)
                    chain.link(g_.tensor_tensor(r, s_, p_[0], ALU.subtract), step)
                    chain.link(g_.tensor_scalar(p_[1], r, 1.0, 0.0, ALU.mult, ALU.add), step)
                    g_.tensor_tensor(p_[2], r, p_[1], ALU.subtract).then_inc(m[done], 1)
                    wait_apart(step, pool, (m[done], after))

                def rsqrt(step, dst, src, scale, eps):
                    chain.link(g_.tensor_scalar(tmp_r[:, :].rearrange("p (a b) -> p a b", b=1), src, scale, eps, ALU.mult, ALU.add), step)
                    return g_.tensor_tensor(dst, tmp_r[:, :], half[:, 0:QT], ALU.pow)

                def extra(step, s):
                    cross, own, past, ahead = step.cross, step.own, step.past, step.ahead
                    if s in (0, 1) and own is not None:
                        o = "qk"[s]
                        flat = (flat_q, flat_k)[s]
                        step.wait(pool, m["rope_q" if s == 0 else "rope_k"], (own + 1) * (2 * DC))
                        sin = rope_sb[:, 1:2, :].broadcast_to([P, DC, S])
                        chain.link(g_.tensor_tensor(turned[:, :, :], turned[:, :, :], sin, ALU.mult), step)
                        g_.tensor_tensor(flat[:, :, :], turned[:, :, :], with_cos[:, :, :], ALU.add).then_inc(m["rope_used"], 1)
                        wait_apart(step, pool, (m["rope_used"], own * 2 + (s + 1)))
                        split(step, flat, parts[o], "oq_parts" if s == 0 else "ok_parts", own + 1,
                              ("x_st" if s == 0 else "c_st", most(own + 2, B) * 96))
                    if s == 3 and ahead is not None:
                        step.wait(pool, m["x_stat"], ahead + 1)
                        wait_apart(step, pool, (m["x_norm"], ahead))
                        rsqrt(step, r_x[:, :], mv_x[:, :, 1:2], 1.0, 1e-5).then_inc(m["x_rstd"], 1)
                    if s == 4 and past is not None:
                        step.wait(pool, m["h_sq"], (past + 1) * QT)
                        wait_apart(step, pool, (m["h_norm"], past))
                        rsqrt(step, r_h[:, :], ss[:, :].rearrange("p (a b) -> p a b", b=1), 1.0 / D, 1e-6).then_inc(m["h_rstd"], 1)
                    if s == 6 and past is not None:
                        wait_apart(step, pool, (m["base_st"], past * 16), (m["h_sum"], (past + 1) * DC), (m["kept_ld"], (past + 1) * 32))
                        chain.link(g_.tensor_scalar(base[:, :, :], h[:, :, :], gate[:, 1:2], None, ALU.mult), step)
                        g_.tensor_tensor(base[:, :, :], base[:, :, :], kept[:, 0, :, :], ALU.add).then_inc(m["h_base"], 1)
                    if s in (4, 5) and ahead is not None:
                        o = "qk"[s - 4]
                        src, ev, done = ((flat_q, "x_ev", "x_parts"), (flat_k, "c_ev", "c_parts"))[s - 4]
                        wait_apart(step, pool, (m[ev], (ahead + 1) * DC))
                        if own is not None:
                            sent = ("oq_st" if s == 4 else "ok_st", (own + 1) * 96)
                        else:
                            sent = ("x_st" if s == 4 else "c_st", ahead * 96)
                        split(step, src, parts[o], done, ahead + 1, sent)
                    if s == 6 and ahead is not None:
                        if cross is not None:
                            step.wait(pool, m["pv_mm"], (step.u_cross + 1) * (G * 16))
                        wait_apart(step, pool, (m["ctx_ld"], (ahead + 1) * 16))
                        g_.tensor_scalar(v_of["cross"][:, :, :, 0:DH].rearrange("p t h d -> p (t h) d"),
                                         ctx_in[:, :, :].rearrange("p t (h d) -> p (t h) d", d=DH), 1.0, 0.0, ALU.mult, ALU.add)\
                            .then_inc(m["v_cross"], 1)
                    if s == 7 and cross is not None:
                        wait_apart(step, pool, (m["x1_stat"], cross + 1), (m["x1_norm"], cross))
                        chain.link(rsqrt(step, r_1[:, 0:QT], mv_1[:, :, 1:2], 1.0, 1e-5), step)
                        var = mv_1[:, :, 1:2].rearrange("p a b -> p (a b)")
                        chain.link(g_.tensor_tensor(tmp_r[:, :], var, r_1[:, 0:QT], ALU.mult), step)
                        chain.link(g_.tensor_tensor(tmp_r[:, :], tmp_r[:, :], r_1[:, 0:QT], ALU.mult), step)
                        rsqrt(step, r_1[:, QT:2 * QT], tmp_r[:, :].rearrange("p (a b) -> p a b", b=1), 1.0, 1e-6).then_inc(m["x1_rstd"], 1)
                    if s == 7 and past is not None:
                        wait_apart(step, pool, (m["route"], past + 1), (m["h_norm"], past + 1))
                        for k in range(2):
                            if k:
                                wait_apart(step, pool, (m["scat"], past * (2 * QT * 16) + QT * 16))
                            chain.link(g_.tensor_copy(hn2[:, :, D + 1:DX], weight[:, k, :].rearrange("p (t e) -> p t e", e=1)), step)
                            for t in range(QT):
                                g_.indirect_dma_start(
                                    out=rows_in, out_offset=bass.IndirectOffsetOnAxis(ap=pos_i[:, k * QT + t:k * QT + t + 1], axis=0),
                                    in_=hn2[:, t, :], in_offset=None).then_inc(m["scat"], 16)

                def body(step):
                    for s in range(8):
                        extra(step, s)

                run_steps(pool, lambda step: chain.loop_body(step, body, POOL_LINKS))
                pool.wait_ge(m["scat"], B * 2 * QT * 16)

        with ExitStack() as st:
            def s2(name, *shape, dt=F32):
                return sb(name, (P, *shape), dt, st)

            def one(name, *shape, dt=F32):
                return sb(name, (1, *shape), dt, st)

            WG, WD = DC * F, FC * D
            wg_sb, wu_sb, wd_sb = s2("wg_sb", 2 * WG), s2("wu_sb", 2 * WG), s2("wd_sb", 2 * WD)
            rows_sb = [s2("rows0", DX), s2("rows1", DX)]
            rows_t = s2("rows_t", DC, P)
            silu, hidden, hidden_t = s2("silu", F), s2("hidden", F), s2("hidden_t", FC, P)
            whose = [s2(f"whose{n}", 1, dt=I32) for n in range(2)]
            weight = [s2(f"row_weight{n}", 1) for n in range(2)]
            so_far = [s2(f"so_far{n}", D) for n in range(2)]
            more = [s2(f"more{n}", D) for n in range(2)]
            table_sb = one("table_sb", 2, TILES, E)
            full_i, full_f, cum = one("full_i", E, dt=I32), one("full_f", E), one("cum", E)
            ones_e, skip = one("ones_e", E), one("skip", E)
            passed, skipped = one("passed", TILES, E), one("skipped", TILES, E)
            expert_f, row_f, odd_f = one("expert_f", TILES), one("row_f", TILES), one("odd_f", TILES)
            start_f, even_f = one("start_f", TILES), one("even_f", TILES)
            expert_i, row_i = one("expert_i", TILES, dt=I32), one("row_i", TILES, dt=I32)
            start_i, half_i = one("start_i", TILES, dt=I32), one("half_i", TILES, dt=I32)
            odd_i, wg_off, wd_off = (one(n, TILES, dt=I32) for n in ("odd_i", "wg_off", "wd_off"))
            old_i = [one(f"old_i{n}", TILES, dt=I32) for n in range(2)]
            end_f, cum_i, pad_i = one("end_f", E), one("cum_i", E, dt=I32), one("pad_i", E, dt=I32)

            def bank(name):
                return st.enter_context(nc.psum_tensor(name, [P, 512], F32))

            gate_ps, up_ps = [bank("gate_ps0"), bank("gate_ps1")], [bank("up_ps0"), bank("up_ps1")]
            rows_ps, y_ps = bank("rows_ps"), bank("y_ps")
            hid_ps = [bank("hid_ps0"), bank("hid_ps1")]

            m = {n: sem("t_" + n, st) for n in """tab_ld chain tab pad pad_at w_ld x_tr x_ev gate_mm up_mm silu hid
                hid_tr hid_ev_a hid_ev_v y_mm y_done owner""".split()}
            x_ld, far_ld, far_st = ([sem(f"t_{k}{n}", st) for n in range(2)] for k in ("x_ld", "far_ld", "far_st"))
            block = st.enter_context(nc.Block())
            PAIRS = TILES // 2

            def pairs(eng, body):
                body(0, True, False)
                with eng.Fori(1, PAIRS - 1) as jj:
                    body(jj, False, False)
                body(PAIRS - 1, False, True)

            def wait_apart(eng, *waits):
                for _, v in waits:
                    if not isinstance(v, int):
                        eng.compute_val(v)
                eng.wait_ge(m["tab"], 1)
                for s_, v in waits:
                    wait(eng, s_, v)

            def wait(eng, s_, v):
                if not isinstance(v, int) or v > 0:
                    eng.wait_ge(s_, v)

            @block.sync
            def _(sp):
                def load_expert(e, par):
                    sp.dma_start(wg_sb[:, par * WG:(par + 1) * WG].rearrange("p (c f) -> p c f", c=DC),
                                 wg[e].rearrange("(c p) f -> p c f", p=P)).then_inc(m["w_ld"], 16)
                    sp.dma_start(wu_sb[:, par * WG:(par + 1) * WG].rearrange("p (c f) -> p c f", c=DC),
                                 wu[e].rearrange("(c p) f -> p c f", p=P)).then_inc(m["w_ld"], 16)
                    whole = (F // P) * P
                    sp.dma_start(wd_sb[:, par * WD:par * WD + whole // P * D].rearrange("p (k d) -> p k d", d=D),
                                 wd[e][0:whole, :].rearrange("(k p) d -> p k d", p=P)).then_inc(m["w_ld"], 16)
                    sp.dma_start(wd_sb[0:F - whole, par * WD + whole // P * D:(par + 1) * WD], wd[e][whole:F, :]).then_inc(m["w_ld"], 16)

                sp.dma_start(table_sb[:, :, :, :], c_table).then_inc(m["tab_ld"], 16)
                load_expert(0, 0)
                sp.wait_ge(m["pad_at"], 1)
                for e in range(E):
                    at = sp.value_load(pad_i[0:1, e:e + 1], min_val=0, max_val=ROWS - P)
                    sp.dma_start(rows_in[bass.ds(at, P), :], padding[:, :]).then_inc(m["pad"], 16)
                sp.wait_ge(m["tab"], 1)
                sp.wait_ge(m["w_ld"], 64)
                load_expert(1, 1)
                with sp.Fori(1, E // 2) as ee:
                    for par in range(2):
                        e = ee * 2 + par
                        done = sp.value_load(cum_i[0:1, bass.ds(e - 2, 1)], min_val=1, max_val=TILES + 1)
                        wait_apart(sp, (m["y_done"], done), (m["w_ld"], e * 64))
                        load_expert(e, par)

            @block.gpsimd
            def _(pool):
                g_ = nc.gpsimd
                for n in range(2):
                    g_.dma_start(so_far[n][:, :], out_rows[0:P, :]).then_inc(far_st[n], 16)
                pool.wait_ge(m["tab"], 1)

                def fetch(j, par):
                    old = [pool.value_load(old_i[n][0:1, bass.ds(j, 1)], min_val=16, max_val=16 * (PAIRS + 1)) for n in range(2)]
                    wait_apart(pool, (far_st[0], old[0]), (far_st[1], old[1]),
                               (m["owner"], j + 1))
                    g_.indirect_dma_start(out=so_far[par][:, :], out_offset=None, in_=out_rows,
                                          in_offset=bass.IndirectOffsetOnAxis(ap=whose[par][:, 0:1], axis=0),
                                          bounds_check=T - 1, oob_is_err=False).then_inc(far_ld[par], 16)

                def store(j, par):
                    wait_apart(pool, (m["y_done"], j + 2))
                    g_.indirect_dma_start(out=out_rows, out_offset=bass.IndirectOffsetOnAxis(ap=whose[par][:, 0:1], axis=0),
                                          in_=more[par][:, :], in_offset=None,
                                          bounds_check=T - 1, oob_is_err=False).then_inc(far_st[par], 16)

                def body(jj, first, last):
                    for h_ in range(2):
                        j = jj * 2 + h_
                        store(j, h_)
                        if not (last and h_):
                            fetch(j + 1, 1 - h_)

                fetch(0, 0)
                pairs(pool, body)
                for n in range(2):
                    pool.wait_ge(far_st[n], 16 * (PAIRS + 1))

            @block.vector
            def _(dve):
                v = nc.vector
                links = [0]

                def link(ins):
                    links[0] += 1
                    ins.then_inc(m["chain"], 1)
                    dve.wait_ge(m["chain"], links[0])

                link(v.tensor_tensor(end_f[:, :], count[0:1, :], region_e[0:1, :], ALU.add))
                v.tensor_copy(pad_i[:, :], end_f[:, :]).then_inc(m["pad_at"], 1)
                link(v.tensor_scalar(full_i[:, :], count[0:1, :], float(P - 1), None, ALU.add))
                link(v.tensor_scalar(full_i[:, :], full_i[:, :], 7, None, ALU.logical_shift_right))
                link(v.tensor_copy(full_f[:, :], full_i[:, :]))
                link(v.memset(ones_e[:, :], 1.0))
                link(v.tensor_tensor_scan(cum[:, :], ones_e[:, :], full_f[:, :], 0.0, ALU.mult, ALU.add))
                dve.wait_ge(m["tab_ld"], 16)
                wide = lambda a: a.rearrange("p (t e) -> p t e", t=1).broadcast_to([1, TILES, E])
                link(v.tensor_tensor(passed[:, :, :], wide(cum[:, :]), table_sb[:, 0, :, :], ALU.is_le))
                link(v.tensor_reduce(expert_f[:, :], passed[:, :, :], op=ALU.add, axis=AX.X))
                link(v.tensor_scalar(expert_f[:, :], expert_f[:, :], float(E - 1), None, ALU.min))
                link(v.tensor_copy(expert_i[:, :], expert_f[:, :]))
                link(v.tensor_scalar(skip[:, :], full_f[:, :], -float(P), float(CAP), ALU.mult, ALU.add))
                link(v.tensor_tensor(skipped[:, :, :], wide(skip[:, :]), passed[:, :, :], ALU.mult))
                link(v.tensor_reduce(row_f[:, :], skipped[:, :, :], op=ALU.add, axis=AX.X))
                link(v.tensor_tensor(row_f[:, :], row_f[:, :], table_sb[:, 1, :, 0:1].rearrange("p t e -> p (t e)"), ALU.add))
                link(v.tensor_copy(row_i[:, :], row_f[:, :]))
                link(v.tensor_tensor(skipped[:, :, :], wide(full_f[:, :]), passed[:, :, :], ALU.mult))
                link(v.tensor_reduce(start_f[:, :], skipped[:, :, :], op=ALU.add, axis=AX.X))
                for n in range(2):
                    link(v.tensor_scalar(start_i[:, :], start_f[:, :], float(1 - n), None, ALU.add))
                    link(v.tensor_scalar(half_i[:, :], start_i[:, :], 1, None, ALU.logical_shift_right))
                    link(v.tensor_copy(even_f[:, :], half_i[:, :]))
                    link(v.tensor_scalar(old_i[n][:, :], even_f[:, :], 16.0, 16.0, ALU.mult, ALU.add))
                link(v.tensor_scalar(odd_i[:, :], expert_i[:, :], 1, None, ALU.bitwise_and))
                link(v.tensor_copy(odd_f[:, :], odd_i[:, :]))
                link(v.tensor_scalar(wg_off[:, :], odd_f[:, :], float(WG), None, ALU.mult))
                link(v.tensor_scalar(wd_off[:, :], odd_f[:, :], float(WD), None, ALU.mult))
                v.tensor_scalar(cum_i[:, :], cum[:, :], 1.0, None, ALU.add).then_inc(m["tab"], 1)
                dve.wait_ge(m["tab"], 1)

                def owner(j, par):
                    wait(dve, x_ld[par], (j - par) * 8 + 16)
                    wait(dve, far_st[par], (j - par) * 8 + 16)
                    v.tensor_copy(whose[par][:, :], rows_sb[par][:, D:D + 1])
                    v.tensor_copy(weight[par][:, :], rows_sb[par][:, D + 1:DX]).then_inc(m["owner"], 1)

                def add_up(j, par):
                    wait(dve, m["y_mm"], j + 1)
                    wait(dve, m["owner"], j + 1)
                    wait(dve, far_ld[par], (j - par) * 8 + 16)
                    wait(dve, far_st[par], (j - par) * 8 + 16)
                    v.scalar_tensor_tensor(out=more[par][:, :], in0=y_ps[:, 0:D], scalar=weight[par][:, 0:1], in1=so_far[par][:, :],
                                           op0=ALU.mult, op1=ALU.add).then_inc(m["y_done"], 1)

                def body(jj, first, last):
                    for h_ in range(2):
                        j = jj * 2 + h_
                        wait(dve, m["hid_tr"], j * 2)
                        for n in range(2):
                            wait(dve, m["silu"], j * 2 + (n + 1))
                            wait(dve, m["up_mm"], j * 2 + (n + 1))
                            v.tensor_tensor(hidden[:, n * FH:(n + 1) * FH], silu[:, n * FH:(n + 1) * FH], up_ps[n][:, 0:FH], ALU.mult)\
                                .then_inc(m["hid"], 1)
                        if not (first and h_ == 0):
                            add_up(j - 1, 1 - h_)
                        wait(dve, m["hid_tr"], j * 2 + 2)
                        v.tensor_copy(hidden_t[:, 4, :], hid_ps[1][:, 0:P])
                        v.tensor_copy(hidden_t[0:F % P, 5, :], hid_ps[1][0:F % P, P:2 * P]).then_inc(m["hid_ev_v"], 1)
                        if not (last and h_):
                            owner(j + 1, 1 - h_)

                v.memset(ones_e[:, :], 1.0).then_inc(m["y_done"], 1)
                owner(0, 0)
                pairs(dve, body)
                add_up(TILES - 1, 1)

            @block.scalar
            def _(act):
                act.wait_ge(m["tab"], 1)
                act.wait_ge(m["pad"], 16 * E)

                def load(j, par):
                    at = act.value_load(row_i[0:1, bass.ds(j, 1)], min_val=0, max_val=ROWS - P)
                    act.dma_start(rows_sb[par][:, :], rows_in[bass.ds(at, P), :]).then_inc(x_ld[par], 16)

                def rows(j):
                    wait(act, m["x_tr"], j + 1)
                    wait(act, m["up_mm"], j * 2)
                    for c in range(DC):
                        act.activation(rows_t[:, c, :], rows_ps[:, c * P:(c + 1) * P], ACT.Identity, scale=g2_sb[:, c:c + 1]).then_inc(m["x_ev"], 1)

                def body(jj, first, last):
                    for h_ in range(2):
                        j = jj * 2 + h_
                        if not last:
                            wait_apart(act, (m["owner"], j + 1))
                            load(j + 2, h_)
                        wait(act, m["hid"], j * 2)
                        for n in range(2):
                            wait(act, m["gate_mm"], j * 2 + (n + 1))
                            act.activation(silu[:, n * FH:(n + 1) * FH], gate_ps[n][:, 0:FH], ACT.Silu).then_inc(m["silu"], 1)
                        if not (last and h_):
                            rows(j + 1)
                        wait(act, m["hid_tr"], j * 2 + 1)
                        act.activation(hidden_t[:, 0:4, :].rearrange("p k t -> p (k t)"), hid_ps[0][:, :], ACT.Copy).then_inc(m["hid_ev_a"], 1)

                load(0, 0)
                load(1, 1)
                rows(0)
                pairs(act, body)

            @block.tensor
            def _(pe):
                mm, tr = nc.tensor.matmul, nc.tensor.transpose
                pe.wait_ge(m["tab"], 1)

                def reg(tab, j, most_):
                    return pe.value_load(tab[0:1, bass.ds(j, 1)], min_val=0, max_val=most_)

                def turn_rows(j, par):
                    wait(pe, m["x_ev"], j * DC)
                    wait(pe, x_ld[par], (j - par) * 8 + 16)
                    for c in range(DC):
                        r = tr(rows_ps[:, c * P:(c + 1) * P], rows_sb[par][:, c * P:(c + 1) * P], ident[:, :])
                    r.then_inc(m["x_tr"], 1)

                def up(j):
                    e = reg(expert_i, j, E - 1)
                    off = reg(wg_off, j, WG)
                    pe.wait_ge(m["w_ld"], e * 64 + 64)
                    wait(pe, m["x_ev"], j * DC + DC)
                    for w, ps, used, done in ((wg_sb, gate_ps, "silu", "gate_mm"), (wu_sb, up_ps, "hid", "up_mm")):
                        for n in range(2):
                            wait(pe, m[used], j * 2 + (n - 1) if n == 0 else j * 2)
                            for c in range(DC):
                                r = mm(ps[n][:, 0:FH], rows_t[:, c, :], w[:, bass.ds(off + (c * F + n * FH), FH)],
                                       start=(c == 0), stop=(c == DC - 1))
                            r.then_inc(m[done], 1)

                def turn_hidden(j):
                    wait(pe, m["hid_ev_a"], j)
                    wait(pe, m["hid_ev_v"], j)
                    for k in range(FC):
                        n = min(P, F - k * P)
                        if k == 0:
                            wait(pe, m["hid"], j * 2 + 1)
                        if k * P + n > FH and (k - 1) * P + P <= FH:
                            wait(pe, m["hid"], j * 2 + 2)
                        r = tr(hid_ps[k // 4][0:n, (k % 4) * P:(k % 4 + 1) * P], hidden[:, k * P:k * P + n], ident[:, :])
                        if k == 3 or k == FC - 1:
                            r.then_inc(m["hid_tr"], 1)

                def down(j):
                    off = reg(wd_off, j, WD)
                    wait(pe, m["hid_ev_a"], j + 1)
                    wait(pe, m["hid_ev_v"], j + 1)
                    wait(pe, m["y_done"], j + 1)
                    for k in range(FC):
                        n = min(P, F - k * P)
                        r = mm(y_ps[:, 0:D], hidden_t[0:n, k, :], wd_sb[0:n, bass.ds(off + k * D, D)], start=(k == 0), stop=(k == FC - 1))
                    r.then_inc(m["y_mm"], 1)

                def body(jj, first, last):
                    for h_ in range(2):
                        j = jj * 2 + h_
                        up(j)
                        if not (last and h_):
                            turn_rows(j + 1, 1 - h_)
                        if not (first and h_ == 0):
                            down(j - 1)
                        turn_hidden(j)

                turn_rows(0, 0)
                pairs(pe, body)
                down(TILES - 1)


_INS = ["x", "ctx_1024", "g_xattn", "g_ffn", "L0_ffn_wq", "L0_ffn_wk", "L0_ffn_wv", "L0_ffn_wo", "L0_ffn_w_router",
        "L0_ffn_wg", "L0_ffn_wu", "L0_ffn_wd", "L0_ffn_g1", "L0_ffn_g2"]


def kernel(**inputs):
    import concourse.bacc as bacc
    from concourse.bass_utils import run_bass_kernel_spmd

    nc = bacc.Bacc("TRN2", target_bir_lowering=False, num_devices=1)
    arrays, args = {}, []
    for name in _INS:
        a = np.ascontiguousarray(inputs[name])
        arrays[f"in_{name}"] = a
        args.append(nc.dram_tensor(f"in_{name}", a.shape, mybir.dt.from_np(a.dtype), kind="ExternalInput").ap())
    out = nc.dram_tensor("out_0", (B, S, D), F32, kind="ExternalOutput").ap()
    flamingo_block(nc, *args, out)
    r = run_bass_kernel_spmd(nc, [arrays], core_ids=[0])
    return r.results[0]["out_0"]
```

```python
from contextlib import ExitStack

import numpy as np
import concourse.bass as bass
from concourse import mybir

ALU = mybir.AluOpType
ACT = mybir.ActivationFunctionType
AX = mybir.AxisListType
F32, BF16, F32R = mybir.dt.float32, mybir.dt.bfloat16, mybir.dt.float32r
I32, U32 = mybir.dt.int32, mybir.dt.uint32

P = 128
B, S, D = 8, 512, 256
H, DH = 16, 16
E, F = 8, 704
QT = S // P
DC = D // P
HG = 4
G = H // HG
KROWS = 6 * DH
STACK_LOADS = 6
NEGROWS = 3
DX = D + 2
T = B * S
NT = T // P
CAP = T + P
TILES = 2 * T // P + E
SPARE = TILES - 2 * T // P
ROWS = E * CAP + SPARE * P
FH = F // 2
FC = (F + P - 1) // P
WG, WD = DC * F, FC * D
WALL = 2 * WG + WD
SCALE = float(DH) ** -0.5
MASKED = -3.0e38
DVE_LINKS, POOL_LINKS = 19, 40
LAST = B - 1
VALUES_AT = 1


class Lin:

    def __init__(self, a, c):
        self.a, self.c = a, c

    def __add__(self, n):
        return Lin(self.a, self.c + n)

    def __sub__(self, n):
        return Lin(self.a, self.c - n)

    def __mul__(self, n):
        return Lin(self.a * n, self.c * n)

    __radd__, __rmul__ = __add__, __mul__


class Step:

    def __init__(self, i, reg=None):
        self.reg = reg
        v = Lin(1, 0) if reg is not None else i
        has = (lambda n: True) if reg is not None else (lambda n: 0 <= i + n <= LAST)
        self.cross = v + 1 if has(1) else None
        self.own = v + 0 if has(0) else None
        self.past = v - 1 if has(-1) else None
        self.ahead = v + 2 if has(2) else None
        if reg is not None:
            self.u_cross, self.u_own, self.u_past = Lin(2, 1), Lin(2, 2), Lin(2, 0)
        else:
            self.u_cross = 0 if i == -1 else 2 * i + 1
            self.u_own = 15 if i == LAST else 2 * i + 2
            self.u_past = 15 if i == LAST + 1 else 2 * i
        self.i = i

    def value(self, v):
        if isinstance(v, Lin):
            return self.reg * v.a + v.c if v.a else v.c
        return v

    def wait(self, eng, sem, v):
        if isinstance(v, Lin) or v > 0:
            eng.wait_ge(sem, self.value(v))

    def named(self, which):
        b, u = {"cross": (self.cross, self.u_cross), "own": (self.own, self.u_own), "past": (self.past, self.u_past)}[which]
        return None if b is None else (which, b, u)

    def max_of(self, s):
        u = self.named("cross" if s < 4 else "own")
        return u and (*u, s % 4)

    def main_of(self, s):
        which, g = [("past", 2), ("past", 3), ("cross", 0), ("cross", 1), ("cross", 2), ("cross", 3), ("own", 0), ("own", 1)][s]
        u = self.named(which)
        return u and (*u, g)

    def tail_of(self, s):
        return self.main_of(s - 1) if s else self._past(1)

    def neg_of(self, s):
        return self.max_of(s - 1) if s else self._past(3)

    def _past(self, g):
        u = self.named("past")
        return u and (*u, g)


def most(v, n):
    return v if isinstance(v, Lin) else min(v, n)


def is_self(which):
    return which != "cross"


PIECES_AT = ((0,), (1,), (2,), (3,), (4,), (5,), (6, 7), ())


def splits_on_dve(step):
    return step.i in (-2, LAST)


def run_steps(eng, body):
    for i in (-2, -1, 0):
        body(Step(i))
    with eng.Fori(1, B - 2) as reg:
        body(Step(None, reg))
    for i in range(B - 2, B + 1):
        body(Step(i))


def reads_before(step, s, kind):
    of = Step.tail_of if kind == "tail" else Step.neg_of
    cur, s = step, s - 1
    while True:
        while s >= 0:
            u = of(cur, s)
            if u:
                return u[2] * G + u[3] + 1
            s -= 1
        if cur.i is None:
            return (Lin(2, 0) * G + 1) if kind == "tail" else (Lin(2, 0) * G + 3)
        if cur.i <= -2:
            return 0
        cur, s = Step(cur.i - 1), 7


def host_constants():
    p = np.arange(P)
    upper = np.where(p[None, :] > p[:, None], MASKED, 0.0)
    squares = np.stack([
        np.eye(P),
        upper,
        upper.T,
        (p[:, None] < p[None, :]) * 1.0,
        np.ones((P, P)),
    ], 1).astype(np.float32)
    inv_freq = 1.0 / 10000.0 ** (np.arange(0, DH, 2, dtype=np.float32) / DH)
    freqs = np.einsum("i,j->ij", np.arange(S, dtype=np.float32), inv_freq)
    emb = np.concatenate([freqs, freqs], -1)
    sign = np.where(np.arange(DH) < DH // 2, -1.0, 1.0).astype(np.float32)
    rope = np.stack([np.tile(np.cos(emb).T, (P // DH, 1)), np.tile((np.sin(emb) * sign).T, (P // DH, 1))], 1)
    small = np.zeros((P, 2 * E + QT), np.float32)
    small[:, :E] = np.arange(E)
    small[:, E:2 * E] = np.arange(E) * CAP
    small[:, 2 * E:] = p[:, None] + P * np.arange(QT)[None, :]
    return squares, rope.astype(np.float32), small


def table_constants():
    return np.repeat(np.arange(TILES, dtype=np.float32), E)[None]


def flamingo_block(nc, x, ctx, g_xattn, g_ffn, wq, wk, wv, wo, w_router, wg, wu, wd, g1, g2, out):
    squares, rope, small = host_constants()
    c_squares = nc.inline_tensor(squares, "c_squares").ap()
    c_rope = nc.inline_tensor(rope, "c_rope").ap()
    c_small = nc.inline_tensor(small, "c_small").ap()
    c_table = nc.inline_tensor(table_constants(), "c_table").ap()

    pieces = [(w_, c * P, 1, n * WG + c * F, F) for n, w_ in enumerate((wg, wu)) for c in range(DC)]
    pieces += [(wd, k * P, 2, 2 * WG + k * D, 2 * D) for k in (0, 2)] + [(wd, k * P, 1, 2 * WG + k * D, D) for k in (4, 5)]

    def scratch(name, shape, dt=F32):
        return nc.dram_tensor(name, shape, dt, kind="Internal").ap()

    parts_d = {(a, o): scratch(f"parts_{a}_{o}", (B, 3, DH, H, S), BF16) for a in ("cross", "own") for o in "qk"}
    kept_d = scratch("kept", (B, 2, P, QT, D))
    rows_in = scratch("rows_in", (ROWS, DX))
    w_split = scratch("w_split", (E, P, 2, WALL))

    x_d = x.rearrange("b (t p) d -> b p t d", p=P)
    ctx_d = ctx.rearrange("b (t p) d -> b p t d", p=P)
    out_d = out.rearrange("b (t p) d -> b p t d", p=P)
    out_rows = out.rearrange("b s d -> (b s) d")

    outer = ExitStack()
    with outer:
        def sb(name, shape, dt=F32, stack=None):
            return (stack or outer).enter_context(nc.sbuf_tensor(name, list(shape), dt))

        def sem(name, stack=None):
            return (stack or outer).enter_context(nc.semaphore(name))

        ident = sb("ident", (P, P))
        small_sb = sb("small_sb", (P, 2 * E + QT))
        iota_e, region_e = small_sb[:, 0:E], small_sb[:, E:2 * E]
        gate = sb("gate", (P, 2))
        g1_sb, g2_sb = sb("g1_sb", (P, DC)), sb("g2_sb", (P, DC))
        count = sb("count", (P, E))

        def one(name, *shape, dt=F32):
            return sb(name, (1, *shape), dt)

        expert_i, row_i, w_off = (one(n, TILES, dt=I32) for n in ("expert_i", "row_i", "w_off"))
        old_i = [one(f"old_i{n}", TILES, dt=I32) for n in range(2)]
        cum_i, pad_i = one("cum_i", E, dt=I32), one("pad_i", E, dt=I32)
        padding = sb("padding", (P, DX))

        with ExitStack() as st:
            def s1(name, *shape, dt=F32):
                return sb(name, (P, *shape), dt, st)

            squares_sb = s1("squares_sb", 5, P)
            squares_b = s1("squares_b", 5, P, dt=BF16)
            ident_b, mask_qk, mask_kq, before_b, ones_b = (squares_b[:, n, :] for n in range(5))
            rope_sb = s1("rope_sb", 2, S)
            w_sb = {n: s1("sb_" + n, DC, D) for n in ("wq", "wk", "wv", "wo")}
            wr_sb = s1("wr_sb", DC, E)
            gates_in = sb("gates_in", (1, 2), F32, st)
            half = s1("half", 2 * QT)

            q_stack = [s1(f"q_stack{g}", HG, S, dt=BF16) for g in range(G)]
            k_stack = [s1(f"k_stack{g}", HG, S, dt=BF16) for g in range(G)]
            probs = s1("probs", 2, HG, S)
            v_of = {"cross": s1("v_cross", QT, H, 32), "own": s1("v_own", QT, H, 32)}
            x_in, ctx_in = s1("x_in", QT, D), s1("ctx_in", QT, D)
            xq = s1("xq", QT, D)
            x1, xn, hn1 = s1("x1", QT, D), s1("xn", QT, D), s1("hn1", QT, D)
            att = {"cross": s1("att_cross", QT, D), "own": s1("att_own", QT, D)}
            hn1_t, flat_q, flat_k = s1("hn1_t", DC, S), s1("flat_q", DC, S), s1("flat_k", DC, S)
            turned, with_cos = s1("turned", DC, S), s1("with_cos", DC, S)
            rest = s1("rest", DC, S)
            parts = {"q": s1("parts_q", 3, DC, S, dt=BF16), "k": s1("parts_k", 3, DC, S, dt=BF16)}
            out_t = s1("out_t", S)
            own_t = s1("own_t", DC, S)
            kept = s1("kept_sb", 2, QT, D)
            h, hn2, base = s1("h", QT, D), s1("hn2", QT, DX), s1("base_sb", QT, D)
            hn2_t = own_t
            w_in, w_parts = s1("w_in", F), s1("w_parts", 2, F, dt=F32R)
            neg = s1("neg", 2, HG, QT)
            neg_rest = s1("neg_rest", 2, HG * QT)
            neg_parts = s1("neg_parts", 2, NEGROWS, HG * QT, dt=BF16)
            neg_rows = sb("neg_rows", (NEGROWS * HG * QT, P), BF16, st)
            recip = s1("recip", HG * QT)
            st_x, mv_x = s1("st_x", QT, 6), s1("mv_x", QT, 2)
            st_1, mv_1 = s1("st_1", QT, 6), s1("mv_1", QT, 2)
            r_x, r_1, r_h = s1("r_x", QT), s1("r_1", 2 * QT), s1("r_h", QT)
            tmp_r = s1("tmp_r", QT)
            sq, ss = s1("sq", D), s1("ss", QT)
            lg, top, idx = s1("lg", QT, E), s1("top", QT, 8), s1("idx", QT, 8, dt=U32)
            idx_f = s1("idx_f", QT, 8)
            hot = s1("hot", 2, QT, E)
            hot_b = s1("hot_b", QT, E, dt=BF16)
            where, picked = s1("where", QT, E), s1("picked", 2, QT, E)
            pos_f, pos_i = s1("pos_f", 2 * QT), s1("pos_i", 2 * QT, dt=I32)
            gap, e_gap, mix, weight = s1("gap", QT), s1("e_gap", QT), s1("mix", 2, QT), s1("weight", 2, QT)
            token = s1("token", QT)

            def bank(name, dt=F32, n=512):
                return st.enter_context(nc.psum_tensor(name, [P, n], dt))

            max_ps = [bank("max_ps0"), bank("max_ps1")]
            key_ps = [bank("key_ps0"), bank("key_ps1")]
            pv_ps, turn_ps = bank("pv_ps"), bank("turn_ps")
            aux = [bank("aux0"), bank("aux1")]
            turn_b = turn_ps[:, :].bitcast(BF16)

            names = """ld_const ld_w ready_c ready_b ready_v gate_mm gate_act
                max_mm max_red neg_split neg_chain neg_tr neg_ev neg_dma
                key_mm exp_done pv_mm out_ev post_tr post_norm post_rc
                x_ld ctx_ld xa_ld kept_ld kept_st base_st x_stat x_rstd x_norm x_tr x_ev c_tr c_ev v_cross
                x1_stat x1_rstd x1_norm dve pool hn1_tr hn1_ev xn_done q_mm q_ev k_mm k_ev v_mm v_ev
                rope_q rope_k rope_used x_parts c_parts oq_parts ok_parts x_st c_st oq_st ok_st
                own_tr own_ev wo_mm h_sum h_sq h_rstd h_norm h_base hn2_tr hn2_ev lg_mm gap_r gap_exp hot_r rank_mm
                rank_r route scat w_in_ld w_part_st tab_ld pad_at pad""".split()
            m = {n: sem("s_" + n, st) for n in names}
            s_stack = [sem(f"s_stack{g}", st) for g in range(G)]

            class Chain:

                def __init__(self, eng, s):
                    self.eng, self.s, self.n, self.per, self.start = eng, s, 0, 0, 0

                def link(self, ins, step=None):
                    ins.then_inc(self.s, 1)
                    self.n += 1
                    if step is None or step.reg is None:
                        self.eng.wait_ge(self.s, self.n)
                    else:
                        wait_apart(step, self.eng, (self.s, Lin(self.per, self.n - self.per)))

                def loop_body(self, step, body, per):
                    if step.reg is None:
                        return body(step)
                    before, self.per = self.n, per
                    body(step)
                    assert self.n - before == per, (self.n - before, per)
                    self.n = before + per * (B - 3)

            block = st.enter_context(nc.Block())

            def wait_apart(step, eng, *waits):
                values = [(s_, step.value(v)) for s_, v in waits]
                for s_, v in values:
                    if not isinstance(v, int):
                        eng.compute_val(v)
                eng.wait_ge(m["ready_c"], 1)
                for s_, v in values:
                    if not isinstance(v, int) or v > 0:
                        eng.wait_ge(s_, v)

            @block.sync
            def _(sp):
                sp.dma_start(x_in[:, :, :], x_d[0]).then_inc(m["x_ld"], 16)
                sp.dma_start(ctx_in[:, :, :], ctx_d[0]).then_inc(m["ctx_ld"], 16)
                sp.dma_start(squares_sb[:, :, :], c_squares).then_inc(m["ld_const"], 16)
                sp.dma_start(ident[:, :], c_squares[:, 0, :]).then_inc(m["ld_const"], 16)
                sp.dma_start(rope_sb[:, :, :], c_rope).then_inc(m["ld_const"], 16)
                sp.dma_start(small_sb[:, :], c_small).then_inc(m["ld_const"], 16)
                sp.dma_start(gates_in[:, 0:1], g_xattn.rearrange("(a n) -> a n", a=1)).then_inc(m["ld_const"], 16)
                sp.dma_start(gates_in[:, 1:2], g_ffn.rearrange("(a n) -> a n", a=1)).then_inc(m["ld_const"], 16)
                sp.dma_start(g1_sb[:, :], g1.rearrange("(c p) -> p c", p=P), allow_slow_non_contiguous=True).then_inc(m["ld_const"], 16)
                sp.dma_start(g2_sb[:, :], g2.rearrange("(c p) -> p c", p=P), allow_slow_non_contiguous=True).then_inc(m["ld_const"], 16)

                def load_x(step):
                    if step.ahead is None:
                        return
                    b = step.ahead
                    step.wait(sp, m["x_norm"], b)
                    sp.dma_start(x_in[:, :, :], x_d[step.value(b)]).then_inc(m["x_ld"], 16)
                    step.wait(sp, m["c_tr"], b)
                    step.wait(sp, m["v_cross"], b)
                    sp.dma_start(ctx_in[:, :, :], ctx_d[step.value(b)]).then_inc(m["ctx_ld"], 16)

                def load_stack(step, which, b, u, g):
                    wait_apart(step, sp, (m["key_mm"], (u - 1) * (16 * G) + (16 * g + 16)))
                    kind = "own" if is_self(which) else "cross"
                    q_d, k_d = (parts_d[kind, o][step.value(b)] for o in "qk")
                    hs = slice(g * HG, (g + 1) * HG)
                    if g == 0:
                        step.wait(sp, m["oq_st" if kind == "own" else "x_st"], (b + 1) * 96)
                        step.wait(sp, m["ok_st" if kind == "own" else "c_st"], (b + 1) * 96)
                    for stack, src, r0, n, first_, same in ((q_stack, q_d, 0, 3, 0, False), (q_stack, q_d, 3, 2, 0, False), (q_stack, q_d, 5, 1, 0, False),
                                                            (k_stack, k_d, 0, 3, 0, True), (k_stack, k_d, 3, 2, 1, True), (k_stack, k_d, 5, 1, 2, True)):
                        if same:
                            a = src[first_:first_ + 1, :, hs, :].rearrange("n d h t -> n d (h t)").broadcast_to([n, DH, HG * S])
                        else:
                            a = src[0:n, :, hs, :].rearrange("n d h t -> (n d) (h t)")
                        sp.dma_start(stack[g][r0 * DH:(r0 + n) * DH, :, :].rearrange("p h t -> p (h t)"), a).then_inc(s_stack[g], 16)

                def store_parts(step, kind, o, b, ready, done):
                    step.wait(sp, m[ready], b + 1)
                    for part in range(3):
                        for c in range(DC):
                            dst = parts_d[kind, o][step.value(b)][part, :, c * 8:(c + 1) * 8, :]
                            sp.dma_start(dst.rearrange("d h t -> h d t"), parts[o][:, part, c, :]).then_inc(m[done], 16)

                def body(step):
                    cross, own, past, ahead = step.cross, step.own, step.past, step.ahead
                    if cross is not None:
                        load_stack(step, "cross", cross, step.u_cross, 1)
                    if own is not None:
                        step.wait(sp, m["xn_done"], own + 1)
                        sp.dma_start(kept_d[step.value(own), 0], x1[:, :, :]).then_inc(m["kept_st"], 16)
                        sp.dma_start(kept_d[step.value(own), 1], xn[:, :, :]).then_inc(m["kept_st"], 16)
                    load_x(step)
                    if cross is not None:
                        load_stack(step, "cross", cross, step.u_cross, 2)
                    if past is not None:
                        wait_apart(step, sp, (m["kept_st"], (past + 1) * 32), (m["h_base"], past))
                        for n in range(2):
                            sp.dma_start(kept[:, n, :, :], kept_d[step.value(past), n]).then_inc(m["kept_ld"], 16)
                    if cross is not None:
                        load_stack(step, "cross", cross, step.u_cross, 3)
                        step.wait(sp, m["kept_st"], cross * 32)
                        step.wait(sp, m["xn_done"], cross)
                        sp.dma_start(x1[:, :, :], x_d[step.value(cross)]).then_inc(m["xa_ld"], 16)
                    if own is not None:
                        store_parts(step, "own", "q", own, "oq_parts", "oq_st")
                        store_parts(step, "own", "k", own, "ok_parts", "ok_st")
                        for g in range(G):
                            load_stack(step, "own", own, step.u_own, g)
                    if ahead is not None:
                        store_parts(step, "cross", "q", ahead, "x_parts", "x_st")
                        store_parts(step, "cross", "k", ahead, "c_parts", "c_st")
                        u_next = 0 if step.i == -2 else step.u_own + 1
                        load_stack(step, "cross", ahead, u_next, 0)
                    if past is not None:
                        step.wait(sp, m["h_base"], past + 1)
                        sp.dma_start(out_d[step.value(past)], base[:, :, :]).then_inc(m["base_st"], 16)

                for name, w in (("wq", wq), ("wk", wk), ("wv", wv), ("wo", wo)):
                    sp.dma_start(w_sb[name][:, :, :], w.rearrange("(c p) n -> p c n", p=P)).then_inc(m["ld_w"], 16)
                sp.dma_start(wr_sb[:, :, :], w_router.rearrange("(c p) n -> p c n", p=P)).then_inc(m["ld_w"], 16)
                sp.wait_ge(m["ready_v"], 1)
                for n in range(SPARE):
                    sp.dma_start(rows_in[E * CAP + n * P:E * CAP + (n + 1) * P, :], padding[:, :]).then_inc(m["ld_w"], 16)
                def sp_body(step):
                    if step.i == -2:
                        store_parts(step, "cross", "q", 0, "x_parts", "x_st")
                        store_parts(step, "cross", "k", 0, "c_parts", "c_st")
                        load_stack(step, "cross", 0, 0, 0)
                    else:
                        body(step)

                run_steps(sp, sp_body)
                sp.wait_ge(m["x1_norm"], B)
                sp.wait_ge(m["kept_st"], 32 * B)
                sp.dma_start(xn[0:1, :, :].rearrange("p t d -> p (t d)")[:, 0:TILES * E], c_table).then_inc(m["tab_ld"], 16)
                sp.wait_ge(m["pad_at"], 1)
                for e in range(E):
                    at = sp.value_load(pad_i[0:1, e:e + 1], min_val=0, max_val=ROWS - P)
                    sp.dma_start(rows_in[bass.ds(at, P), :], padding[:, :]).then_inc(m["pad"], 16)
                sp.wait_ge(m["pad"], 16 * E)
                sp.wait_ge(m["base_st"], 16 * B)
                sp.wait_ge(m["kept_st"], 32 * B)
                sp.wait_ge(m["ld_w"], 16 * (5 + SPARE))

            @block.tensor
            def _(pe):
                mm = nc.tensor.matmul
                tr = nc.tensor.transpose
                pe.wait_ge(m["ready_c"], 1)
                pe.wait_ge(m["ld_const"], 16 * 8)
                mm(aux[0][:, 0:2], squares_sb[0:1, 4, :], gates_in[0:1, 0:2], start=True, stop=True).then_inc(m["gate_mm"], 1)
                pe.wait_ge(m["gate_act"], 1)

                def body_start(step):
                    if step.i == -1:
                        pe.wait_ge(m["ready_b"], G + 4)

                def max_unit(step, unit, qt, hd):
                    which, b, u, g = unit
                    n = u * G + g
                    j = HG * qt + hd
                    if j == 0:
                        step.wait(pe, s_stack[g], (u + 1) * (STACK_LOADS * 16))
                    step.wait(pe, m["max_red"], n * 16 + (j - 1))
                    own = is_self(which)
                    keys = (qt + 1) * P if own else S
                    ps = max_ps[j % 2]
                    r = mm(ps[:, 0:keys], q_stack[g][0:KROWS, hd, qt * P:(qt + 1) * P], k_stack[g][0:KROWS, hd, 0:keys],
                           start=True, stop=not own)
                    if own:
                        r = mm(ps[:, qt * P:keys], ident_b, mask_qk, start=False, stop=True)
                    r.then_inc(m["max_mm"], 1)

                def key_unit(step, unit, kt, hd):
                    which, b, u, g = unit
                    n = u * G + g
                    j = HG * kt + hd
                    if j == 0:
                        step.wait(pe, m["neg_dma"], (n + 1) * 16)
                    step.wait(pe, m["exp_done"], n * 16 + (j - 1))
                    own = is_self(which)
                    q0 = kt * P if own else 0
                    ps = key_ps[j % 2]
                    r = mm(ps[:, q0:S], k_stack[g][0:KROWS + NEGROWS, hd, kt * P:(kt + 1) * P],
                           q_stack[g][0:KROWS + NEGROWS, hd, q0:S], start=True, stop=not own)
                    if own:
                        r = mm(ps[:, q0:q0 + P], ident_b, mask_kq, start=False, stop=True)
                    r.then_inc(m["key_mm"], 1)

                def value_unit(step, unit, kt, hd):
                    which, b, u, g = unit
                    n = u * G + g
                    step.wait(pe, m["exp_done"], n * 16 + (HG * kt + hd + 1))
                    own = is_self(which)
                    if kt == 0 and hd == 0:
                        step.wait(pe, m["out_ev"], n)
                        if g == 0:
                            step.wait(pe, m["v_ev" if own else "v_cross"], (b + 1) * (DC if own else 1))
                    q0 = kt * P if own else 0
                    mm(pv_ps[32 * hd:32 * hd + 32, q0:S], v_of["own" if own else "cross"][:, kt, g * HG + hd, :],
                       probs[:, kt % 2, hd, q0:S], start=(kt == 0), stop=(kt == QT - 1), skip_group_check=True)\
                        .then_inc(m["pv_mm"], 1)

                def neg_turn(step, s):
                    unit = step.neg_of(s)
                    if not unit:
                        return
                    n = unit[2] * G + unit[3]
                    wait_apart(step, pe, (m["neg_split"], n + 1), (m["neg_ev"], n), (m["post_norm"], reads_before(step, s + 1, "tail")))
                    tr(turn_b[0:NEGROWS * HG * QT, 0:P], neg_parts[:, unit[3] % 2, :, :].rearrange("p a b -> p (a b)"), ident_b)\
                        .then_inc(m["neg_tr"], 1)

                def post_turn(step, s):
                    unit = step.tail_of(s)
                    if not unit:
                        return
                    n = unit[2] * G + unit[3]
                    step.wait(pe, m["out_ev"], n + 1)
                    step.wait(pe, m["post_norm"], n)
                    step.wait(pe, m["neg_ev"], reads_before(step, s, "neg"))
                    for qt in range(QT):
                        r = tr(turn_ps[:, qt * P:(qt + 1) * P], out_t[:, qt * P:(qt + 1) * P], ident[:, :])
                    r.then_inc(m["post_tr"], 1)

                def turn(c, src, done):
                    for t in range(QT):
                        r = tr(aux[c][:, t * P:(t + 1) * P], src[:, t, c * P:(c + 1) * P], ident[:, :])
                    r.then_inc(m[done], 1)

                def project(k, w, src, done):
                    o, c = k // DC, k % DC
                    r = mm(aux[o][:, :], w[:, c, o * P:(o + 1) * P], src[:, c, :], start=(c == 0), stop=(c == DC - 1))
                    if c == DC - 1:
                        r.then_inc(m[done], 1)

                def project_rows(t, src, w, done):
                    for c in range(DC):
                        r = mm(aux[t // 2][:, (t % 2) * D:(t % 2 + 1) * D], src[:, c, t * P:(t + 1) * P], w[:, c, :],
                               start=(c == 0), stop=(c == DC - 1))
                    if t % 2:
                        r.then_inc(m[done], 1)

                def extra(step, s, kt, hd):
                    cross, own, past, ahead = step.cross, step.own, step.past, step.ahead
                    at = (s, kt, hd)
                    if own is not None:
                        if at == (0, 1, 0):
                            step.wait(pe, m["x1_norm"], own + 1)
                            step.wait(pe, m["rank_r"], own - 1)
                            step.wait(pe, m["c_ev"], most(own + 2, B) * DC)
                            step.wait(pe, m["hn2_ev"], (own - 1) * DC)
                            turn(0, hn1, "hn1_tr")
                        if at == (0, 1, 2):
                            turn(1, hn1, "hn1_tr")
                        for k, where_ in enumerate(((0, 2, 2), (0, 3, 0), (0, 3, 2), (1, 0, 0))):
                            if at == where_:
                                if k == 0:
                                    if step.i == 0:
                                        pe.wait_ge(m["ld_w"], 16 * (5 + SPARE))
                                    step.wait(pe, m["hn1_ev"], (own + 1) * DC)
                                project(k, w_sb["wq"], hn1_t, "q_mm")
                        for k, where_ in enumerate(((1, 1, 0), (1, 1, 2), (1, 2, 0), (1, 2, 2))):
                            if at == where_:
                                if k % DC == 0:
                                    step.wait(pe, m["q_ev"], own * DC + (k // DC + 1))
                                project(k, w_sb["wk"], hn1_t, "k_mm")
                        for k, where_ in enumerate(((2, 0, 0), (2, 0, 2), (2, 1, 0), (2, 1, 2))):
                            if at == where_:
                                if k % 2 == 0:
                                    step.wait(pe, m["k_ev"], own * DC + (k // 2 + 1))
                                project_rows(k, hn1_t, w_sb["wv"], "v_mm")
                    if past is not None:
                        if at == (3, 0, 2):
                            step.wait(pe, m["post_norm"], step.u_past * G + 4)
                            step.wait(pe, m["v_ev"], most(past + 2, B) * DC)
                            step.wait(pe, m["rank_r"], past)
                            turn(0, att["own"], "own_tr")
                        if at == (3, 1, 0):
                            turn(1, att["own"], "own_tr")
                        for k, where_ in enumerate(((3, 2, 0), (3, 2, 2), (3, 3, 0), (3, 3, 2))):
                            if at == where_:
                                if k == 0:
                                    step.wait(pe, m["own_ev"], (past + 1) * DC)
                                project_rows(k, own_t, w_sb["wo"], "wo_mm")
                    if ahead is not None:
                        if at == (4, 2, 0):
                            step.wait(pe, m["x_norm"], ahead + 1)
                            if past is not None:
                                step.wait(pe, m["h_sum"], (past + 1) * DC)
                            elif own is not None:
                                step.wait(pe, m["v_ev"], (own + 1) * DC)
                            else:
                                step.wait(pe, m["c_ev"], ahead * DC)
                            turn(0, xq, "x_tr")
                        if at == (4, 2, 2):
                            turn(1, xq, "x_tr")
                        if at == (5, 0, 0):
                            step.wait(pe, m["x_ev"], (ahead + 1) * DC)
                            step.wait(pe, m["ctx_ld"], (ahead + 1) * 16)
                            turn(0, ctx_in, "c_tr")
                        if at == (5, 0, 2):
                            turn(1, ctx_in, "c_tr")
                    if past is not None:
                        if at == (5, 2, 0):
                            step.wait(pe, m["h_norm"], past + 1)
                            step.wait(pe, m["h_sum"], (past + 1) * DC)
                            if ahead is not None:
                                step.wait(pe, m["c_ev"], (ahead + 1) * DC)
                            turn(0, hn2, "hn2_tr")
                        if at == (5, 2, 2):
                            turn(1, hn2, "hn2_tr")
                        if at[:2] == (6, 0):
                            if hd == 0:
                                step.wait(pe, m["hn2_ev"], (past + 1) * DC)
                            for c in range(DC):
                                r = mm(aux[0][:, hd * E:(hd + 1) * E], hn2_t[:, c, hd * P:(hd + 1) * P], wr_sb[:, c, :],
                                       start=(c == 0), stop=(c == DC - 1))
                            if hd == QT - 1:
                                r.then_inc(m["lg_mm"], 1)
                        if at == (6, 2, 2):
                            step.wait(pe, m["hot_r"], past + 1)
                            for t in range(QT + 1):
                                for s_ in range(min(t + 1, QT)):
                                    r = mm(aux[1][:, t * E:(t + 1) * E], before_b if s_ == t else ones_b, hot_b[:, s_, :],
                                           start=(s_ == 0), stop=(s_ == min(t, QT - 1)))
                            r.then_inc(m["rank_mm"], 1)

                def body(step):
                    body_start(step)
                    for s in range(8):
                        mx, mn, tail = step.max_of(s), step.main_of(s), step.tail_of(s)
                        for kt in range(QT):
                            for hd in range(HG):
                                extra(step, s, kt, hd)
                                if mx:
                                    max_unit(step, mx, kt, hd)
                                if mn:
                                    key_unit(step, mn, kt, hd)
                                if hd == VALUES_AT:
                                    for each in range(HG):
                                        if kt == 0 and tail:
                                            value_unit(step, tail, QT - 1, each)
                                        if kt and mn:
                                            value_unit(step, mn, kt - 1, each)
                            if kt == 1:
                                post_turn(step, s)
                            if kt == 2:
                                neg_turn(step, s)

                run_steps(pe, body)

            @block.scalar
            def _(act):
                act.wait_ge(m["gate_mm"], 1)
                act.activation(gate[:, :], aux[0][:, 0:2], ACT.Tanh).then_inc(m["gate_act"], 1)
                act.wait_ge(m["ld_const"], 16 * 8)

                def exp_unit(step, unit, kt, hd):
                    which, b, u, g = unit
                    n = u * G + g
                    j = HG * kt + hd
                    step.wait(act, m["key_mm"], n * 16 + (j + 1))
                    step.wait(act, m["pv_mm"], n * 16 + (HG * (kt - 2) + hd + 1))
                    q0 = kt * P if is_self(which) else 0
                    act.activation(probs[:, kt % 2, hd, q0:S], key_ps[j % 2][:, q0:S], ACT.Exp).then_inc(m["exp_done"], 1)

                def evacuate(step, c, b, mm_done, ev_done, dst, scale=1.0):
                    step.wait(act, m[mm_done], b * DC + (c + 1))
                    plain = isinstance(scale, float)
                    act.activation(dst[:, c, :], aux[c][:, :], ACT.Copy if plain else ACT.Identity, scale=scale if plain else scale[:, c:c + 1])\
                        .then_inc(m[ev_done], 1)

                def extra(step, s, kt, hd):
                    cross, own, past, ahead = step.cross, step.own, step.past, step.ahead
                    at = (s, kt, hd)
                    if own is not None:
                        if at[:2] == (0, 0) and hd < 2:
                            if hd == 0:
                                step.wait(act, m["xn_done"], own + 1)
                                step.wait(act, m["hn1_tr"], own * DC)
                            for t in (2 * hd, 2 * hd + 1):
                                r = act.activation(hn1[:, t, :], xn[:, t, :], ACT.Identity, scale=r_1[:, QT + t:QT + t + 1])
                            if hd == 1:
                                r.then_inc(m["x1_norm"], 1)
                        for c, where_ in enumerate(((0, 1, 2), (0, 2, 0))):
                            if at == where_:
                                if c == 0:
                                    step.wait(act, m["v_mm"], own * DC)
                                evacuate(step, c, own, "hn1_tr", "hn1_ev", hn1_t, g1_sb)
                        for c, where_ in enumerate(((0, 3, 2), (1, 0, 2))):
                            if at == where_:
                                if c == 0:
                                    step.wait(act, m["x_parts"], most(own + 2, B))
                                evacuate(step, c, own, "q_mm", "q_ev", flat_q, SCALE)
                        for c, where_ in enumerate(((1, 2, 0), (1, 3, 0))):
                            if at == where_:
                                if c == 0:
                                    step.wait(act, m["c_parts"], most(own + 2, B))
                                evacuate(step, c, own, "k_mm", "k_ev", flat_k)
                        for c, where_ in enumerate(((2, 1, 0), (2, 2, 0))):
                            if at == where_:
                                if c == 0 and past is not None:
                                    step.wait(act, m["pv_mm"], (step.u_past + 1) * (G * 16))
                                step.wait(act, m["v_mm"], own * DC + (c + 1))
                                act.activation(v_of["own"][:, 2 * c:2 * c + 2, :, 0:DH],
                                               aux[c][:, :].rearrange("p (t h d) -> p t h d", t=2, d=DH), ACT.Copy).then_inc(m["v_ev"], 1)
                    if past is not None:
                        for c, where_ in enumerate(((3, 1, 0), (3, 1, 2))):
                            if at == where_:
                                if c == 0:
                                    step.wait(act, m["wo_mm"], past * DC)
                                    step.wait(act, m["lg_mm"], past)
                                evacuate(step, c, past, "own_tr", "own_ev", own_t)
                        if at[:2] == (4, 1):
                            if hd == 0:
                                step.wait(act, m["h_sum"], (past + 1) * DC)
                                step.wait(act, m["h_rstd"], past)
                            step.wait(act, m["h_sq"], past * QT + hd)
                            act.activation(sq[:, :], h[:, hd, :], ACT.Square, accum_out=ss[:, hd:hd + 1]).then_inc(m["h_sq"], 1)
                    if ahead is not None:
                        for c, where_ in enumerate(((4, 2, 2), (4, 3, 0))):
                            if at == where_:
                                if c == 0:
                                    step.wait(act, m["x_parts"], ahead)
                                    if own is not None:
                                        step.wait(act, m["oq_parts"], own + 1)
                                evacuate(step, c, ahead, "x_tr", "x_ev", flat_q, SCALE)
                        for c, where_ in enumerate(((5, 0, 2), (5, 1, 0))):
                            if at == where_:
                                if c == 0:
                                    step.wait(act, m["c_parts"], ahead)
                                    if own is not None:
                                        step.wait(act, m["ok_parts"], own + 1)
                                evacuate(step, c, ahead, "c_tr", "c_ev", flat_k)
                    if past is not None:
                        for c, where_ in enumerate(((5, 2, 2), (5, 3, 0))):
                            if at == where_:
                                if c == 0:
                                    step.wait(act, m["wo_mm"], (past + 1) * DC)
                                evacuate(step, c, past, "hn2_tr", "hn2_ev", hn2_t, g2_sb)
                        if at == (6, 2, 0):
                            step.wait(act, m["gap_r"], past + 1)
                            act.activation(e_gap[:, :], gap[:, :], ACT.Exp).then_inc(m["gap_exp"], 1)

                def body(step):
                    for s in range(8):
                        mn, tail, ng = step.main_of(s), step.tail_of(s), step.neg_of(s)
                        for kt in range(QT):
                            if kt == 1 and tail:
                                n = tail[2] * G + tail[3]
                                step.wait(act, m["pv_mm"], (n + 1) * 16)
                                step.wait(act, m["post_tr"], n)
                                act.activation(out_t[:, :], pv_ps[:, :], ACT.Copy).then_inc(m["out_ev"], 1)
                            if kt == 3 and ng:
                                n = ng[2] * G + ng[3]
                                step.wait(act, m["neg_tr"], n + 1)
                                step.wait(act, m["neg_dma"], n * 16)
                                act.activation(neg_rows[:, :], turn_b[0:NEGROWS * HG * QT, 0:P], ACT.Copy).then_inc(m["neg_ev"], 1)
                                step.wait(act, m["neg_ev"], n + 1)
                                act.dma_start(q_stack[ng[3]][KROWS:KROWS + NEGROWS, :, :], neg_rows[:, :]).then_inc(m["neg_dma"], 16)
                            for hd in range(HG):
                                extra(step, s, kt, hd)
                                if mn:
                                    exp_unit(step, mn, kt, hd)

                run_steps(act, body)

            @block.vector
            def _(dve):
                v = nc.vector
                chain = Chain(dve, m["dve"])
                dve.wait_ge(m["ld_const"], 16 * 8)
                v.tensor_copy(squares_b[:, :, :], squares_sb[:, :, :]).then_inc(m["ready_c"], 1)
                v.memset(count[:, :], 0.0)
                v.memset(half[:, :], -0.5)
                v.tensor_copy(token[:, :], small_sb[:, 2 * E:2 * E + QT])
                v.memset(padding[:, D:D + 1], float(T))
                v.memset(padding[:, D + 1:DX], 0.0)
                v.memset(padding[:, 0:D], 0.0).then_inc(m["ready_v"], 1)

                def reduce_unit(step, unit, qt, hd):
                    which, b, u, g = unit
                    n = u * G + g
                    j = HG * qt + hd
                    step.wait(dve, m["max_mm"], n * 16 + (j + 1))
                    if j == 0:
                        step.wait(dve, m["neg_split"], n - 1)
                    keys = (qt + 1) * P if is_self(which) else S
                    v.tensor_reduce(neg[:, g % 2, hd, qt:qt + 1], max_ps[j % 2][:, 0:keys], op=ALU.max, axis=AX.X,
                                    negate=True).then_inc(m["max_red"], 1)

                def split_neg(step, unit, k):
                    n, g2 = unit[2] * G + unit[3], unit[3] % 2
                    src = neg[:, g2, :, :].rearrange("p a b -> p (a b)")
                    rest_, part = neg_rest[:, g2, :], lambda a: neg_parts[:, g2, a, :]
                    if k == 0:
                        step.wait(dve, m["max_red"], (n + 1) * 16)
                        step.wait(dve, m["neg_tr"], n - 1)
                        v.tensor_copy(part(0), src).then_inc(m["neg_chain"], 1)
                        return
                    step.wait(dve, m["neg_chain"], n * 3 + k)
                    if k == 1:
                        v.tensor_tensor(rest_, src, part(0), ALU.subtract).then_inc(m["neg_chain"], 1)
                    if k == 2:
                        v.tensor_copy(part(1), rest_).then_inc(m["neg_chain"], 1)
                    if k == 3:
                        v.tensor_tensor(part(2), rest_, part(1), ALU.subtract).then_inc(m["neg_split"], 1)

                def post_norm(step, unit):
                    which, b, u, g = unit
                    n = u * G + g
                    kind = "own" if is_self(which) else "cross"
                    step.wait(dve, m["post_tr"], n + 1)
                    step.wait(dve, m["post_norm"], n)
                    if g == 0 and kind == "own":
                        step.wait(dve, m["own_tr"], b * DC)
                    if g == 0 and kind == "cross":
                        step.wait(dve, m["x1_stat"], b)
                    o = turn_ps[:, :].rearrange("p (t e) -> p t e", e=32)
                    v.reciprocal(recip[:, :].rearrange("p (t e) -> p t e", e=1), o[:, :, DH:DH + 1]).then_inc(m["post_rc"], 1)
                    step.wait(dve, m["post_rc"], n + 1)
                    src = turn_ps[:, :].rearrange("p (t h e) -> p t h e", h=HG, e=32)[:, :, :, 0:DH]
                    dst = att[kind][:, :, g * HG * DH:(g + 1) * HG * DH].rearrange("p t (h d) -> p t h d", d=DH)
                    rc = recip[:, :].rearrange("p (t h e) -> p t h e", h=HG, e=1).broadcast_to([P, QT, HG, DH])
                    v.tensor_tensor(dst, src, rc, ALU.mult).then_inc(m["post_norm"], 1)

                def split(step, src, dst, rest_):
                    chain.link(v.tensor_copy(dst[:, 0, :, :], src[:, :, :]), step)
                    chain.link(v.tensor_tensor(rest_[:, :, :], src[:, :, :], dst[:, 0, :, :], ALU.subtract), step)
                    chain.link(v.tensor_copy(dst[:, 1, :, :], rest_[:, :, :]), step)
                    return v.tensor_tensor(dst[:, 2, :, :], rest_[:, :, :], dst[:, 1, :, :], ALU.subtract)

                def extra(step, s, kt, hd):
                    cross, own, past, ahead = step.cross, step.own, step.past, step.ahead
                    at = (s, kt, hd)
                    if at == (4, 3, 3) and ahead is not None and splits_on_dve(step):
                        step.wait(dve, m["x_ev"], (ahead + 1) * DC)
                        split(step, flat_q, parts["q"], turned).then_inc(m["x_parts"], 1)
                    if at == (1, 1, 0) and own is not None and splits_on_dve(step):
                        step.wait(dve, m["rope_q"], (own + 1) * (2 * DC))
                        step.wait(dve, m["x_st"], most(own + 2, B) * 96)
                        sin = rope_sb[:, 1:2, :].broadcast_to([P, DC, S])
                        chain.link(v.tensor_tensor(turned[:, :, :], turned[:, :, :], sin, ALU.mult), step)
                        v.tensor_tensor(flat_q[:, :, :], turned[:, :, :], with_cos[:, :, :], ALU.add).then_inc(m["rope_used"], 1)
                        step.wait(dve, m["rope_used"], own * 2 + 1)
                        split(step, flat_q, parts["q"], turned).then_inc(m["oq_parts"], 1)
                        step.wait(dve, m["oq_parts"], own + 1)
                    if own is not None:
                        for flat, ev, done, c, where_ in ((flat_q, "q_ev", "rope_q", 0, (1, 0, 0)), (flat_q, "q_ev", "rope_q", 1, (1, 0, 3)),
                                                          (flat_k, "k_ev", "rope_k", 0, (2, 0, 0)), (flat_k, "k_ev", "rope_k", 1, (2, 0, 2))):
                            if at == where_:
                                step.wait(dve, m[ev], own * DC + (c + 1))
                                if c == 0:
                                    step.wait(dve, m["rope_used"], own * 2 + (0 if done == "rope_q" else 1))
                                v.tensor_tensor(with_cos[:, c, :], flat[:, c, :], rope_sb[:, 0, :], ALU.mult).then_inc(m[done], 1)
                                swap = [(p + DH // 2) % DH + (p // DH) * DH for p in range(32)]
                                v.stream_shuffle(out=turned[:, c, :], in_=flat[:, c, :], mask=swap).then_inc(m[done], 1)
                    if ahead is not None:
                        if at[:2] == (3, 2):
                            if hd == 0:
                                step.wait(dve, m["x_ld"], (ahead + 1) * 16)
                                step.wait(dve, m["x_rstd"], ahead)
                            r = v.bn_stats(st_x[:, hd, :], x_in[:, hd, :])
                            if hd == QT - 1:
                                chain.link(r, step)
                        if at == (3, 3, 0):
                            for t in range(QT):
                                r = v.bn_aggr(mv_x[:, t, :], st_x[:, t, :])
                            r.then_inc(m["x_stat"], 1)
                        if at[:2] == (4, 1):
                            if hd == 0:
                                step.wait(dve, m["x_rstd"], ahead + 1)
                                step.wait(dve, m["x_tr"], ahead * DC)
                                step.wait(dve, m["x_stat"], ahead + 1)
                            r = v.tensor_scalar(xq[:, hd, :], x_in[:, hd, :], mv_x[:, hd, 0:1], r_x[:, hd:hd + 1], ALU.subtract, ALU.mult)
                            if hd == QT - 1:
                                r.then_inc(m["x_norm"], 1)
                    if past is not None:
                        for c, where_ in enumerate(((4, 0, 0), (4, 0, 2))):
                            if at == where_:
                                if c == 0:
                                    step.wait(dve, m["kept_ld"], (past + 1) * 32)
                                    step.wait(dve, m["h_norm"], past)
                                    step.wait(dve, m["h_sq"], past * QT)
                                    step.wait(dve, m["h_base"], past)
                                step.wait(dve, m["wo_mm"], past * DC + (c + 1))
                                v.tensor_tensor(h[:, 2 * c:2 * c + 2, :], kept[:, 1, 2 * c:2 * c + 2, :],
                                                aux[c][:, :].rearrange("p (t d) -> p t d", t=2), ALU.add).then_inc(m["h_sum"], 1)
                        if at[:2] == (5, 0):
                            if hd == 0:
                                step.wait(dve, m["h_rstd"], past + 1)
                                step.wait(dve, m["hn2_tr"], past * DC)
                                step.wait(dve, m["scat"], past * (2 * QT * 16))
                            r = v.tensor_scalar(hn2[:, hd, 0:D], h[:, hd, :], r_h[:, hd:hd + 1], None, ALU.mult)
                            if hd == QT - 1:
                                r.then_inc(m["h_norm"], 1)
                    if at == (6, 1, 0) and past is not None:
                        step.wait(dve, m["lg_mm"], past + 1)
                        chain.link(v.tensor_copy(lg[:, :, :], aux[0][:, 0:QT * E].rearrange("p (t e) -> p t e", e=E)), step)
                        for t in range(QT):
                            r = v.max(top[:, t, :], lg[:, t, :])
                        chain.link(r, step)
                        step.wait(dve, m["gap_exp"], past)
                        v.tensor_tensor(gap[:, :].rearrange("p (t e) -> p t e", e=1), top[:, :, 1:2], top[:, :, 0:1], ALU.subtract)\
                            .then_inc(m["gap_r"], 1)
                    if at == (6, 1, 2) and past is not None:
                        for t in range(QT):
                            r = v.max_index(idx[:, t, :], top[:, t, :], lg[:, t, :])
                        chain.link(r, step)
                        chain.link(v.tensor_copy(idx_f[:, :, :], idx[:, :, :]), step)
                    if at == (6, 2, 0) and past is not None:
                        experts = iota_e.rearrange("p (t e) -> p t e", t=1).broadcast_to([P, QT, E])
                        for k in range(2):
                            r = v.tensor_tensor(hot[:, k, :, :], idx_f[:, :, k:k + 1].broadcast_to([P, QT, E]), experts, ALU.is_equal)
                        chain.link(r, step)
                        step.wait(dve, m["rank_mm"], past)
                        v.tensor_tensor(hot_b[:, :, :], hot[:, 0, :, :], hot[:, 1, :, :], ALU.add).then_inc(m["hot_r"], 1)
                    if at == (6, 3, 0) and past is not None:
                        step.wait(dve, m["rank_mm"], past + 1)
                        step.wait(dve, m["hot_r"], past + 1)
                        ranks = aux[1][:, 0:QT * E].rearrange("p (t e) -> p t e", e=E)
                        so_far = count[:, :].rearrange("p (t e) -> p t e", t=1).broadcast_to([P, QT, E])
                        regions = region_e.rearrange("p (t e) -> p t e", t=1).broadcast_to([P, QT, E])
                        chain.link(v.tensor_tensor(where[:, :, :], ranks, so_far, ALU.add), step)
                        chain.link(v.tensor_tensor(count[:, :], aux[1][:, QT * E:(QT + 1) * E], count[:, :], ALU.add), step)
                        v.tensor_tensor(where[:, :, :], where[:, :, :], regions, ALU.add).then_inc(m["rank_r"], 1)
                        step.wait(dve, m["rank_r"], past + 1)
                    if at == (6, 3, 2) and past is not None:
                        for k in range(2):
                            r = v.tensor_tensor(picked[:, k, :, :], where[:, :, :], hot[:, k, :, :], ALU.mult)
                        chain.link(r, step)
                        chain.link(v.tensor_reduce(pos_f[:, :], picked[:, :, :, :].rearrange("p k t e -> p (k t) e"), op=ALU.add, axis=AX.X), step)
                        step.wait(dve, m["scat"], past * (2 * QT * 16))
                        chain.link(v.tensor_copy(pos_i[:, :], pos_f[:, :]), step)
                    if at == (6, 3, 3) and past is not None:
                        step.wait(dve, m["gap_exp"], past + 1)
                        chain.link(v.tensor_scalar(mix[:, 1, :], e_gap[:, :], 1.0, None, ALU.add), step)
                        chain.link(v.reciprocal(mix[:, 0, :], mix[:, 1, :]), step)
                        chain.link(v.tensor_tensor(mix[:, 1, :], mix[:, 0, :], e_gap[:, :], ALU.mult), step)
                        v.tensor_copy(hn2[:, :, D:D + 1], token[:, :].rearrange("p (t e) -> p t e", e=1))
                        chain.link(v.tensor_scalar(weight[:, :, :].rearrange("p a b -> p (a b)"),
                                                   mix[:, :, :].rearrange("p a b -> p (a b)"), gate[:, 1:2], None, ALU.mult), step)
                        v.tensor_scalar(token[:, :], token[:, :], float(S), None, ALU.add).then_inc(m["route"], 1)
                    if cross is not None:
                        for c, where_ in enumerate(((7, 0, 0), (7, 0, 2))):
                            if at == where_:
                                if c == 0:
                                    step.wait(dve, m["xa_ld"], (cross + 1) * 16)
                                    step.wait(dve, m["post_norm"], step.u_cross * G + 4)
                                    step.wait(dve, m["kept_st"], cross * 32)
                                two = slice(2 * c, 2 * c + 2)
                                chain.link(v.scalar_tensor_tensor(out=x1[:, two, :], in0=att["cross"][:, two, :], scalar=gate[:, 0:1],
                                                                  in1=x1[:, two, :], op0=ALU.mult, op1=ALU.add), step)
                        for c, where_ in enumerate(((7, 0, 1), (7, 0, 3))):
                            if at == where_:
                                for t in (2 * c, 2 * c + 1):
                                    r = v.bn_stats(st_1[:, t, :], x1[:, t, :])
                                chain.link(r, step)
                        if at == (7, 1, 0):
                            wait_apart(step, dve, (m["x1_rstd"], cross))
                            for t in range(QT):
                                r = v.bn_aggr(mv_1[:, t, :], st_1[:, t, :])
                            r.then_inc(m["x1_stat"], 1)
                        if at[:2] == (7, 3):
                            if hd == 0:
                                step.wait(dve, m["x1_rstd"], cross + 1)
                                step.wait(dve, m["x1_stat"], cross + 1)
                                step.wait(dve, m["x1_norm"], cross)
                            r = v.tensor_scalar(xn[:, hd, :], x1[:, hd, :], mv_1[:, hd, 0:1], r_1[:, hd:hd + 1], ALU.subtract, ALU.mult)
                            if hd == QT - 1:
                                r.then_inc(m["xn_done"], 1)

                def table(v, chain):
                    link = chain.link
                    wait_apart(Step(LAST), dve, (m["rope_used"], 2 * B))
                    line = lambda buf, c, n, dt=F32: buf[0:1, c, 0:n] if dt == F32 else buf[0:1, c, 0:n].bitcast(dt)
                    by_expert = lambda a: a.rearrange("p (t e) -> p t e", e=E)
                    end_f, full_f, cum, ones_e = (line(turned, 0, (n + 1) * E)[:, n * E:] for n in range(4))
                    skip, full_i = line(turned, 0, 5 * E)[:, 4 * E:], line(turned, 0, 6 * E)[:, 5 * E:].bitcast(I32)
                    rest_of_line = turned[0:1, 1, :]
                    expert_f, row_f, start_f, float_f = (rest_of_line[:, n * TILES:(n + 1) * TILES] for n in range(4))
                    int_a, int_b = (rest_of_line[:, n * TILES:(n + 1) * TILES].bitcast(I32) for n in (4, 5))
                    tile_no = by_expert(xn[0:1, :, :].rearrange("p t d -> p (t d)")[:, 0:TILES * E])
                    passed = by_expert(with_cos[0:1, :, :].rearrange("p c t -> p (c t)")[:, 0:TILES * E])
                    among = by_expert(xq[0:1, :, :].rearrange("p t d -> p (t d)")[:, 0:TILES * E])
                    link(v.tensor_tensor(end_f, count[0:1, :], region_e[0:1, :], ALU.add))
                    v.tensor_copy(pad_i[:, :], end_f).then_inc(m["pad_at"], 1)
                    link(v.tensor_scalar(full_i, count[0:1, :], float(P - 1), None, ALU.add))
                    link(v.tensor_scalar(full_i, full_i, P.bit_length() - 1, None, ALU.logical_shift_right))
                    link(v.tensor_copy(full_f, full_i))
                    link(v.memset(ones_e, 1.0))
                    link(v.tensor_tensor_scan(cum, ones_e, full_f, 0.0, ALU.mult, ALU.add))
                    dve.wait_ge(m["tab_ld"], 16)
                    wide = lambda a: a.rearrange("p (t e) -> p t e", t=1).broadcast_to([1, TILES, E])
                    link(v.tensor_tensor(passed, wide(cum), tile_no, ALU.is_le))
                    link(v.tensor_reduce(expert_f, passed, op=ALU.add, axis=AX.X))
                    link(v.tensor_scalar(expert_f, expert_f, float(E - 1), None, ALU.min))
                    link(v.tensor_copy(expert_i[:, :], expert_f))
                    link(v.tensor_scalar(skip, full_f, -float(P), float(CAP), ALU.mult, ALU.add))
                    link(v.tensor_tensor(among, wide(skip), passed, ALU.mult))
                    link(v.tensor_reduce(row_f, among, op=ALU.add, axis=AX.X))
                    link(v.tensor_scalar(float_f, tile_no[:, :, 0:1].rearrange("p t e -> p (t e)"), float(P), None, ALU.mult))
                    link(v.tensor_tensor(row_i[:, :], row_f, float_f, ALU.add))
                    link(v.tensor_tensor(among, wide(full_f), passed, ALU.mult))
                    link(v.tensor_reduce(start_f, among, op=ALU.add, axis=AX.X))
                    for n in range(2):
                        link(v.tensor_scalar(int_a, start_f, float(1 - n), None, ALU.add))
                        link(v.tensor_scalar(int_b, int_a, 1, None, ALU.logical_shift_right))
                        link(v.tensor_copy(float_f, int_b))
                        link(v.tensor_scalar(old_i[n][:, :], float_f, 16.0, 16.0, ALU.mult, ALU.add))
                    link(v.tensor_scalar(int_a, expert_i[:, :], 1, None, ALU.bitwise_and))
                    link(v.tensor_copy(float_f, int_a))
                    link(v.tensor_scalar(w_off[:, :], float_f, float(2 * WALL), None, ALU.mult))
                    link(v.tensor_scalar(cum_i[:, :], cum, 1.0, None, ALU.add))

                def body(step):
                    for s in range(8):
                        mx, tail, ng = step.max_of(s), step.tail_of(s), step.neg_of(s)
                        for kt in range(QT):
                            for hd in range(HG):
                                extra(step, s, kt, hd)
                                if kt == 0 and ng:
                                    split_neg(step, ng, hd)
                                if (kt, hd) == (2, 1) and tail:
                                    post_norm(step, tail)
                                if mx:
                                    reduce_unit(step, mx, kt, hd)

                run_steps(dve, lambda step: chain.loop_body(step, body, DVE_LINKS))
                table(v, chain)

            @block.gpsimd
            def _(pool):
                g_ = nc.gpsimd
                chain = Chain(pool, m["pool"])
                for g in range(G):
                    g_.memset(k_stack[g][KROWS:KROWS + NEGROWS, :, :], 1.0).then_inc(m["ready_b"], 1)
                    pool.wait_ge(m["ready_b"], g + 1)
                for n, kind in enumerate(("cross", "own")):
                    g_.memset(v_of[kind][:, :, :, DH + 1:32], 0.0).then_inc(m["ready_b"], 1)
                    pool.wait_ge(m["ready_b"], G + 2 * n + 1)
                    g_.memset(v_of[kind][:, :, :, DH:DH + 1], 1.0).then_inc(m["ready_b"], 1)
                    pool.wait_ge(m["ready_b"], G + 2 * n + 2)
                pool.wait_ge(m["ready_v"], 1)

                def split(step, src, dst, done, after, sent):
                    flat = lambda a: a.rearrange("p a b -> p (a b)")
                    s_, r = flat(src[:, :, :]), flat(rest[:, :, :])
                    p_ = [flat(dst[:, n, :, :]) for n in range(3)]
                    wait_apart(step, pool, (m[sent[0]], sent[1]))
                    chain.link(g_.tensor_scalar(p_[0], s_, 1.0, 0.0, ALU.mult, ALU.add), step)
                    chain.link(g_.tensor_tensor(r, s_, p_[0], ALU.subtract), step)
                    chain.link(g_.tensor_scalar(p_[1], r, 1.0, 0.0, ALU.mult, ALU.add), step)
                    g_.tensor_tensor(p_[2], r, p_[1], ALU.subtract).then_inc(m[done], 1)
                    wait_apart(step, pool, (m[done], after))

                def load_piece(e, k):
                    w_, row, n, _, width = pieces[k]
                    n_rows = min(n * P, w_.shape[1] - row)
                    rows_ = min(P, n_rows)
                    g_.dma_start(w_in[0:rows_, 0:width].rearrange("p (n f) -> p n f", n=n),
                                 w_[e][row:row + n_rows, :].rearrange("(n p) f -> p n f", p=rows_)).then_inc(m["w_in_ld"], 16)

                def split_piece(step, k):
                    e = step.cross
                    _, _, _, at, width = pieces[k]
                    n = len(pieces)
                    wait_apart(step, pool, (m["w_in_ld"], (e * n + (k + 1)) * 16), (m["w_part_st"], (e * n + k) * 16))
                    chain.link(g_.tensor_scalar(w_parts[:, 0, 0:width], w_in[:, 0:width], 1.0, 0.0, ALU.mult, ALU.add), step)
                    chain.link(g_.tensor_tensor(w_parts[:, 1, 0:width], w_in[:, 0:width], w_parts[:, 0, 0:width], ALU.subtract), step)
                    if k < n - 1:
                        load_piece(step.value(e), k + 1)
                    g_.dma_start(w_split[step.value(e)][:, :, at:at + width], w_parts[:, :, 0:width].bitcast(F32)).then_inc(m["w_part_st"], 16)

                def rsqrt(step, dst, src, scale, eps):
                    chain.link(g_.tensor_scalar(tmp_r[:, :].rearrange("p (a b) -> p a b", b=1), src, scale, eps, ALU.mult, ALU.add), step)
                    return g_.tensor_tensor(dst, tmp_r[:, :], half[:, 0:QT], ALU.pow)

                def extra(step, s):
                    cross, own, past, ahead = step.cross, step.own, step.past, step.ahead
                    if s in (0, 1) and own is not None and not (s == 0 and splits_on_dve(step)):
                        o = "qk"[s]
                        flat = (flat_q, flat_k)[s]
                        step.wait(pool, m["rope_q" if s == 0 else "rope_k"], (own + 1) * (2 * DC))
                        sin = rope_sb[:, 1:2, :].broadcast_to([P, DC, S])
                        chain.link(g_.tensor_tensor(turned[:, :, :], turned[:, :, :], sin, ALU.mult), step)
                        g_.tensor_tensor(flat[:, :, :], turned[:, :, :], with_cos[:, :, :], ALU.add).then_inc(m["rope_used"], 1)
                        wait_apart(step, pool, (m["rope_used"], own * 2 + (s + 1)))
                        split(step, flat, parts[o], "oq_parts" if s == 0 else "ok_parts", own + 1,
                              ("x_st" if s == 0 else "c_st", most(own + 2, B) * 96))
                    if s == 3 and ahead is not None:
                        wait_apart(step, pool, (m["x_stat"], ahead + 1), (m["x_norm"], ahead))
                        rsqrt(step, r_x[:, :], mv_x[:, :, 1:2], 1.0, 1e-5).then_inc(m["x_rstd"], 1)
                    if s == 4 and past is not None:
                        step.wait(pool, m["h_sq"], (past + 1) * QT)
                        wait_apart(step, pool, (m["h_norm"], past))
                        rsqrt(step, r_h[:, :], ss[:, :].rearrange("p (a b) -> p a b", b=1), 1.0 / D, 1e-6).then_inc(m["h_rstd"], 1)
                    if s == 6 and past is not None:
                        wait_apart(step, pool, (m["base_st"], past * 16), (m["h_sum"], (past + 1) * DC), (m["kept_ld"], (past + 1) * 32))
                        chain.link(g_.tensor_scalar(base[:, :, :], h[:, :, :], gate[:, 1:2], None, ALU.mult), step)
                        g_.tensor_tensor(base[:, :, :], base[:, :, :], kept[:, 0, :, :], ALU.add).then_inc(m["h_base"], 1)
                    if s in (4, 5) and ahead is not None and not (s == 4 and splits_on_dve(step)):
                        o = "qk"[s - 4]
                        src, ev, done = ((flat_q, "x_ev", "x_parts"), (flat_k, "c_ev", "c_parts"))[s - 4]
                        wait_apart(step, pool, (m[ev], (ahead + 1) * DC))
                        if own is not None:
                            sent = ("oq_st" if s == 4 else "ok_st", (own + 1) * 96)
                        else:
                            sent = ("x_st" if s == 4 else "c_st", ahead * 96)
                        split(step, src, parts[o], done, ahead + 1, sent)
                    if s == 6 and ahead is not None:
                        if cross is not None:
                            step.wait(pool, m["pv_mm"], (step.u_cross + 1) * (G * 16))
                        wait_apart(step, pool, (m["ctx_ld"], (ahead + 1) * 16))
                        g_.tensor_scalar(v_of["cross"][:, :, :, 0:DH].rearrange("p t h d -> p (t h) d"),
                                         ctx_in[:, :, :].rearrange("p t (h d) -> p (t h) d", d=DH), 1.0, 0.0, ALU.mult, ALU.add)\
                            .then_inc(m["v_cross"], 1)
                    if s == 7 and cross is not None:
                        wait_apart(step, pool, (m["x1_stat"], cross + 1), (m["x1_norm"], cross))
                        chain.link(rsqrt(step, r_1[:, 0:QT], mv_1[:, :, 1:2], 1.0, 1e-5), step)
                        var = mv_1[:, :, 1:2].rearrange("p a b -> p (a b)")
                        chain.link(g_.tensor_tensor(tmp_r[:, :], var, r_1[:, 0:QT], ALU.mult), step)
                        chain.link(g_.tensor_tensor(tmp_r[:, :], tmp_r[:, :], r_1[:, 0:QT], ALU.mult), step)
                        rsqrt(step, r_1[:, QT:2 * QT], tmp_r[:, :].rearrange("p (a b) -> p a b", b=1), 1.0, 1e-6).then_inc(m["x1_rstd"], 1)
                    if s == 7 and past is not None:
                        wait_apart(step, pool, (m["route"], past + 1), (m["h_norm"], past + 1))
                        for k in range(2):
                            if k:
                                wait_apart(step, pool, (m["scat"], past * (2 * QT * 16) + QT * 16))
                            chain.link(g_.tensor_copy(hn2[:, :, D + 1:DX], weight[:, k, :].rearrange("p (t e) -> p t e", e=1)), step)
                            for t in range(QT):
                                g_.indirect_dma_start(
                                    out=rows_in, out_offset=bass.IndirectOffsetOnAxis(ap=pos_i[:, k * QT + t:k * QT + t + 1], axis=0),
                                    in_=hn2[:, t, :], in_offset=None).then_inc(m["scat"], 16)

                def body(step):
                    for s in range(8):
                        if s == 0 and step.cross is not None:
                            load_piece(step.value(step.cross), 0)
                        extra(step, s)
                        if step.cross is not None:
                            for k in PIECES_AT[s]:
                                split_piece(step, k)

                run_steps(pool, lambda step: chain.loop_body(step, body, POOL_LINKS))
                pool.wait_ge(m["scat"], B * 2 * QT * 16)
                pool.wait_ge(m["w_part_st"], E * len(pieces) * 16)

        with ExitStack() as st:
            def s2(name, *shape, dt=F32):
                return sb(name, (P, *shape), dt, st)

            weights = s2("weights", 2 * 2 * WALL, dt=F32R)
            rows_sb = [s2("rows0", DX), s2("rows1", DX)]
            rows_t = s2("rows_t", 2, DC, P, dt=F32R)
            silu, hidden, hidden_t = s2("silu", F), s2("hidden", F), s2("hidden_t", 2, FC, P, dt=F32R)
            whose = [s2(f"whose{n}", 1, dt=I32) for n in range(2)]
            weight = [s2(f"row_weight{n}", 1) for n in range(2)]
            so_far = [s2(f"so_far{n}", D) for n in range(2)]
            more = [s2(f"more{n}", D) for n in range(2)]

            def bank(name):
                return st.enter_context(nc.psum_tensor(name, [P, 512], F32))

            gate_ps, up_ps = [bank("gate_ps0"), bank("gate_ps1")], [bank("up_ps0"), bank("up_ps1")]
            rows_ps, y_ps = bank("rows_ps"), bank("y_ps")
            hid_ps = [bank("hid_ps0"), bank("hid_ps1")]

            m = {n: sem("t_" + n, st) for n in """begun w_ld x_tr x_ev x_lo gate_mm up_mm silu hid
                hid_tr hid_hi hid_lo y_mm y_done owner""".split()}
            x_ld, far_ld, far_st = ([sem(f"t_{k}{n}", st) for n in range(2)] for k in ("x_ld", "far_ld", "far_st"))
            block = st.enter_context(nc.Block())
            PAIRS = TILES // 2

            def pairs(eng, body):
                body(0, True, False)
                with eng.Fori(1, PAIRS - 1) as jj:
                    body(jj, False, False)
                body(PAIRS - 1, False, True)

            def wait_apart(eng, *waits):
                for _, v in waits:
                    if not isinstance(v, int):
                        eng.compute_val(v)
                eng.wait_ge(m["begun"], 1)
                for s_, v in waits:
                    wait(eng, s_, v)

            def wait(eng, s_, v):
                if not isinstance(v, int) or v > 0:
                    eng.wait_ge(s_, v)

            @block.sync
            def _(sp):
                def load_expert(e, par):
                    dst = weights[:, par * 2 * WALL:(par + 1) * 2 * WALL].rearrange("p (a n) -> p a n", a=2)
                    for part in (slice(0, 2 * WG), slice(2 * WG, WALL)):
                        sp.dma_start(dst[:, :, part].bitcast(F32), w_split[e][:, :, part]).then_inc(m["w_ld"], 16)

                load_expert(0, 0)
                sp.wait_ge(m["w_ld"], 32)
                load_expert(1, 1)
                with sp.Fori(1, E // 2) as ee:
                    for par in range(2):
                        e = ee * 2 + par
                        done = sp.value_load(cum_i[0:1, bass.ds(e - 2, 1)], min_val=1, max_val=TILES + 1)
                        wait_apart(sp, (m["y_done"], done), (m["w_ld"], e * 32))
                        load_expert(e, par)

            @block.gpsimd
            def _(pool):
                g_ = nc.gpsimd
                for n in range(2):
                    g_.dma_start(so_far[n][:, :], out_rows[0:P, :]).then_inc(far_st[n], 16)
                def fetch(j, par):
                    old = [pool.value_load(old_i[n][0:1, bass.ds(j, 1)], min_val=16, max_val=16 * (PAIRS + 1)) for n in range(2)]
                    wait_apart(pool, (far_st[0], old[0]), (far_st[1], old[1]),
                               (m["owner"], j + 1))
                    g_.indirect_dma_start(out=so_far[par][:, :], out_offset=None, in_=out_rows,
                                          in_offset=bass.IndirectOffsetOnAxis(ap=whose[par][:, 0:1], axis=0),
                                          bounds_check=T - 1, oob_is_err=False).then_inc(far_ld[par], 16)

                def store(j, par):
                    wait_apart(pool, (m["y_done"], j + 2))
                    g_.indirect_dma_start(out=out_rows, out_offset=bass.IndirectOffsetOnAxis(ap=whose[par][:, 0:1], axis=0),
                                          in_=more[par][:, :], in_offset=None,
                                          bounds_check=T - 1, oob_is_err=False).then_inc(far_st[par], 16)

                def body(jj, first, last):
                    for h_ in range(2):
                        j = jj * 2 + h_
                        store(j, h_)
                        if not (last and h_):
                            fetch(j + 1, 1 - h_)

                fetch(0, 0)
                pairs(pool, body)
                for n in range(2):
                    pool.wait_ge(far_st[n], 16 * (PAIRS + 1))

            @block.vector
            def _(dve):
                v = nc.vector
                def owner(j, par):
                    wait(dve, x_ld[par], (j - par) * 8 + 16)
                    wait(dve, far_st[par], (j - par) * 8 + 16)
                    v.tensor_copy(whose[par][:, :], rows_sb[par][:, D:D + 1])
                    v.tensor_copy(weight[par][:, :], rows_sb[par][:, D + 1:DX]).then_inc(m["owner"], 1)

                def rows_low(j):
                    wait(dve, m["x_ev"], j * DC + DC)
                    for c in range(DC):
                        v.scalar_tensor_tensor(out=rows_t[:, 1, c, :], in0=rows_ps[:, c * P:(c + 1) * P], scalar=g2_sb[:, c:c + 1],
                                               in1=rows_t[:, 0, c, :], op0=ALU.mult, op1=ALU.subtract).then_inc(m["x_lo"], 1)

                def add_up(j, par):
                    wait(dve, m["y_mm"], j + 1)
                    wait(dve, m["owner"], j + 1)
                    wait(dve, far_ld[par], (j - par) * 8 + 16)
                    wait(dve, far_st[par], (j - par) * 8 + 16)
                    v.scalar_tensor_tensor(out=more[par][:, :], in0=y_ps[:, 0:D], scalar=weight[par][:, 0:1], in1=so_far[par][:, :],
                                           op0=ALU.mult, op1=ALU.add).then_inc(m["y_done"], 1)

                def body(jj, first, last):
                    for h_ in range(2):
                        j = jj * 2 + h_
                        wait(dve, m["hid_tr"], j * 2)
                        for n in range(2):
                            wait(dve, m["silu"], j * 2 + (n + 1))
                            wait(dve, m["up_mm"], j * 2 + (n + 1))
                            v.tensor_tensor(hidden[:, n * FH:(n + 1) * FH], silu[:, n * FH:(n + 1) * FH], up_ps[n][:, 0:FH], ALU.mult)\
                                .then_inc(m["hid"], 1)
                        if not (last and h_):
                            rows_low(j + 1)
                        if not (first and h_ == 0):
                            add_up(j - 1, 1 - h_)
                        hi, lo = hidden_t[:, 0, :, :], hidden_t[:, 1, :, :]
                        wait(dve, m["hid_hi"], j * 2 + 1)
                        v.tensor_tensor(lo[:, 0:4, :].rearrange("p k t -> p (k t)"), hid_ps[0][:, :],
                                        hi[:, 0:4, :].rearrange("p k t -> p (k t)"), ALU.subtract)
                        wait(dve, m["hid_hi"], j * 2 + 2)
                        v.tensor_tensor(lo[:, 4, :], hid_ps[1][:, 0:P], hi[:, 4, :], ALU.subtract)
                        v.tensor_tensor(lo[0:F % P, 5, :], hid_ps[1][0:F % P, P:2 * P], hi[0:F % P, 5, :], ALU.subtract).then_inc(m["hid_lo"], 1)
                        if not (last and h_):
                            owner(j + 1, 1 - h_)

                v.memset(weight[0][:, :], 0.0).then_inc(m["begun"], 1)
                v.memset(weight[1][:, :], 0.0).then_inc(m["y_done"], 1)
                dve.wait_ge(m["begun"], 1)
                dve.wait_ge(m["y_done"], 1)
                owner(0, 0)
                rows_low(0)
                pairs(dve, body)
                add_up(TILES - 1, 1)

            @block.scalar
            def _(act):
                def load(j, par):
                    at = act.value_load(row_i[0:1, bass.ds(j, 1)], min_val=0, max_val=ROWS - P)
                    act.dma_start(rows_sb[par][:, :], rows_in[bass.ds(at, P), :]).then_inc(x_ld[par], 16)

                def rows(j):
                    wait(act, m["x_tr"], j + 1)
                    wait(act, m["up_mm"], j * 2)
                    for c in range(DC):
                        act.activation(rows_t[:, 0, c, :], rows_ps[:, c * P:(c + 1) * P], ACT.Identity, scale=g2_sb[:, c:c + 1]).then_inc(m["x_ev"], 1)

                def body(jj, first, last):
                    for h_ in range(2):
                        j = jj * 2 + h_
                        wait(act, m["hid"], j * 2)
                        for n in range(2):
                            wait(act, m["gate_mm"], j * 2 + (n + 1))
                            act.activation(silu[:, n * FH:(n + 1) * FH], gate_ps[n][:, 0:FH], ACT.Silu).then_inc(m["silu"], 1)
                        if not (last and h_):
                            rows(j + 1)
                        if not last:
                            wait_apart(act, (m["owner"], j + 1))
                            load(j + 2, h_)
                        wait(act, m["hid_tr"], j * 2 + 1)
                        wait(act, m["y_mm"], j)
                        hi = hidden_t[:, 0, :, :]
                        act.activation(hi[:, 0:4, :].rearrange("p k t -> p (k t)"), hid_ps[0][:, :], ACT.Copy).then_inc(m["hid_hi"], 1)
                        wait(act, m["hid_tr"], j * 2 + 2)
                        act.activation(hi[:, 4, :], hid_ps[1][:, 0:P], ACT.Copy)
                        act.activation(hi[0:F % P, 5, :], hid_ps[1][0:F % P, P:2 * P], ACT.Copy).then_inc(m["hid_hi"], 1)

                load(0, 0)
                load(1, 1)
                rows(0)
                pairs(act, body)

            @block.tensor
            def _(pe):
                mm, tr = nc.tensor.matmul, nc.tensor.transpose
                def reg(tab, j, most_):
                    return pe.value_load(tab[0:1, bass.ds(j, 1)], min_val=0, max_val=most_)

                def turn_rows(j, par):
                    wait(pe, m["x_ev"], j * DC)
                    wait(pe, m["x_lo"], j * DC)
                    wait(pe, x_ld[par], (j - par) * 8 + 16)
                    for c in range(DC):
                        r = tr(rows_ps[:, c * P:(c + 1) * P], rows_sb[par][:, c * P:(c + 1) * P], ident[:, :])
                    r.then_inc(m["x_tr"], 1)

                PASSES = ((0, 0), (0, 1), (1, 0))

                def up(j, e, off):
                    pe.wait_ge(m["w_ld"], e * 32 + 32)
                    wait(pe, m["x_ev"], j * DC + DC)
                    wait(pe, m["x_lo"], j * DC + DC)
                    for at, ps, used, done in ((0, gate_ps, "silu", "gate_mm"), (WG, up_ps, "hid", "up_mm")):
                        for n in range(2):
                            wait(pe, m[used], j * 2 + (n - 1) if n == 0 else j * 2)
                            for c in range(DC):
                                for a, w_ in PASSES:
                                    r = mm(ps[n][:, 0:FH], rows_t[:, a, c, :], weights[:, bass.ds(off + (w_ * WALL + at + c * F + n * FH), FH)],
                                           start=(c == 0 and (a, w_) == PASSES[0]), stop=(c == DC - 1 and (a, w_) == PASSES[-1]))
                            r.then_inc(m[done], 1)

                def turn_hidden(j):
                    wait(pe, m["hid_hi"], j * 2)
                    wait(pe, m["hid_lo"], j)
                    for k in range(FC):
                        n = min(P, F - k * P)
                        if k == 0:
                            wait(pe, m["hid"], j * 2 + 1)
                        if k * P + n > FH and (k - 1) * P + P <= FH:
                            wait(pe, m["hid"], j * 2 + 2)
                        r = tr(hid_ps[k // 4][0:n, (k % 4) * P:(k % 4 + 1) * P], hidden[:, k * P:k * P + n], ident[:, :])
                        if k == 3 or k == FC - 1:
                            r.then_inc(m["hid_tr"], 1)

                def down(j):
                    off = reg(w_off, j, 2 * WALL)
                    wait(pe, m["hid_hi"], j * 2 + 2)
                    wait(pe, m["hid_lo"], j + 1)
                    wait(pe, m["y_done"], j + 1)
                    for k in range(FC):
                        n = min(P, F - k * P)
                        for a, w_ in PASSES:
                            r = mm(y_ps[:, 0:D], hidden_t[0:n, a, k, :], weights[0:n, bass.ds(off + (w_ * WALL + 2 * WG + k * D), D)],
                                   start=(k == 0 and (a, w_) == PASSES[0]), stop=(k == FC - 1 and (a, w_) == PASSES[-1]))
                    r.then_inc(m["y_mm"], 1)

                def body(jj, first, last):
                    for h_ in range(2):
                        j = jj * 2 + h_
                        e, off = reg(expert_i, j, E - 1), reg(w_off, j, 2 * WALL)
                        if not (first and h_ == 0):
                            turn_hidden(j - 1)
                        up(j, e, off)
                        if not (last and h_):
                            turn_rows(j + 1, 1 - h_)
                        if not (first and h_ == 0):
                            down(j - 1)

                turn_rows(0, 0)
                pairs(pe, body)
                turn_hidden(TILES - 1)
                down(TILES - 1)


_INS = ["x", "ctx_1024", "g_xattn", "g_ffn", "L0_ffn_wq", "L0_ffn_wk", "L0_ffn_wv", "L0_ffn_wo", "L0_ffn_w_router",
        "L0_ffn_wg", "L0_ffn_wu", "L0_ffn_wd", "L0_ffn_g1", "L0_ffn_g2"]


def kernel(**inputs):
    import concourse.bacc as bacc
    from concourse.bass_utils import run_bass_kernel_spmd

    nc = bacc.Bacc("TRN2", target_bir_lowering=False, num_devices=1)
    arrays, args = {}, []
    for name in _INS:
        a = np.ascontiguousarray(inputs[name])
        arrays[f"in_{name}"] = a
        args.append(nc.dram_tensor(f"in_{name}", a.shape, mybir.dt.from_np(a.dtype), kind="ExternalInput").ap())
    out = nc.dram_tensor("out_0", (B, S, D), F32, kind="ExternalOutput").ap()
    flamingo_block(nc, *args, out)
    r = run_bass_kernel_spmd(nc, [arrays], core_ids=[0])
    return r.results[0]["out_0"]
```
